# Optimizing a Trainium2 kernel written in Bass

```python
import numpy as np
import jax
import jax.numpy as jnp

def _softmax(x, axis=-1):
    return jax.nn.softmax(x, axis=axis)

def _gelu(x):
    return jax.nn.gelu(x, approximate=True)

def _silu(x):
    return jax.nn.silu(x)

def _sigmoid(x):
    return jax.nn.sigmoid(x)

def _layernorm(x, axis=-1, eps=1e-05):
    m = jnp.mean(x, axis=axis, keepdims=True)
    v = jnp.var(x, axis=axis, keepdims=True)
    return (x - m) / jnp.sqrt(v + eps)

def _scatter_add(tgt, idx, src, axis=0):
    return tgt.at[idx].add(src)

def _segment_sum(src, seg, n):
    return jax.ops.segment_sum(src, seg, n)
kernel_name = 'mk_adj_preln_d4_adj_r2_3b94be'

def setup_inputs(seed: int=0):
    np.random.seed(seed)
    _w = jnp.asarray

    def _rec_inputs():
        import jax
        import jax.numpy as jnp
        _gk = jax.random.key(seed)
        x = -0.0005207 + 1.001 * jax.random.normal(jax.random.fold_in(_gk, 1), (8, 1024, 128), jnp.float32)
        _a = jax.random.bernoulli(jax.random.fold_in(_gk, 2), 0.00390625, (1024, 1024))
        _a = jnp.logical_or(_a, jnp.swapaxes(_a, -1, -2))
        _a = jnp.logical_or(_a, jnp.eye(1024, dtype=bool))
        adj = _a.astype(jnp.int32)
        return (x, adj)
    x, adj = _rec_inputs()

    def _L0_gnn_setup():
        import jax, jax.numpy as jnp
        import numpy as np
        NEG_BIG = -9000000000000000.0
        key = jax.random.key(seed)
        k1, k2, k3, k4, k5 = jax.random.split(key, 5)
        B, N, D_IN, D_HID, D_OUT = (4, 2048, 128, 64, 128)
        h = jax.random.normal(k1, (B, N, D_IN), dtype=jnp.float32)
        adj = jax.random.randint(k2, (N, N), 0, 2, dtype=jnp.int32)
        Ws = jax.random.normal(k3, (D_IN, D_HID), dtype=jnp.float32) * (1.414 / np.sqrt(D_IN))
        Wt = jax.random.normal(k4, (D_IN, D_HID), dtype=jnp.float32) * (1.414 / np.sqrt(D_IN))
        Wc = jax.random.normal(k5, (D_IN, D_OUT), dtype=jnp.float32) * np.sqrt(2.0 / D_IN)
        return {'h': h, 'adj': adj, 'Ws': Ws, 'Wt': Wt, 'Wc': Wc}
    _L0_gnn_all = _L0_gnn_setup()
    _L0_gnn_in = {k: v for k, v in _L0_gnn_all.items() if k in ('Ws', 'Wt', 'Wc')}
    del _L0_gnn_all

    def _L1_gnn_setup():
        import jax, jax.numpy as jnp
        import numpy as np
        IN_DIM = 128
        OUT_DIM = 128
        NUM_HEADS = 4
        HEAD_DIM = OUT_DIM // NUM_HEADS
        B, N = (2, 2048)
        key = jax.random.key(seed)
        ks = jax.random.split(key, 7)
        x = jax.random.normal(ks[0], (B, N, IN_DIM), dtype=jnp.float32)
        adjacency = jax.random.randint(ks[1], (N, N), 0, 2, dtype=jnp.int32)
        s = 1.0 / np.sqrt(IN_DIM)
        Wq = jax.random.normal(ks[2], (OUT_DIM, IN_DIM), dtype=jnp.float32) * s
        Wk = jax.random.normal(ks[3], (OUT_DIM, IN_DIM), dtype=jnp.float32) * s
        Wv = jax.random.normal(ks[4], (OUT_DIM, IN_DIM), dtype=jnp.float32) * s
        Wo = jax.random.normal(ks[5], (OUT_DIM, OUT_DIM), dtype=jnp.float32) * (1.0 / np.sqrt(OUT_DIM))
        bo = jax.random.normal(ks[6], (OUT_DIM,), dtype=jnp.float32) * 0.01
        return {'x': x, 'adjacency': adjacency, 'Wq': Wq, 'Wk': Wk, 'Wv': Wv, 'Wo': Wo, 'bo': bo}
    _L1_gnn_all = _L1_gnn_setup()
    _L1_gnn_in = {k: v for k, v in _L1_gnn_all.items() if k in ('Wq', 'Wk', 'Wv', 'Wo', 'bo')}
    del _L1_gnn_all

    def _L2_gnn_setup():
        import jax, jax.numpy as jnp
        import numpy as np
        ALPHA = 0.2
        LN_EPS = 1e-05
        NEG_INF = -9000000000000000.0
        key = jax.random.key(seed)
        ks = jax.random.split(key, 6)
        B, N, Fin, Fout = (8, 1024, 128, 128)
        x = jax.random.normal(ks[0], (B, N, Fin), dtype=jnp.float32)
        adj = jax.random.randint(ks[1], (N, N), 0, 2, dtype=jnp.int32)
        W = jax.random.normal(ks[2], (Fin, Fout), dtype=jnp.float32) * 0.05
        a = jax.random.normal(ks[3], (2 * Fout, 1), dtype=jnp.float32) * 0.05
        node_weights = jax.random.normal(ks[4], (N,), dtype=jnp.float32)
        node_bias = jnp.zeros((N,), dtype=jnp.float32)
        ln_gamma = jnp.ones((Fout,), dtype=jnp.float32)
        ln_beta = jnp.zeros((Fout,), dtype=jnp.float32)
        return {'x': x, 'adj': adj, 'W': W, 'a': a, 'node_weights': node_weights, 'node_bias': node_bias, 'ln_gamma': ln_gamma, 'ln_beta': ln_beta}
    _L2_gnn_all = _L2_gnn_setup()
    _L2_gnn_in = {k: v for k, v in _L2_gnn_all.items() if k in ('W', 'a', 'node_weights', 'node_bias', 'ln_gamma', 'ln_beta')}
    del _L2_gnn_all

    def _L3_gnn_setup():
        import jax, jax.numpy as jnp
        import numpy as np
        ALPHA = 0.2
        NEG_BIG = -9000000000000000.0
        key = jax.random.key(seed)
        k1, k2, k3, k4 = jax.random.split(key, 4)
        B, N, Fin, Fout = (8, 1024, 128, 128)
        h = jax.random.normal(k1, (B, N, Fin), dtype=jnp.float32)
        adj = jax.random.randint(k2, (N, N), 0, 2, dtype=jnp.int32)
        limW = 1.414 * np.sqrt(6.0 / (Fin + Fout))
        W = jax.random.uniform(k3, (Fin, Fout), minval=-limW, maxval=limW, dtype=jnp.float32)
        lima = 1.414 * np.sqrt(6.0 / (2 * Fout + 1))
        a = jax.random.uniform(k4, (2 * Fout, 1), minval=-lima, maxval=lima, dtype=jnp.float32)
        return {'h': h, 'adj': adj, 'W': W, 'a': a}
    _L3_gnn_all = _L3_gnn_setup()
    _L3_gnn_in = {k: v for k, v in _L3_gnn_all.items() if k in ('W', 'a')}
    del _L3_gnn_all
    return {'x': x, 'adj': adj, 'L0_gnn_Ws': _L0_gnn_in['Ws'], 'L0_gnn_Wt': _L0_gnn_in['Wt'], 'L0_gnn_Wc': _L0_gnn_in['Wc'], 'L1_gnn_Wq': _L1_gnn_in['Wq'], 'L1_gnn_Wk': _L1_gnn_in['Wk'], 'L1_gnn_Wv': _L1_gnn_in['Wv'], 'L1_gnn_Wo': _L1_gnn_in['Wo'], 'L1_gnn_bo': _L1_gnn_in['bo'], 'L2_gnn_W': _L2_gnn_in['W'], 'L2_gnn_a': _L2_gnn_in['a'], 'L2_gnn_node_weights': _L2_gnn_in['node_weights'], 'L2_gnn_node_bias': _L2_gnn_in['node_bias'], 'L2_gnn_ln_gamma': _L2_gnn_in['ln_gamma'], 'L2_gnn_ln_beta': _L2_gnn_in['ln_beta'], 'L3_gnn_W': _L3_gnn_in['W'], 'L3_gnn_a': _L3_gnn_in['a']}

def reference(x, adj, L0_gnn_Ws, L0_gnn_Wt, L0_gnn_Wc, L1_gnn_Wq, L1_gnn_Wk, L1_gnn_Wv, L1_gnn_Wo, L1_gnn_bo, L2_gnn_W, L2_gnn_a, L2_gnn_node_weights, L2_gnn_node_bias, L2_gnn_ln_gamma, L2_gnn_ln_beta, L3_gnn_W, L3_gnn_a):
    import jax
    import jax.numpy as jnp

    def _L0_gnn_ref(h, adj, Ws, Wt, Wc):
        import jax, jax.numpy as jnp
        import numpy as np
        NEG_BIG = -9000000000000000.0
        Whs = jnp.matmul(h, Ws)
        Wht = jnp.matmul(h, Wt)
        e = jnp.einsum('bnh,bmh->bnm', Whs, Wht)
        z = jnp.where(adj > 0, e, NEG_BIG)
        alpha = jax.nn.softmax(z, axis=-1)
        Whc = jnp.matmul(h, Wc)
        h_prime = jnp.matmul(alpha, Whc)
        return h_prime

    def _L1_gnn_ref(x, adjacency, Wq, Wk, Wv, Wo, bo):
        import jax, jax.numpy as jnp
        import numpy as np
        IN_DIM = 128
        OUT_DIM = 128
        NUM_HEADS = 4
        HEAD_DIM = OUT_DIM // NUM_HEADS
        B, N = (2, 2048)
        b, n, _ = x.shape

        def proj(W):
            return (x @ W.T).reshape(b, n, NUM_HEADS, HEAD_DIM).transpose(0, 2, 1, 3)
        Q, K, V = (proj(Wq), proj(Wk), proj(Wv))
        scores = jnp.einsum('bhnd,bhmd->bhnm', Q, K) / np.sqrt(HEAD_DIM)
        adj = (adjacency != 0)[None, None, :, :]
        scores = jnp.where(adj, scores, -jnp.inf)
        attn = jax.nn.softmax(scores, axis=-1)
        out = jnp.einsum('bhnm,bhmd->bhnd', attn, V)
        out = out.transpose(0, 2, 1, 3).reshape(b, n, NUM_HEADS * HEAD_DIM)
        return out @ Wo.T + bo

    def _L2_gnn_ref(x, adj, W, a, node_weights, node_bias, ln_gamma, ln_beta):
        import jax, jax.numpy as jnp
        import numpy as np
        ALPHA = 0.2
        LN_EPS = 1e-05
        NEG_INF = -9000000000000000.0
        x = x * node_weights[None, :, None] + node_bias[None, :, None] + x
        Fout = W.shape[1]
        h = jnp.einsum('bnf,fo->bno', x, W)
        mu = jnp.mean(h, axis=-1, keepdims=True)
        var = jnp.mean((h - mu) ** 2, axis=-1, keepdims=True)
        h = (h - mu) * jax.lax.rsqrt(var + LN_EPS) * ln_gamma + ln_beta
        residual = h
        a1, a2 = (a[:Fout, 0], a[Fout:, 0])
        s1 = h @ a1
        s2 = h @ a2
        e = jax.nn.leaky_relu(s1[:, :, None] + s2[:, None, :], negative_slope=ALPHA)
        attention = jnp.where(adj[None, :, :] > 0, e, NEG_INF)
        attention = jax.nn.softmax(attention, axis=-1)
        h_prime = jnp.einsum('bij,bjo->bio', attention, h) + residual
        return jax.nn.elu(h_prime)

    def _L3_gnn_ref(h, adj, W, a):
        import jax, jax.numpy as jnp
        import numpy as np
        ALPHA = 0.2
        NEG_BIG = -9000000000000000.0
        Wh = jnp.einsum('bnf,fo->bno', h, W)
        Fout = W.shape[1]
        a1, a2 = (a[:Fout, 0], a[Fout:, 0])
        s1 = Wh @ a1
        s2 = Wh @ a2
        e = s1[:, :, None] + s2[:, None, :]
        e = jnp.where(e > 0, e, ALPHA * e)
        e = jnp.where(adj[None, :, :] > 0, e, NEG_BIG)
        attention = jax.nn.softmax(e, axis=2)
        h_prime = jnp.einsum('bij,bjf->bif', attention, Wh)
        return h_prime
    h = jnp.maximum(_layernorm(x, axis=-1), 0.0)
    x = x + _L0_gnn_ref(h, adj, L0_gnn_Ws, L0_gnn_Wt, L0_gnn_Wc)
    h = jnp.maximum(_layernorm(x, axis=-1), 0.0)
    x = x + _L1_gnn_ref(h, adj, L1_gnn_Wq, L1_gnn_Wk, L1_gnn_Wv, L1_gnn_Wo, L1_gnn_bo)
    h = jnp.maximum(_layernorm(x, axis=-1), 0.0)
    x = x + _L2_gnn_ref(h, adj, L2_gnn_W, L2_gnn_a, L2_gnn_node_weights, L2_gnn_node_bias, L2_gnn_ln_gamma, L2_gnn_ln_beta)
    h = jnp.maximum(_layernorm(x, axis=-1), 0.0)
    x = x + _L3_gnn_ref(h, adj, L3_gnn_W, L3_gnn_a)
    return x

_drawn_inputs = setup_inputs


def setup_inputs(seed=0):
    import zlib

    import numpy as np

    out = dict(_drawn_inputs(seed))
    spreads = {'L2_gnn_node_bias': (0.0, 0.1),
     'L2_gnn_ln_gamma': (1.0, 0.2),
     'L2_gnn_ln_beta': (0.0, 0.1)}
    factors = {'L1_gnn_bo': 7.16}
    for name, (base, spread) in spreads.items():
        noise = np.random.default_rng([zlib.crc32(name.encode()), seed]).standard_normal(out[name].shape)
        drawn = base * np.exp(spread * noise) if base else spread * noise
        out[name] = jnp.asarray(drawn.astype(out[name].dtype))
    for name, factor in factors.items():
        out[name] = (out[name] * factor).astype(out[name].dtype)
    return out
```

```python
from contextlib import ExitStack

import numpy as np
import concourse.bass as bass
from concourse import mybir
from concourse.alu_op_type import AluOpType as ALU

ACT = mybir.ActivationFunctionType
F32, F16, BF16, I32 = mybir.dt.float32, mybir.dt.float16, mybir.dt.bfloat16, mybir.dt.int32

P = 128
B = 8
N = 1024
D = 128
T = N // P
HALF = 512
BIG = 1.0e30
EPS = 1e-5
SPLIT = 64.0
VSCALE = 256.0
SHIFT = 1024.0
PBIAS = float(12 * np.log(2.0))
ALPHA = 0.2


def build(nc, x, adj, adj_t, w_st, w_c, w_q, w_k, w_v, w_o, b_o, w_2, a_2, nw, nb, gamma, beta, w_3, w_3t, a_3, out):
    with ExitStack() as ctx:
        x_sb = ctx.enter_context(nc.sbuf_tensor("x_sb", [P, B * T, D], F32))
        mask_a = ctx.enter_context(nc.sbuf_tensor("mask_a", [P, T, N], BF16))
        mask_t = ctx.enter_context(nc.sbuf_tensor("mask_t", [P, T, N], BF16))
        ident_f = ctx.enter_context(nc.sbuf_tensor("ident_f", [P, P], F32))
        ident_b = ctx.enter_context(nc.sbuf_tensor("ident_b", [P, P], BF16))
        ident_h = ctx.enter_context(nc.sbuf_tensor("ident_h", [P, P], F16))
        shared = dict(x_sb=x_sb, mask_a=mask_a, mask_t=mask_t, ident_f=ident_f, ident_b=ident_b, ident_h=ident_h)
        set_up(nc, x, adj, adj_t, **shared)
        score_layer(nc, Score("L0", heads=1, maps=2, work_banks=1, rot=0, pool=(1, 3, 5, 7)),
                    dict(qk=[w_st], v=w_c), **shared)
        score_layer(nc, Score("L1", heads=4, maps=4, work_banks=2, rot=3, pool=(1, 3, 5, 7)),
                    dict(qk=[w_q, w_k], v=w_v, o=w_o, b=b_o), **shared)
        gat_layer(nc, Gat("L2", gated=True), dict(v=w_2, s=a_2, gate=nw, shift=nb, gamma=gamma, beta=beta), **shared)
        gat_layer(nc, Gat("L3", gated=False), dict(v=w_3, vt=w_3t, s=a_3), **shared)
        finish(nc, x_sb, out)


def set_up(nc, x, adj, adj_t, x_sb, mask_a, mask_t, ident_f, ident_b, ident_h):
    RING = 4
    with ExitStack() as ctx:
        ring = ctx.enter_context(nc.sbuf_tensor("adj_ring", [P, RING, N], I32))
        x_in = ctx.enter_context(nc.semaphore("x_in"))
        adj_in = [ctx.enter_context(nc.semaphore(f"adj_in{r}")) for r in range(RING)]
        masked = ctx.enter_context(nc.semaphore("masked"))
        blank = ctx.enter_context(nc.semaphore("blank"))
        block = ctx.enter_context(nc.Block())

        @block.sync
        def _(sp):
            for k in range(2 * T):
                if k >= RING:
                    sp.wait_ge(masked, k - RING + 1)
                src = (adj, adj_t)[k // T]
                nc.sync.dma_start(ring[:, k % RING], src[(k % T) * P:(k % T + 1) * P, :]).then_inc(adj_in[k % RING], 16)

        @block.scalar
        def _(act):
            for b in range(B):
                nc.scalar.dma_start(x_sb[:, b * T:(b + 1) * T], x[b].rearrange("(t p) d -> p t d", p=P)).then_inc(x_in, 16)
            act.wait_ge(x_in, 16 * B)

        @block.vector
        def _(dve):
            for k in range(2 * T):
                dve.wait_ge(adj_in[k % RING], 16 * (k // RING + 1))
                nc.vector.tensor_scalar((mask_a, mask_t)[k // T][:, k % T], ring[:, k % RING], 0.0, -BIG,
                                        ALU.is_le, ALU.mult).then_inc(masked, 1)

        @block.gpsimd
        def _(pool):
            for ident in (ident_f, ident_b, ident_h):
                nc.gpsimd.memset(ident[:], 0.0).then_inc(blank, 1)
            for k, ident in enumerate((ident_f, ident_b, ident_h)):
                pool.wait_ge(blank, k + 1)
                nc.gpsimd.affine_select(out=ident[:], in_=ident[:], compare_op=ALU.not_equal, fill=1.0,
                                        base=0, pattern=[[-1, P]], channel_multiplier=1)


class Score:

    LOW, AHEAD = 2, 3

    def __init__(self, name, heads, maps, work_banks, rot, pool):
        self.name, self.heads, self.maps, self.work_banks, self.rot, self.pool = name, heads, maps, work_banks, rot, pool
        self.batches = maps // heads
        self.iters = B // self.batches
        self.steps = T * maps
        self.dh = D // heads
        self.multi = heads > 1
        self.mrow = 96 if self.multi else 64
        self.projections = 4 if self.multi else 2
        self.vw = 2 * self.dh + 1
        self.aw = self.vw if self.multi else self.dh + 1
        self.acc_per_bank = 4 if self.multi else 3
        self.acc_banks = -(-T // self.acc_per_bank)
        self.root_lag = 2 if self.multi else 1
        self.pre = list(range(-(rot + 24) if self.multi else -(rot + 16), 0))

    def before(self, s, n):
        return divmod(s + self.rot + self.AHEAD + n, T)

    def norm_at(self, part, s, later=0):
        if self.multi:
            return 0 if part == "pre" and s == self.pre[0] + later else 1 if part == "body" and s == 1 + later else None
        m, t = self.before(s - later, 13)
        return m if t == 0 and m >= 0 and (part != "last" or m < self.maps) else None

    def work(self, part, s):
        prologue = [("T", 0), ("T", 1)] + [("QK", k) for k in range(self.projections)] + [("V", 0), ("V", 1)]
        if self.multi:
            if part == "pre" and s - self.pre[0] < 10:
                j = s - self.pre[0] - 2
                return [(kind, 0, k) for kind, k in prologue[j:j + 1]] if j >= 0 else []
            m, t = self.before(s, 11)
            got = [("S1", m, 2 * t), ("S1", m, 2 * t + 1)]
            m, t = self.before(s, 2)
            if t == 0:
                got += [("M", m, 0), ("M", m, 1)]
            got = [g for g in got if g[1] >= 0 and (part != "last" or g[1] < self.maps)]
            if part == "body" and 4 <= s < 12:
                got.append((prologue[s - 4][0], 1, prologue[s - 4][1]))
            if part != "pre":
                got += [("OT", 0, 0), ("OT", 0, 1)] if s == 30 else []
                got = ([("WO", 0, 0), ("WO", 0, 1)] if s == 31 else []) + got
            return got
        got = []
        for n, uses in ((7, [("S1", k) for k in (0, 1, 2)]), (6, [("S1", k) for k in (3, 4, 5)]),
                        (5, [("S1", k) for k in (6, 7, 8)]), (4, [("S1", k) for k in (9, 10, 11)]),
                        (3, [("S1", k) for k in (12, 13)]), (2, [("S1", k) for k in (14, 15)]),
                        (1, [("M", 0), ("M", 1)]), (11, [("T", 0)]), (10, [("T", 1)]), (9, [("QK", 0), ("QK", 1)]),
                        (8, [("V", 0), ("V", 1)])):
            m, t = self.before(s, n)
            if t == 0:
                got += [(kind, m, k) for kind, k in uses]
        return [g for g in got if g[1] >= 0 and (part != "last" or g[1] < self.maps)]

    def uses(self, part):
        steps = self.pre if part == "pre" else range(self.steps)
        return [g for s in steps for g in self.work(part, s)]


def rsqrt_steps(pool, nc, mean_var, rvar, guess, rstd, root_s, done, var_ready, tick):
    NEWTON = 4
    WAITS = 3 + 4 * NEWTON - 1

    tmp = guess[:].bitcast(F32)

    def inverse_root(b):
        k = [b * WAITS]

        def step(instruction):
            instruction.then_inc(root_s, 1)
            k[0] = k[0] + 1
            pool.wait_ge(root_s, k[0])
            pool.sem_inc(tick, 1)

        pool.wait_ge(var_ready, b + 1)
        pool.sem_inc(tick, 1)
        step(pool.tensor_scalar(rvar[:], mean_var[:, :, 1], EPS, None, ALU.add))
        step(pool.tensor_scalar(guess[:], rvar[:].bitcast(I32), -0.5, float(0x5F3759DF), ALU.mult, ALU.add))
        step(pool.tensor_copy(rstd[:].bitcast(I32), guess[:]))
        for n in range(NEWTON):
            step(pool.tensor_tensor(tmp, rstd[:], rstd[:], ALU.mult))
            step(pool.tensor_tensor(tmp, tmp, rvar[:], ALU.mult))
            step(pool.tensor_scalar(tmp, tmp, -0.5, 1.5, ALU.mult, ALU.add))
            y = pool.tensor_tensor(rstd[:], rstd[:], tmp, ALU.mult)
            if n < NEWTON - 1:
                step(y)
        y.then_inc(done, 1)

    return inverse_root


def score_layer(nc, sc, w, x_sb, mask_a, mask_t, ident_f, ident_b, ident_h):
    NS, S, L, dh, multi = sc.maps, sc.steps, sc.name, sc.dh, sc.multi
    PLACES = 4
    EXP_SCALE = 1.0 / SPLIT ** 2 / (float(np.sqrt(dh)) if multi else 1.0)
    KH = sc.projections + 2
    N_QK = len(w["qk"])
    N_ST = 1 if multi else 2
    S1_ROWS = [96] if multi else [128, 64]
    S2_ROWS = [97] if multi else [128, 65]
    USES = {part: sc.uses(part) for part in ("pre", "body", "last")}
    N_PRE, N_BODY = len(USES["pre"]), len(USES["body"])
    assert N_BODY % sc.work_banks == 0

    with ExitStack() as ctx:
        def sb(name, shape, dt):
            return ctx.enter_context(nc.sbuf_tensor(f"{L}_{name}", shape, dt))

        def ps(name, shape, dt=F32):
            return ctx.enter_context(nc.psum_tensor(f"{L}_{name}", shape, dt))

        def sem(name):
            return ctx.enter_context(nc.semaphore(f"{L}_{name}"))

        def sem_multi(name):
            return sem(name) if multi else None

        w_qk = [sb(f"w_qk{k}", [P, P], F32) for k in range(N_QK)]
        w_v = sb("w_v", [P, D], F32)
        stats = sb("stats", [P, T, 6], F32)
        mean_var = sb("mean_var", [P, T, 2], F32)
        rvar = sb("rvar", [P, T], F32)
        guess = sb("guess", [P, T], I32)
        rstd = sb("rstd", [P, T], F32)
        hn = sb("hn", [P, T, D], F32)
        h_t = sb("h_t", [P, N], F32)
        stage_hi = [sb(f"stage_hi{k}", [P, N], F16) for k in range(N_QK)]
        stage_lo = [sb(f"stage_lo{k}", [P, N], F16) for k in range(N_QK)]
        stage_v = sb("stage_v", [P, sc.heads, T, sc.vw], F16)
        st_q = [[sb(f"st_q{m}_{k}", [P, N], F16) for k in range(N_ST)] for m in range(NS)]
        st_k = [[sb(f"st_k{m}_{k}", [P, N], F16) for k in range(N_ST)] for m in range(NS)]
        v_sl = [sb(f"v{m}", [P, T, sc.vw], F16) for m in range(NS)]
        junk = sb("junk", [P, sc.work_banks, HALF], BF16)
        mx_half = sb("mx_half", [P, NS, 2, T], F32)
        mx = sb("mx", [P, NS, T], F32)
        mneg = sb("mneg", [P, NS, T], F16)
        pbias = sb("pbias", [P, 1], F32)
        p32 = sb("p32", [P, PLACES, N], F32)
        p_hi = sb("p_hi", [P, PLACES, N], F16)
        p_lo = sb("p_lo", [P, PLACES, N], F16)
        rec = sb("rec", [P, T], F32)
        if multi:
            w_o = sb("w_o", [P, D], F32)
            b_o = sb("b_o", [P, D], F32)
            lo_sum = sb("lo_sum", [P, T, dh], F32)
            num = sb("num", [P, T, dh], F32)
            o = sb("o", [P, T, D], F32)
            o_t = sb("o_t", [P, N], F32)

        s2 = ps("s2", [P, 2, N])
        wk = ps("wk", [P, sc.work_banks, HALF])
        acc = ps("acc", [P, sc.acc_banks, HALF])

        def acc_tile(t, a, b):
            base = (t % sc.acc_per_bank) * sc.aw
            return acc[:, t // sc.acc_per_bank, base + a:base + b]

        def acc_cols(bank, a, b):
            n = min(sc.acc_per_bank, T - bank * sc.acc_per_bank)
            tiles = slice(bank * sc.acc_per_bank, bank * sc.acc_per_bank + n)
            return acc[:, bank, 0:n * sc.aw].rearrange("p (t c) -> p t c", t=n)[:, :, a:b], tiles

        w_in = sem("w_in")
        ready = sem("ready")
        tick_dve = sem("tick_dve")
        tick_pool = sem("tick_pool")
        stat_s = sem("stat_s")
        var_ready = sem("var_ready")
        root_s = sem("root_s")
        rstd_ready = sem("rstd_ready")
        ln_ready = sem("ln_ready")
        wk_full = sem("wk_full")
        hi_done = sem("hi_done")
        h_ready = sem("h_ready")
        qk_ready = sem("qk_ready")
        v_ready = sem("v_ready")
        s1_done = sem("s1_done")
        m_row = sem("m_row")
        ot_ready = sem_multi("ot_ready")
        x_done = sem_multi("x_done")
        st_in = [sem(f"st_in{m}") for m in range(NS)]
        v_in = [sem(f"v_in{m}") for m in range(NS)]
        mx_s = sem("mx_s")
        m_col = sem("m_col")
        s2_full = sem("s2_full")
        p32_done = sem("p32_done")
        phi_done = sem("phi_done")
        plo_dve = sem("plo_dve")
        plo_pool = sem("plo_pool")
        av_done = sem("av_done")
        acc_lo = sem_multi("acc_lo")
        ep_s = sem("ep_s")
        acc_free = sem("acc_free")
        o_ready = sem_multi("o_ready")
        xb_ready = sem_multi("xb_ready")

        def map_no(i, m):
            return i * NS + m

        def batch_no(i, m):
            return i * sc.batches + m // sc.heads

        def wait_released(eng, i, kind, m, k):
            if kind == "T":
                eng.wait_ge(h_ready, 2 * (i * sc.batches + m) + k + 1)
            elif kind == "QK":
                eng.wait_ge(qk_ready, sc.projections * (i * sc.batches + m) + k + 1)
            elif kind == "V":
                eng.wait_ge(v_ready, 2 * (i * sc.batches + m) + k + 1)
            elif kind == "S1":
                eng.wait_ge(s1_done, 2 * T * map_no(i, m) + k + 1)
            elif kind == "M":
                eng.wait_ge(m_row, 2 * map_no(i, m) + k + 1)
            elif kind == "OT":
                eng.wait_ge(ot_ready, 2 * i + k + 1)
            elif kind == "WO":
                eng.wait_ge(x_done, 2 * i + k + 1)

        def use_no(part, i, n):
            return n if part == "pre" else N_PRE + i * N_BODY + n

        def bank_of(part, n):
            return (n if part == "pre" else N_PRE + n) % sc.work_banks

        def pooled(t):
            return sum(a <= t for a in sc.pool)

        def wait_low(eng, i, u):
            m, t = divmod(u, T)
            if t in sc.pool:
                eng.wait_ge(plo_pool, map_no(i, m) * pooled(T - 1) + pooled(t))
            else:
                eng.wait_ge(plo_dve, map_no(i, m) * (T - pooled(T - 1)) + t + 1 - pooled(t))

        def parts(eng, body):
            body("pre", 0, sc.pre)
            with eng.Fori(0, sc.iters - 1) as i:
                body("body", i, range(S))
            body("last", sc.iters - 1, range(S))

        def has(part, u):
            return u >= 0 and (part != "last" or u < S)

        def ordered(part, s):
            got = [(kind, m, k) for kind, m, k in sc.work(part, s)]
            if has(part, s + sc.rot):
                got.insert(2, ("values", 0, 0))
            if has(part, s + sc.rot + sc.AHEAD):
                got.insert(sc.work_banks == 1, ("scores", 0, 0))
            return got

        block = ctx.enter_context(nc.Block())

        @block.sync
        def _(sp):
            for dst, src in [*zip(w_qk, w["qk"]), (w_v, w["v"])] + ([(w_o, w["o"]), (b_o, w["b"])] if multi else []):
                sp.dma_start(dst[:], src).then_inc(w_in, 16)
            sp.wait_ge(ready, 1)

            def fill_stack(i, m):
                slot, h = m % NS, m % sc.heads
                sp.wait_ge(qk_ready, sc.projections * batch_no(i, m) + sc.projections)
                if multi:
                    rows = slice(h * dh, (h + 1) * dh)
                    moves = [(st_q[slot][0], stage_hi[0], rows, 0), (st_q[slot][0], stage_hi[0], rows, dh),
                             (st_q[slot][0], stage_lo[0], rows, 2 * dh), (st_k[slot][0], stage_hi[1], rows, 0),
                             (st_k[slot][0], stage_lo[1], rows, dh), (st_k[slot][0], stage_hi[1], rows, 2 * dh)]
                else:
                    q, k = slice(0, 64), slice(64, 128)
                    moves = [(st_q[slot][0], stage_hi[0], q, 0), (st_q[slot][0], stage_lo[0], q, 64),
                             (st_k[slot][0], stage_hi[0], k, 0), (st_k[slot][0], stage_hi[0], k, 64),
                             (st_q[slot][1], stage_hi[0], q, 0), (st_k[slot][1], stage_lo[0], k, 0)]
                for dst, src, rows, at in moves:
                    sp.dma_start(dst[at:at + rows.stop - rows.start, :], src[rows, :]).then_inc(st_in[slot], 16)

            def fill_values(i, m):
                sp.wait_ge(v_ready, 2 * batch_no(i, m) + 2)
                sp.dma_start(v_sl[m % NS][:], stage_v[:, m % sc.heads]).then_inc(v_in[m % NS], 16)

            def body(part, i, steps):
                for s in steps:
                    if multi and part == "pre" and s == steps[0]:
                        for m in range(NS):
                            fill_stack(i, m)
                            fill_values(i, m)
                    elif multi and part == "body" and s == 0:
                        for m in range(NS):
                            sp.wait_ge(av_done, (map_no(i, m) + 1) * T)
                            fill_stack(i, NS + m)
                            fill_values(i, NS + m)
                    elif not multi:
                        m, t = sc.before(s, 8)
                        if t == 0 and m >= 0 and (part != "last" or m < NS):
                            if m >= NS:
                                sp.wait_ge(s2_full, map_no(i, m - 1) * T)
                            fill_stack(i, m)
                        m, t = sc.before(s, 6)
                        if t == 0 and m >= 0 and (part != "last" or m < NS):
                            if m >= NS:
                                sp.wait_ge(av_done, map_no(i, m - 1) * T)
                            fill_values(i, m)

            parts(sp, body)

        @block.tensor
        def _(pe):
            pe.wait_ge(ready, 2)

            def take_bank(part, i, n):
                uses, back = USES[part], n - sc.work_banks
                if back >= 0:
                    wait_released(pe, i, *uses[back])
                elif part != "pre":
                    wait_released(pe, 0, *USES["pre"][N_PRE + back])
                    wait_released(pe, i - 1, *USES["body"][N_BODY + back])
                return wk[:, bank_of(part, n)]

            def work(part, i, n, kind, m, k):
                bank = take_bank(part, i, n)
                if kind == "T":
                    pe.wait_ge(ln_ready, T * (i * sc.batches + m) + 4 * k + 4)
                    for t in range(4):
                        last = pe.transpose(bank[:, t * P:(t + 1) * P], hn[:, 4 * k + t], ident_f[:])
                elif kind == "QK":
                    pe.wait_ge(h_ready, 2 * (i * sc.batches + m) + 2)
                    last = pe.matmul(bank, w_qk[k // 2][:], h_t[:, k % 2 * HALF:(k % 2 + 1) * HALF], start=True,
                                     stop=True)
                elif kind == "V":
                    for t in range(4):
                        last = pe.matmul(bank[:, t * P:(t + 1) * P], h_t[:, (4 * k + t) * P:(4 * k + t + 1) * P], w_v[:],
                                         start=(t == 0), stop=(t == 3), skip_group_check=True)
                elif kind == "S1":
                    slot, t, half = m % NS, k // 2, k % 2
                    if k == 0:
                        pe.wait_ge(st_in[slot], (i + m // NS + 1) * 6 * 16)
                    for j, r in enumerate(S1_ROWS):
                        last = pe.matmul(bank, st_q[slot][j][0:r, t * P:(t + 1) * P],
                                         st_k[slot][j][0:r, half * HALF:(half + 1) * HALF],
                                         start=(j == 0), stop=(j == N_ST - 1))
                elif kind == "M":
                    pe.wait_ge(m_col, map_no(i, m) + 1)
                    for t in range(4):
                        last = pe.matmul(bank[sc.mrow:sc.mrow + 1, t * P:(t + 1) * P],
                                         mneg[:, m % NS, 4 * k + t:4 * k + t + 1], ident_h[:], start=(t == 0),
                                         stop=(t == 3), skip_group_check=True)
                elif kind == "OT":
                    pe.wait_ge(o_ready, map_no(i, NS))
                    for t in range(4):
                        last = pe.transpose(bank[:, t * P:(t + 1) * P], o[:, 4 * k + t], ident_f[:])
                elif kind == "WO":
                    pe.wait_ge(ot_ready, 2 * i + k + 1)
                    for t in range(4):
                        last = pe.matmul(bank[:, t * P:(t + 1) * P], o_t[:, (4 * k + t) * P:(4 * k + t + 1) * P], w_o[:],
                                         start=(t == 0), stop=(t == 3), skip_group_check=True)
                last.then_inc(wk_full, 1)

            def values(part, i, u):
                m, t = divmod(u, T)
                slot = m % NS
                if t == 0:
                    pe.wait_ge(v_in[slot], (i + m // NS + 1) * 16)
                    pe.wait_ge(acc_free, map_no(i, m) + 1)
                pe.wait_ge(phi_done, i * S + u + 1)
                wait_low(pe, i, u)
                v = v_sl[slot]
                for n in range(T):
                    hi = p_hi[:, u % PLACES, n * P:(n + 1) * P]
                    lo = p_lo[:, u % PLACES, n * P:(n + 1) * P]
                    first = t == 0 and n % sc.acc_per_bank == 0
                    pe.matmul(acc_tile(n, 0, sc.aw), hi, v[:, t, 0:sc.aw], start=first, stop=False,
                              skip_group_check=True)
                    if not multi:
                        pe.matmul(acc_tile(n, 0, dh), hi, v[:, t, dh + 1:], start=False, stop=False,
                                  skip_group_check=True)
                    last = pe.matmul(acc_tile(n, 0, dh + 1), lo, v[:, t, 0:dh + 1], start=False, stop=(t == T - 1),
                                     skip_group_check=True)
                last.then_inc(av_done, 1)

            def scores(part, i, u):
                m, t = divmod(u, T)
                slot = m % NS
                if u >= 2:
                    pe.wait_ge(phi_done, i * S + u - 1)
                if t == 0:
                    pe.wait_ge(m_row, 2 * map_no(i, m) + 2)
                for half in range(2):
                    cols = slice(half * HALF, (half + 1) * HALF)
                    pe.matmul(s2[:, u % 2, cols], ident_b[:], mask_t[:, t, cols], start=True, stop=False)
                    for j, r in enumerate(S2_ROWS):
                        last = pe.matmul(s2[:, u % 2, cols], st_k[slot][j][0:r, t * P:(t + 1) * P],
                                         st_q[slot][j][0:r, cols], start=False, stop=(j == N_ST - 1))
                last.then_inc(s2_full, 1)

            def body(part, i, steps):
                n = 0
                for s in steps:
                    for kind, m, k in ordered(part, s):
                        if kind == "scores":
                            scores(part, i, s + sc.rot + sc.AHEAD)
                        elif kind == "values":
                            values(part, i, s + sc.rot)
                        else:
                            work(part, i, n, kind, m, k)
                            n += 1

            parts(pe, body)

        @block.scalar
        def _(act):
            act.wait_ge(ready, 1)

            def work(part, i, n, kind, m, k):
                bank = wk[:, bank_of(part, n)]
                act.wait_ge(wk_full, use_no(part, i, n) + 1)
                b = i * sc.batches + m
                if kind == "T":
                    act.activation(h_t[:, k * HALF:(k + 1) * HALF], bank, ACT.Relu).then_inc(h_ready, 1)
                elif kind == "OT":
                    act.activation(o_t[:, k * HALF:(k + 1) * HALF], bank, ACT.Copy).then_inc(ot_ready, 1)
                elif kind == "QK":
                    if k == 0 and not (part == "pre" and m == 0):
                        for slot in (range(NS) if multi else [(m - 1) % NS]):
                            act.wait_ge(st_in[slot], (i + 1 if multi else i + (m - 1) // NS + 1) * 6 * 16)
                    act.activation(stage_hi[k // 2][:, k % 2 * HALF:(k % 2 + 1) * HALF], bank, ACT.Copy)\
                       .then_inc(hi_done, 1)
                elif kind == "V":
                    if k == 0 and not (part == "pre" and m == 0):
                        for slot in (range(NS) if multi else [(m - 1) % NS]):
                            act.wait_ge(v_in[slot], (i + 1 if multi else i + (m - 1) // NS + 1) * 16)
                    act.activation(stage_v[:, :, 4 * k:4 * k + 4, 0:dh].rearrange("p h t d -> p t h d"),
                                   bank.rearrange("p (t h d) -> p t h d", t=4, h=sc.heads), ACT.Copy)\
                       .then_inc(hi_done, 1)

            def probabilities(part, i, u):
                act.wait_ge(s2_full, i * S + u + 1)
                if u >= PLACES:
                    wait_low(act, i, u - PLACES)
                act.activation(p32[:, u % PLACES], s2[:, u % 2], ACT.Exp, bias=pbias[:], scale=EXP_SCALE)\
                   .then_inc(p32_done, 1)
                act.activation(p_hi[:, u % PLACES], s2[:, u % 2], ACT.Exp, bias=pbias[:], scale=EXP_SCALE)\
                   .then_inc(phi_done, 1)

            def low_columns(i, m):
                act.wait_ge(av_done, (map_no(i, m) + 1) * T)
                act.wait_ge(acc_free, map_no(i, m) + 1)
                for bank in range(sc.acc_banks):
                    src, tiles = acc_cols(bank, dh + 1, sc.aw)
                    act.activation(lo_sum[:, tiles], src, ACT.Copy).then_inc(acc_lo, 1)

            def body(part, i, steps):
                n = 0
                for s in steps:
                    for kind, m, k in ordered(part, s):
                        if kind == "scores":
                            probabilities(part, i, s + sc.rot + sc.AHEAD)
                        elif kind != "values":
                            if kind in ("T", "QK", "V", "OT"):
                                work(part, i, n, kind, m, k)
                            n += 1
                    u = s + sc.rot
                    if multi and has(part, u) and u % T == T - 1:
                        low_columns(i, u // T)

            parts(act, body)

        @block.vector
        def _(dve):
            dve.memset(pbias[:], PBIAS).then_inc(acc_free, 1)
            for m in range(NS):
                dve.memset(st_k[m][-1][sc.mrow:sc.mrow + 1, :], SHIFT)
            dve.memset(stage_v[:, :, :, dh], VSCALE).then_inc(ready, 1)
            dve.wait_ge(w_in, 16 * (N_QK + 1 + 2 * multi))
            for t in w_qk:
                dve.tensor_scalar(t[:], t[:], SPLIT, None, ALU.mult)
            dve.tensor_scalar(w_v[:], w_v[:], VSCALE, None, ALU.mult).then_inc(ready, 1)

            def norm_stats(i, m):
                b = i * sc.batches + m
                dve.wait_ge(ln_ready, T * b)
                for t in range(T):
                    last = dve.bn_stats(stats[:, t], x_sb[:, b * T + t])
                last.then_inc(stat_s, 1)
                dve.wait_ge(stat_s, b + 1)
                dve.sem_inc(tick_dve, 1)
                for t in range(T):
                    last = dve.bn_aggr(mean_var[:, t], stats[:, t])
                last.then_inc(var_ready, 1)

            def norm_rows(i, m):
                b = i * sc.batches + m
                dve.wait_ge(rstd_ready, b + 1)
                dve.wait_ge(h_ready, 2 * b)
                for t in range(T):
                    dve.tensor_scalar(hn[:, t], x_sb[:, b * T + t], mean_var[:, t, 0:1], rstd[:, t:t + 1],
                                      ALU.subtract, ALU.mult).then_inc(ln_ready, 1)

            def work(part, i, n, kind, m, k):
                bank = wk[:, bank_of(part, n)]
                half = slice(k % 2 * HALF, (k % 2 + 1) * HALF)
                if kind == "QK":
                    dve.wait_ge(hi_done, (i * sc.batches + m) * KH + k + 1)
                    dve.tensor_tensor(stage_lo[k // 2][:, half], bank, stage_hi[k // 2][:, half], ALU.subtract)\
                       .then_inc(qk_ready, 1)
                elif kind == "V":
                    dve.wait_ge(hi_done, (i * sc.batches + m) * KH + sc.projections + k + 1)
                    tiles = slice(4 * k, 4 * k + 4)
                    dve.tensor_tensor(stage_v[:, :, tiles, dh + 1:].rearrange("p h t d -> p t h d"),
                                      bank.rearrange("p (t h d) -> p t h d", t=4, h=sc.heads),
                                      stage_v[:, :, tiles, 0:dh].rearrange("p h t d -> p t h d"),
                                      ALU.subtract).then_inc(v_ready, 1)
                elif kind == "S1":
                    g = m % NS
                    dve.wait_ge(wk_full, use_no(part, i, n) + 1)
                    dve.sem_inc(tick_dve, 1)
                    dve.tensor_tensor_reduce(junk[:, bank_of(part, n)], bank, mask_a[:, k // 2, half], 1.0, -3.0e38, ALU.add, ALU.max,
                                             mx_half[:, g, k % 2, k // 2:k // 2 + 1]).then_inc(s1_done, 1)
                    if k == 2 * T - 1:
                        dve.wait_ge(s1_done, 2 * T * (map_no(i, m) + 1))
                        dve.tensor_tensor(mx[:, g], mx_half[:, g, 0], mx_half[:, g, 1], ALU.max).then_inc(mx_s, 1)
                        dve.wait_ge(mx_s, map_no(i, m) + 1)
                        dve.tensor_scalar(mneg[:, g], mx[:, g], -1.0 / SHIFT, None, ALU.mult).then_inc(m_col, 1)
                elif kind == "M":
                    dve.wait_ge(wk_full, use_no(part, i, n) + 1)
                    dve.tensor_copy(st_q[m % NS][-1][sc.mrow:sc.mrow + 1, half], bank[sc.mrow:sc.mrow + 1, :])\
                       .then_inc(m_row, 1)
                elif kind == "WO":
                    dve.wait_ge(wk_full, use_no(part, i, n) + 1)
                    dve.wait_ge(xb_ready, i + 1)
                    xs = x_sb[:, bass.ds(i * T + 4 * k, 4)]
                    dve.tensor_tensor(xs, xs, bank.rearrange("p (t d) -> p t d", t=4), ALU.add).then_inc(x_done, 1)

            def low_parts(i, u):
                dve.wait_ge(phi_done, i * S + u + 1)
                dve.tensor_tensor(p_lo[:, u % PLACES], p32[:, u % PLACES], p_hi[:, u % PLACES], ALU.subtract)\
                   .then_inc(plo_dve, 1)

            def head_output(i, m):
                g, h = map_no(i, m), m % sc.heads
                for bank in range(sc.acc_banks):
                    dve.wait_ge(acc_lo, g * sc.acc_banks + bank + 1)
                    hi, tiles = acc_cols(bank, 0, dh)
                    dve.tensor_tensor(num[:, tiles], hi, lo_sum[:, tiles], ALU.add)
                    den, tiles = acc_cols(bank, dh, dh + 1)
                    last = dve.reciprocal(rec[:, tiles].unsqueeze(2), den)
                last.then_inc(acc_free, 1)
                dve.wait_ge(acc_free, g + 2)
                dve.tensor_tensor(o[:, :, h * dh:(h + 1) * dh], num[:], rec[:].unsqueeze(2).to_broadcast([P, T, dh]),
                                  ALU.mult).then_inc(o_ready, 1)

            def batch_output(i, m):
                g = map_no(i, m)
                dve.wait_ge(av_done, (g + 1) * T)
                for bank in range(sc.acc_banks):
                    den, tiles = acc_cols(bank, dh, dh + 1)
                    last = dve.reciprocal(rec[:, tiles].unsqueeze(2), den)
                last.then_inc(ep_s, 1)
                dve.wait_ge(ep_s, g + 1)
                for t in range(T):
                    xs = x_sb[:, g * T + t]
                    last = dve.scalar_tensor_tensor(out=xs, in0=acc_tile(t, 0, dh), scalar=rec[:, t:t + 1], in1=xs,
                                                    op0=ALU.mult, op1=ALU.add)
                last.then_inc(acc_free, 1)

            def body(part, i, steps):
                n = 0
                for s in steps:
                    u = s + sc.rot
                    uses = sc.work(part, s)
                    for kind, m, k in uses[:2]:
                        work(part, i, n, kind, m, k)
                        n += 1
                    if has(part, u + sc.LOW) and (u + sc.LOW) % T not in sc.pool:
                        low_parts(i, u + sc.LOW)
                    for kind, m, k in uses[2:]:
                        work(part, i, n, kind, m, k)
                        n += 1
                    if sc.norm_at(part, s) is not None:
                        norm_stats(i, sc.norm_at(part, s))
                    if sc.norm_at(part, s, sc.root_lag) is not None:
                        norm_rows(i, sc.norm_at(part, s, sc.root_lag))
                    if has(part, u) and u % T == T - 1:
                        (head_output if multi else batch_output)(i, u // T)

            parts(dve, body)

        @block.gpsimd
        def _(pool):
            if multi:
                pool.wait_ge(w_in, 16 * (N_QK + 3))

            def low_parts(i, u):
                pool.wait_ge(phi_done, i * S + u + 1)
                pool.tensor_tensor(p_lo[:, u % PLACES], p32[:, u % PLACES], p_hi[:, u % PLACES], ALU.subtract)\
                    .then_inc(plo_pool, 1)

            inverse_root = rsqrt_steps(pool, nc, mean_var, rvar, guess, rstd, root_s, rstd_ready, var_ready, tick_pool)

            def add_bias(b):
                pool.wait_ge(ln_ready, T * (b + 1))
                xs = x_sb[:, bass.ds(b * T, T)]
                pool.tensor_tensor(xs, xs, b_o[:].unsqueeze(1).to_broadcast([P, T, D]), ALU.add).then_inc(xb_ready, 1)

            def body(part, i, steps):
                for s in steps:
                    if sc.norm_at(part, s) is not None:
                        inverse_root(i * sc.batches + sc.norm_at(part, s))
                    if multi and sc.norm_at(part, s, sc.root_lag + 1) is not None:
                        add_bias(i + sc.norm_at(part, s, sc.root_lag + 1))
                    u = s + sc.rot + sc.LOW
                    if has(part, u) and u % T in sc.pool:
                        low_parts(i, u)

            parts(pool, body)


def finish(nc, x_sb, out):
    with nc.semaphore("stored") as stored, nc.Block() as block:
        @block.sync
        def _(sp):
            for b in range(B):
                sp.dma_start(out[b].rearrange("(t p) d -> p t d", p=P), x_sb[:, b * T:(b + 1) * T]).then_inc(stored, 16)
            sp.wait_ge(stored, 16 * B)


class Gat:
    maps, steps, iters, LAG = 2, 2 * T, B // 2, 2

    def __init__(self, name, gated):
        self.name, self.gated = name, gated
        self.pre = list(range(-16, 0))
        first = -13 if gated else -11
        self.order = {first: [("T", 0), ("T", 1)], first + 1: [("V", 0), ("V", 1)],
                      -8: [("SB", 0), ("SB", 1)], -7: [("SC", 0), ("SA", 0), ("SA", 1)],
                      -2: [("CR", 0), ("CR", 1)]}
        if gated:
            self.order[-9] = [("T2", 0), ("T2", 1)]
        self.first = first

    def lead(self, part, s, n):
        m, t = divmod(s + self.LAG + n, T)
        return m if t == 0 and m >= 0 and (part != "last" or m < self.maps) else None

    def work(self, part, s):
        return [(kind, self.lead(part, s, -at), k) for at in sorted(self.order, reverse=True)
                if self.lead(part, s, -at) is not None for kind, k in self.order[at]]

    def uses(self, part):
        steps = self.pre if part == "pre" else range(self.steps)
        return [g for s in steps for g in self.work(part, s)]


def gat_layer(nc, sc, w, x_sb, mask_a, mask_t, ident_f, ident_b, ident_h):
    S, L, gated, NS = sc.steps, sc.name, sc.gated, sc.maps
    PLACES = 4
    USES = {part: sc.uses(part) for part in ("pre", "body", "last")}
    N_PRE, N_BODY = len(USES["pre"]), len(USES["body"])
    VW = D + 1
    APB = 3
    ACC_BANKS = -(-T // APB)

    with ExitStack() as ctx:
        def sb(name, shape, dt):
            return ctx.enter_context(nc.sbuf_tensor(f"{L}_{name}", shape, dt))

        def ps(name, shape, dt=F32):
            return ctx.enter_context(nc.psum_tensor(f"{L}_{name}", shape, dt))

        def sem(name):
            return ctx.enter_context(nc.semaphore(f"{L}_{name}"))

        def sem_gated(name):
            return sem(name) if gated else None

        w_v = sb("w_v", [P, D], F32)
        w_s = sb("w_s", [P, 2], F32)
        w_r = sb("w_r", [P, 2, P], F32)
        stats = sb("stats", [P, T, 6], F32)
        mean_var = sb("mean_var", [P, T, 2], F32)
        rvar = sb("rvar", [P, T], F32)
        guess = sb("guess", [P, T], I32)
        rstd = sb("rstd", [P, T], F32)
        hn = sb("hn", [P, T, D], F32)
        h_t = sb("h_t", [P, N], F32)
        stage_v = sb("stage_v", [P, T, VW], F32)
        v_sl = [sb(f"v{m}", [P, T, VW], F32) for m in range(2)]
        s1_col = sb("s1_col", [P, 2, T], F32)
        s2_rise = sb("s2_rise", [P, 2, T], F32)
        s2_slope = sb("s2_slope", [P, 2, T], F32)
        s2_all = sb("s2_all", [P, 2, N], F32)
        s1_all = sb("s1_all", [P, 2, N], F32)
        c_row = sb("c_row", [1, 2, N], F16)
        ones = sb("ones", [1, P], F16)
        junk = sb("junk", [P, 2, N], BF16)
        g_max = sb("g_max", [P, 2, T], F32)
        top = sb("top", [P, 2, T], F32)
        most = sb("most", [P, 2, T], F32)
        c_col = sb("c_col", [P, 2, T], F16)
        r = sb("r", [P, PLACES, N], F32)
        z = sb("z", [P, PLACES, N], F32)
        p = sb("p", [P, PLACES, N], F32)
        rec = sb("rec", [P, T], F32)
        if gated:
            gate, shift = sb("gate", [P, T], F32), sb("shift", [P, T], F32)
            gamma, beta = sb("gamma", [P, D], F32), sb("beta", [P, D], F32)
            raw = sb("raw", [P, T, D], F32)
            v_t = sb("v_t", [P, N], F32)
            stats2 = sb("stats2", [P, T, 6], F32)
            mean_var2 = sb("mean_var2", [P, T, 2], F32)
            rvar2 = sb("rvar2", [P, T], F32)
            guess2 = sb("guess2", [P, T], I32)
            rstd2 = sb("rstd2", [P, T], F32)
            hp = sb("hp", [P, T, D], F32)
            neg = sb("neg", [P, T, D], F32)
        else:
            w_vt, a_s = sb("w_vt", [P, D], F32), sb("a_s", [P, 2], F32)
            v_t = h_t

        s2 = ps("s2", [P, 2, N])
        wk = ps("wk", [P, HALF])
        acc = ps("acc", [P, ACC_BANKS, HALF])

        def acc_tile(t, a, b):
            return acc[:, t // APB, t % APB * VW + a:t % APB * VW + b]

        w_in = sem("w_in")
        ready = sem("ready")
        fold = sem("fold")
        tick_dve, tick_pool, tick_sp = sem("tick_dve"), sem("tick_pool"), sem("tick_sp")
        stat_s = sem("stat_s")
        var_ready = sem("var_ready")
        root_s = sem("root_s")
        rstd_ready = sem("rstd_ready")
        ln_dve = sem("ln_dve")
        ln_ready = sem("ln_ready") if gated else ln_dve
        wk_full = sem("wk_full")
        h_ready = sem("h_ready")
        v_ready = sem("v_ready")
        st2_s = sem_gated("st2_s")
        var2_ready = sem_gated("var2_ready")
        root2_s = sem_gated("root2_s")
        rstd2_ready = sem_gated("rstd2_ready")
        n2_ready = sem_gated("n2_ready")
        gb_s = sem_gated("gb_s")
        staged = sem("staged") if gated else v_ready
        per_stage = 1 if gated else 2
        t2_ready = sem_gated("t2_ready")
        sc_ready = sem("sc_ready")
        sb_ready = sem("sb_ready")
        sa_ready = sem("sa_ready")
        cr_ready = sem("cr_ready")
        v_in = [sem(f"v_in{m}") for m in range(2)]
        g_done = sem("g_done")
        top_s = sem("top_s")
        c_ready = sem("c_ready")
        s2_full = sem("s2_full")
        r_done = sem("r_done")
        z_done = sem("z_done")
        p_done = sem("p_done")
        av_done = sem("av_done")
        rec_s = sem_gated("rec_s")
        x_out = sem_gated("x_out")
        acc_free = sem("acc_free")
        neg_s = sem_gated("neg_s")
        elu_ready = sem_gated("elu_ready")
        xa_s = sem("xa_s")

        def wait_released(eng, i, kind, m, k):
            b = i * NS + m
            if kind == "T":
                eng.wait_ge(h_ready, 2 * b + k + 1)
            elif kind == "V":
                eng.wait_ge(v_ready, 2 * b + k + 1)
            elif kind == "T2":
                eng.wait_ge(t2_ready, 2 * b + k + 1)
            elif kind == "SC":
                eng.wait_ge(sc_ready, b + 1)
            elif kind == "SB":
                eng.wait_ge(sb_ready, 2 * b + k + 1)
            elif kind == "SA":
                eng.wait_ge(sa_ready, 2 * b + k + 1)
            elif kind == "CR":
                eng.wait_ge(cr_ready, 2 * b + k + 1)

        def use_no(part, i, n):
            return n if part == "pre" else N_PRE + i * N_BODY + n

        def parts(eng, body):
            body("pre", 0, sc.pre)
            with eng.Fori(0, sc.iters - 1) as i:
                body("body", i, range(S))
            body("last", sc.iters - 1, range(S))

        def has(part, u):
            return u >= 0 and (part != "last" or u < S)

        block = ctx.enter_context(nc.Block())

        @block.sync
        def _(sp):
            loads = [(w_v, w["v"])]
            loads += [(w_s, w["s"]), (gate, w["gate"]), (shift, w["shift"]), (gamma, w["gamma"]), (beta, w["beta"])] \
                if gated else [(w_vt, w["vt"]), (a_s, w["s"])]
            for dst, src in loads:
                sp.dma_start(dst[:], src).then_inc(w_in, 16)
            sp.wait_ge(ready, 2)

            def body(part, i, steps):
                for s in steps:
                    m = sc.lead(part, s, 6)
                    if m is not None:
                        sp.wait_ge(staged, per_stage * (i * NS + m + 1))
                        sp.sem_inc(tick_sp, 1)
                        if part != "pre":
                            sp.wait_ge(acc_free, i * NS + m)
                        sp.dma_start(v_sl[m % 2][:], stage_v[:]).then_inc(v_in[m % 2], 16)

            parts(sp, body)

        @block.tensor
        def _(pe):
            if gated:
                pe.wait_ge(ready, 3)
            else:
                pe.wait_ge(w_in, 16 * 3)
                pe.matmul(wk[:, 0:2], w_vt[:], a_s[:], start=True, stop=True).then_inc(fold, 1)
                pe.wait_ge(ready, 3)

            def work(part, i, n, kind, m, k):
                b = i * NS + m
                if n > 0:
                    wait_released(pe, i, *USES[part][n - 1])
                elif part != "pre":
                    wait_released(pe, 0, *USES["pre"][-1])
                    wait_released(pe, i - 1, *USES["body"][-1])
                half = slice(k * HALF, (k + 1) * HALF)
                if kind in ("T", "T2"):
                    src = hn if kind == "T" else stage_v
                    if kind == "T":
                        pe.wait_ge(ln_ready, b + 1)
                    else:
                        pe.wait_ge(staged, b + 1)
                    for t in range(4):
                        last = pe.transpose(wk[:, t * P:(t + 1) * P], src[:, 4 * k + t, 0:D], ident_f[:])
                elif kind == "V":
                    pe.wait_ge(h_ready, 2 * b + 2)
                    for t in range(4):
                        last = pe.matmul(wk[:, t * P:(t + 1) * P], h_t[:, (4 * k + t) * P:(4 * k + t + 1) * P], w_v[:],
                                         start=(t == 0), stop=(t == 3), skip_group_check=True)
                elif kind == "SC":
                    for t in range(T):
                        last = pe.matmul(wk[:, 2 * t:2 * t + 2], v_t[:, t * P:(t + 1) * P], w_s[:], start=(t == 0),
                                         stop=(t == T - 1), skip_group_check=True)
                elif kind == "SB":
                    if gated:
                        pe.wait_ge(t2_ready, 2 * b + 2)
                    last = pe.matmul(wk[:], w_r[:, 1], v_t[:, half], start=True, stop=True)
                elif kind == "SA":
                    last = pe.matmul(wk[:], w_r[:, 0], v_t[:, half], start=True, stop=True)
                elif kind == "CR":
                    pe.wait_ge(c_ready, b + 1)
                    for t in range(4):
                        last = pe.matmul(wk[0:1, t * P:(t + 1) * P], c_col[:, m % 2, 4 * k + t:4 * k + t + 1], ident_h[:],
                                         start=(t == 0), stop=(t == 3), skip_group_check=True)
                last.then_inc(wk_full, 1)

            def values(part, i, u):
                m, t = divmod(u, T)
                if t == 0:
                    pe.wait_ge(v_in[m % 2], (i + m // 2 + 1) * 16)
                    pe.wait_ge(acc_free, i * NS + m + 1)
                pe.wait_ge(p_done, i * S + u + 1)
                for n in range(T):
                    last = pe.matmul(acc_tile(n, 0, VW), p[:, u % PLACES, n * P:(n + 1) * P], v_sl[m % 2][:, t],
                                     start=(t == 0 and n % APB == 0), stop=(t == T - 1), skip_group_check=True)
                last.then_inc(av_done, 1)

            def scores(part, i, u):
                m, t = divmod(u, T)
                if u >= 2:
                    pe.wait_ge(z_done, i * S + u - 1)
                if t == 0:
                    pe.wait_ge(cr_ready, 2 * (i * NS + m) + 2)
                for half in (slice(0, HALF), slice(HALF, N)):
                    pe.matmul(s2[:, u % 2, half], ident_b[:], mask_t[:, t, half], start=True, stop=False)
                    last = pe.matmul(s2[:, u % 2, half], ones[:], c_row[:, m % 2, half], start=False, stop=True)
                last.then_inc(s2_full, 1)

            def body(part, i, steps):
                n = 0
                for s in steps:
                    for kind, m, k in sc.work(part, s):
                        work(part, i, n, kind, m, k)
                        n += 1
                    if has(part, s):
                        values(part, i, s)
                    if has(part, s + sc.LAG):
                        scores(part, i, s + sc.LAG)

            parts(pe, body)

        @block.scalar
        def _(act):
            act.wait_ge(ready, 3)

            def work(part, i, n, kind, m, k):
                act.wait_ge(wk_full, use_no(part, i, n) + 1)
                b = i * NS + m
                half = slice(k * HALF, (k + 1) * HALF)
                if kind == "T":
                    act.activation(h_t[:, half], wk[:], ACT.Copy if gated else ACT.Relu).then_inc(h_ready, 1)
                elif kind == "V":
                    dst = raw if gated else stage_v
                    if not gated and k == 0 and not (part == "pre" and m == 0):
                        act.wait_ge(v_in[(m - 1) % 2], (i + (m - 1) // 2 + 1) * 16)
                    act.activation(dst[:, 4 * k:4 * k + 4, 0:D], wk[:].rearrange("p (t d) -> p t d", t=4), ACT.Copy)\
                       .then_inc(v_ready, 1)
                elif kind == "T2":
                    act.activation(v_t[:, half], wk[:], ACT.Copy).then_inc(t2_ready, 1)
                elif kind == "SC":
                    if m >= 2:
                        act.wait_ge(p_done, (b - 1) * T)
                    cols = wk[:, 0:2 * T].rearrange("p (t s) -> p t s", s=2)
                    act.activation(s1_col[:, m % 2].unsqueeze(2), cols[:, :, 0:1], ACT.Copy)
                    act.activation(s2_rise[:, m % 2].unsqueeze(2), cols[:, :, 1:2], ACT.Copy, scale=1.0 - ALPHA)
                    act.activation(s2_slope[:, m % 2].unsqueeze(2), cols[:, :, 1:2], ACT.Copy, scale=ALPHA)\
                       .then_inc(sc_ready, 1)
                elif kind == "SB":
                    act.activation(s2_all[:, m % 2, half], wk[:], ACT.Copy).then_inc(sb_ready, 1)
                elif kind == "SA":
                    act.activation(s1_all[:, m % 2, half], wk[:], ACT.Copy).then_inc(sa_ready, 1)
                elif kind == "CR":
                    act.activation(c_row[:, m % 2, half], wk[0:1, :], ACT.Copy).then_inc(cr_ready, 1)

            def rises(i, u):
                m, t = divmod(u, T)
                if t == 0:
                    act.wait_ge(sa_ready, 2 * (i * NS + m) + 2)
                act.activation(r[:, u % PLACES], s1_all[:, m % 2], ACT.Relu, bias=s2_rise[:, m % 2, t:t + 1],
                               scale=1.0 - ALPHA).then_inc(r_done, 1)

            def probabilities(i, u):
                m, t = divmod(u, T)
                act.wait_ge(z_done, i * S + u + 1)
                act.activation(p[:, u % PLACES], z[:, u % PLACES], ACT.Exp, bias=s2_slope[:, m % 2, t:t + 1])\
                   .then_inc(p_done, 1)

            def elu(i, m):
                act.wait_ge(acc_free, i * NS + m + 2)
                act.activation(neg[:], hp[:], ACT.Relu, scale=-1.0).then_inc(neg_s, 1)
                act.wait_ge(neg_s, i * NS + m + 1)
                act.activation(neg[:], neg[:], ACT.Exp, scale=-1.0).then_inc(elu_ready, 1)

            def body(part, i, steps):
                n = 0
                for s in steps:
                    for kind, m, k in sc.work(part, s):
                        work(part, i, n, kind, m, k)
                        n += 1
                    if has(part, s + sc.LAG):
                        rises(i, s + sc.LAG)
                    if has(part, s + sc.LAG - 1):
                        probabilities(i, s + sc.LAG - 1)
                    if gated and has(part, s) and s % T == T - 1:
                        elu(i, s // T)

            parts(act, body)

        @block.vector
        def _(dve):
            dve.memset(ones[:], 1.0).then_inc(acc_free, 1)
            dve.wait_ge(acc_free, 1)
            dve.sem_inc(ready, 1)
            dve.memset(stage_v[:, :, D], 1.0).then_inc(ready, 1)
            if gated:
                dve.wait_ge(w_in, 16 * 6)
                dve.tensor_scalar(gate[:], gate[:], 1.0, None, ALU.add)
            else:
                dve.wait_ge(fold, 1)
                dve.tensor_copy(w_s[:], wk[:, 0:2]).then_inc(top_s, 1)
                dve.wait_ge(top_s, 1)
            dve.tensor_copy(w_r[:, 0], w_s[:, 0:1].to_broadcast([P, P]))
            dve.tensor_copy(w_r[:, 1], w_s[:, 1:2].to_broadcast([P, P])).then_inc(ready, 1)

            def norm_stats(i, m):
                b = i * NS + m
                dve.wait_ge(ln_dve, b)
                for t in range(T):
                    last = dve.bn_stats(stats[:, t], x_sb[:, b * T + t])
                last.then_inc(stat_s, 1)
                dve.wait_ge(stat_s, b + 1)
                dve.sem_inc(tick_dve, 1)
                for t in range(T):
                    last = dve.bn_aggr(mean_var[:, t], stats[:, t])
                last.then_inc(var_ready, 1)

            def norm_rows(i, m):
                b = i * NS + m
                dve.wait_ge(rstd_ready, b + 1)
                dve.wait_ge(h_ready, 2 * b)
                for t in range(T):
                    last = dve.tensor_scalar(hn[:, t], x_sb[:, b * T + t], mean_var[:, t, 0:1], rstd[:, t:t + 1],
                                             ALU.subtract, ALU.mult)
                if not gated:
                    last.then_inc(ln_dve, 1)
                    return
                last.then_inc(rec_s, 1)
                dve.wait_ge(rec_s, b + 1)
                for t in range(T):
                    last = dve.tensor_scalar(hn[:, t], hn[:, t], 0.0, gate[:, t:t + 1], ALU.max, ALU.mult)
                last.then_inc(ln_dve, 1)

            def project_stats(i, m):
                b = i * NS + m
                dve.wait_ge(v_ready, 2 * b + 2)
                for t in range(T):
                    last = dve.bn_stats(stats2[:, t], raw[:, t])
                last.then_inc(st2_s, 1)
                dve.wait_ge(st2_s, b + 1)
                dve.sem_inc(tick_dve, 1)
                for t in range(T):
                    last = dve.bn_aggr(mean_var2[:, t], stats2[:, t])
                last.then_inc(var2_ready, 1)

            def project_rows(i, m):
                b = i * NS + m
                dve.wait_ge(rstd2_ready, b + 1)
                for t in range(T):
                    last = dve.tensor_scalar(raw[:, t], raw[:, t], mean_var2[:, t, 0:1], rstd2[:, t:t + 1],
                                             ALU.subtract, ALU.mult)
                last.then_inc(n2_ready, 1)

            def neighbours(i, m, t):
                b = i * NS + m
                if t == 0:
                    dve.wait_ge(sb_ready, 2 * b + 2)
                    dve.sem_inc(tick_dve, 1)
                if t >= 2:
                    dve.wait_ge(g_done, T * b + t - 1)
                    dve.sem_inc(tick_dve, 1)
                dve.tensor_tensor_reduce(junk[:, t % 2], s2_all[:, m % 2], mask_a[:, t], 1.0, -3.0e38, ALU.add, ALU.max,
                                         g_max[:, m % 2, t:t + 1]).then_inc(g_done, 1)
                if t == T - 1:
                    dve.wait_ge(g_done, T * b + T)
                    extra = 0 if gated else 1
                    dve.wait_ge(sc_ready, b + 1)
                    dve.tensor_tensor(top[:, m % 2], g_max[:, m % 2], s1_col[:, m % 2], ALU.add).then_inc(top_s, 1)
                    dve.wait_ge(top_s, 2 * b + 1 + extra)
                    dve.scalar_tensor_tensor(out=most[:, m % 2], in0=top[:, m % 2], scalar=ALPHA, in1=top[:, m % 2],
                                             op0=ALU.mult, op1=ALU.max).then_inc(top_s, 1)
                    dve.wait_ge(top_s, 2 * b + 2 + extra)
                    dve.scalar_tensor_tensor(out=c_col[:, m % 2], in0=s1_col[:, m % 2], scalar=ALPHA, in1=most[:, m % 2],
                                             op0=ALU.mult, op1=ALU.subtract).then_inc(c_ready, 1)

            def sums(i, u):
                dve.wait_ge(s2_full, i * S + u + 1)
                dve.wait_ge(r_done, i * S + u + 1)
                dve.tensor_tensor(z[:, u % PLACES], s2[:, u % 2], r[:, u % PLACES], ALU.add).then_inc(z_done, 1)

            def output(i, m):
                b = i * NS + m
                dve.wait_ge(av_done, (b + 1) * T)
                for bank in range(ACC_BANKS):
                    n = min(APB, T - bank * APB)
                    den = acc[:, bank, 0:n * VW].rearrange("p (t c) -> p t c", t=n)[:, :, D:VW]
                    last = dve.reciprocal(rec[:, bank * APB:bank * APB + n].unsqueeze(2), den)
                last.then_inc(xa_s, 1)
                dve.wait_ge(xa_s, (b + 1) if not gated else 2 * b + 1)
                for t in range(T):
                    xs = x_sb[:, b * T + t]
                    dst, add = (hp[:, t], v_sl[m % 2][:, t, 0:D]) if gated else (xs, xs)
                    last = dve.scalar_tensor_tensor(out=dst, in0=acc_tile(t, 0, D), scalar=rec[:, t:t + 1], in1=add,
                                                    op0=ALU.mult, op1=ALU.add)
                last.then_inc(acc_free, 1)
                if gated:
                    xs = x_sb[:, bass.ds(b * T, T)]
                    dve.wait_ge(acc_free, b + 2)
                    dve.scalar_tensor_tensor(out=xs, in0=hp[:], scalar=0.0, in1=xs, op0=ALU.max, op1=ALU.add)\
                       .then_inc(xa_s, 1)
                    dve.wait_ge(elu_ready, b + 1)
                    dve.wait_ge(xa_s, 2 * b + 2)
                    dve.scalar_tensor_tensor(out=xs, in0=neg[:], scalar=-1.0, in1=xs, op0=ALU.add, op1=ALU.add)\
                       .then_inc(x_out, 1)

            def body(part, i, steps):
                for s in steps:
                    for at, act_on in ((14 if gated else 12, norm_stats), (13 if gated else 11, norm_rows)):
                        if sc.lead(part, s, at) is not None:
                            act_on(i, sc.lead(part, s, at))
                    if gated and sc.lead(part, s, 11) is not None:
                        project_stats(i, sc.lead(part, s, 11))
                    if gated and sc.lead(part, s, 10) is not None:
                        project_rows(i, sc.lead(part, s, 10))
                    for at in (6, 5, 4, 3):
                        if sc.lead(part, s, at) is not None:
                            for t in (2 * (6 - at), 2 * (6 - at) + 1):
                                neighbours(i, sc.lead(part, s, at), t)
                    if has(part, s + sc.LAG):
                        sums(i, s + sc.LAG)
                    if has(part, s) and s % T == T - 1:
                        output(i, s // T)

            parts(dve, body)

        @block.gpsimd
        def _(pool):
            pool.wait_ge(w_in, 16 * (6 if gated else 3))
            root = rsqrt_steps(pool, nc, mean_var, rvar, guess, rstd, root_s, rstd_ready, var_ready, tick_pool)
            if gated:
                root2 = rsqrt_steps(pool, nc, mean_var2, rvar2, guess2, rstd2, root2_s, rstd2_ready, var2_ready,
                                    tick_pool)

            def body(part, i, steps):
                for s in steps:
                    m = sc.lead(part, s, 14 if gated else 12)
                    if m is not None:
                        root(i * NS + m)
                    m = sc.lead(part, s, 13)
                    if gated and m is not None:
                        pool.wait_ge(ln_dve, i * NS + m + 1)
                        pool.tensor_tensor(hn[:], hn[:], shift[:].unsqueeze(2).to_broadcast([P, T, D]), ALU.add)\
                            .then_inc(ln_ready, 1)
                    m = sc.lead(part, s, 11)
                    if gated and m is not None:
                        root2(i * NS + m)
                    m = sc.lead(part, s, 10)
                    if gated and m is not None:
                        b = i * NS + m
                        pool.wait_ge(n2_ready, b + 1)
                        pool.tensor_tensor(raw[:], raw[:], gamma[:].unsqueeze(1).to_broadcast([P, T, D]), ALU.mult)\
                            .then_inc(gb_s, 1)
                        if not (part == "pre" and m == 0):
                            pool.wait_ge(v_in[(m - 1) % 2], (i + (m - 1) // 2 + 1) * 16)
                        pool.wait_ge(gb_s, b + 1)
                        pool.tensor_tensor(stage_v[:, :, 0:D], raw[:], beta[:].unsqueeze(1).to_broadcast([P, T, D]),
                                           ALU.add).then_inc(staged, 1)

            parts(pool, body)


def kernel(x, adj, L0_gnn_Ws, L0_gnn_Wt, L0_gnn_Wc, L1_gnn_Wq, L1_gnn_Wk, L1_gnn_Wv, L1_gnn_Wo, L1_gnn_bo, L2_gnn_W,
           L2_gnn_a, L2_gnn_node_weights, L2_gnn_node_bias, L2_gnn_ln_gamma, L2_gnn_ln_beta, L3_gnn_W, L3_gnn_a):
    import concourse.bacc as bacc
    from concourse.bass_utils import run_bass_kernel_spmd

    def rows(v):
        return np.broadcast_to(np.asarray(v)[None, :], (P, len(v)))

    arrays = {
        "x": x, "adj": adj, "adj_t": np.asarray(adj).T,
        "w_st": np.concatenate([L0_gnn_Ws, L0_gnn_Wt], axis=1), "w_c": L0_gnn_Wc,
        "w_q": np.asarray(L1_gnn_Wq).T, "w_k": np.asarray(L1_gnn_Wk).T, "w_v": np.asarray(L1_gnn_Wv).T,
        "w_o": np.asarray(L1_gnn_Wo).T, "b_o": rows(L1_gnn_bo),
        "w_2": L2_gnn_W, "a_2": np.asarray(L2_gnn_a).reshape(2, D).T,
        "nw": np.asarray(L2_gnn_node_weights).reshape(T, P).T, "nb": np.asarray(L2_gnn_node_bias).reshape(T, P).T,
        "gamma": rows(L2_gnn_ln_gamma), "beta": rows(L2_gnn_ln_beta),
        "w_3": L3_gnn_W, "w_3t": np.asarray(L3_gnn_W).T, "a_3": np.asarray(L3_gnn_a).reshape(2, D).T,
    }
    arrays = {k: np.ascontiguousarray(v) for k, v in arrays.items()}
    nc = bacc.Bacc("TRN2", target_bir_lowering=False, num_devices=1)
    args = {k: nc.dram_tensor(k, v.shape, mybir.dt.from_np(v.dtype), kind="ExternalInput").ap() for k, v in arrays.items()}
    out = nc.dram_tensor("out", (B, N, D), F32, kind="ExternalOutput").ap()
    build(nc, out=out, **args)
    return run_bass_kernel_spmd(nc, [arrays], core_ids=[0]).results[0]["out"]
```

```python
from contextlib import ExitStack

import numpy as np
import concourse.bass as bass
from concourse import mybir
from concourse.alu_op_type import AluOpType as ALU

ACT = mybir.ActivationFunctionType
F32, F16, BF16, I32 = mybir.dt.float32, mybir.dt.float16, mybir.dt.bfloat16, mybir.dt.int32

P = 128
B = 8
N = 1024
D = 128
T = N // P
HALF = 512
BIG = 1.0e30
EPS = 1e-5
SPLIT = 64.0
VSCALE = 256.0
SHIFT = 1024.0
PBIAS = float(12 * np.log(2.0))
ALPHA = 0.2


def build(nc, x, adj, adj_t, w_st, w_c, w_q, w_k, w_v, w_o, b_o, w_2, a_2, nw, nb, gamma, beta, gamma_c, beta_c, w_3, w_3t, a_3, out):
    with ExitStack() as ctx:
        x_sb = ctx.enter_context(nc.sbuf_tensor("x_sb", [P, B * T, D], F32))
        mask_a = ctx.enter_context(nc.sbuf_tensor("mask_a", [P, T, N], BF16))
        mask_t = ctx.enter_context(nc.sbuf_tensor("mask_t", [P, T, N], BF16))
        ident_f = ctx.enter_context(nc.sbuf_tensor("ident_f", [P, P], F32))
        ident_b = ctx.enter_context(nc.sbuf_tensor("ident_b", [P, P], BF16))
        ident_h = ctx.enter_context(nc.sbuf_tensor("ident_h", [P, P], F16))
        shared = dict(x_sb=x_sb, mask_a=mask_a, mask_t=mask_t, ident_f=ident_f, ident_b=ident_b, ident_h=ident_h)
        set_up(nc, x, adj, adj_t, **shared)
        score_layer(nc, Score("L0", heads=1, maps=2, work_banks=3, rot=0, pool=(1, 3, 5, 7)),
                    dict(qk=[w_st], v=w_c), **shared)
        score_layer(nc, Score("L1", heads=4, maps=4, work_banks=2, rot=3, pool=(1, 3, 5, 7)),
                    dict(qk=[w_q, w_k], v=w_v, o=w_o, b=b_o), **shared)
        gat_layer(nc, Gat("L2", gated=True), dict(v=w_2, s=a_2, gate=nw, shift=nb, gamma=gamma, beta=beta,
                                                    gamma_c=gamma_c, beta_c=beta_c), **shared)
        gat_layer(nc, Gat("L3", gated=False), dict(v=w_3, vt=w_3t, s=a_3), **shared)
        finish(nc, x_sb, out)


def set_up(nc, x, adj, adj_t, x_sb, mask_a, mask_t, ident_f, ident_b, ident_h):
    RING = 4
    with ExitStack() as ctx:
        ring = ctx.enter_context(nc.sbuf_tensor("adj_ring", [P, RING, N], I32))
        x_in = ctx.enter_context(nc.semaphore("x_in"))
        adj_in = [ctx.enter_context(nc.semaphore(f"adj_in{r}")) for r in range(RING)]
        masked = ctx.enter_context(nc.semaphore("masked"))
        blank = ctx.enter_context(nc.semaphore("blank"))
        block = ctx.enter_context(nc.Block())

        @block.sync
        def _(sp):
            for k in range(2 * T):
                if k >= RING:
                    sp.wait_ge(masked, k - RING + 1)
                src = (adj, adj_t)[k // T]
                nc.sync.dma_start(ring[:, k % RING], src[(k % T) * P:(k % T + 1) * P, :]).then_inc(adj_in[k % RING], 16)

        @block.scalar
        def _(act):
            for b in range(B):
                nc.scalar.dma_start(x_sb[:, b * T:(b + 1) * T], x[b].rearrange("(t p) d -> p t d", p=P)).then_inc(x_in, 16)
            act.wait_ge(x_in, 16 * B)

        @block.vector
        def _(dve):
            for k in range(2 * T):
                dve.wait_ge(adj_in[k % RING], 16 * (k // RING + 1))
                nc.vector.tensor_scalar((mask_a, mask_t)[k // T][:, k % T], ring[:, k % RING], 0.0, -BIG,
                                        ALU.is_le, ALU.mult).then_inc(masked, 1)

        @block.gpsimd
        def _(pool):
            for ident in (ident_f, ident_b, ident_h):
                nc.gpsimd.memset(ident[:], 0.0).then_inc(blank, 1)
            for k, ident in enumerate((ident_f, ident_b, ident_h)):
                pool.wait_ge(blank, k + 1)
                nc.gpsimd.affine_select(out=ident[:], in_=ident[:], compare_op=ALU.not_equal, fill=1.0,
                                        base=0, pattern=[[-1, P]], channel_multiplier=1)


class Score:

    LOW, AHEAD = 2, 3

    def __init__(self, name, heads, maps, work_banks, rot, pool):
        self.name, self.heads, self.maps, self.work_banks, self.rot, self.pool = name, heads, maps, work_banks, rot, pool
        self.batches = maps // heads
        self.iters = B // self.batches
        self.steps = T * maps
        self.dh = D // heads
        self.multi = heads > 1
        self.mrow = 96 if self.multi else 64
        self.projections = 4 if self.multi else 2
        self.vw = 2 * self.dh + 1
        self.aw = self.vw if self.multi else self.dh + 1
        self.acc_per_bank = 4 if self.multi else 3
        self.acc_banks = -(-T // self.acc_per_bank)
        self.root_lag = 2 if self.multi else 1
        self.pre = list(range(-(rot + 24) if self.multi else -(rot + 16), 0))

    def before(self, s, n):
        return divmod(s + self.rot + self.AHEAD + n, T)

    def norm_at(self, part, s, later=0):
        if self.multi:
            return 0 if part == "pre" and s == self.pre[0] + later else 1 if part == "body" and s == 1 + later else None
        m, t = self.before(s - later, 13)
        return m if t == 0 and m >= 0 and (part != "last" or m < self.maps) else None

    def work(self, part, s):
        prologue = [("T", 0), ("T", 1)] + [("QK", k) for k in range(self.projections)] + [("V", 0), ("V", 1)]
        if self.multi:
            if part == "pre" and s - self.pre[0] < 10:
                j = s - self.pre[0] - 2
                return [(kind, 0, k) for kind, k in prologue[j:j + 1]] if j >= 0 else []
            m, t = self.before(s, 11)
            got = [("S1", m, 2 * t), ("S1", m, 2 * t + 1)]
            m, t = self.before(s, 2)
            if t == 0:
                got += [("M", m, 0), ("M", m, 1)]
            got = [g for g in got if g[1] >= 0 and (part != "last" or g[1] < self.maps)]
            if part == "body" and 4 <= s < 12:
                got.append((prologue[s - 4][0], 1, prologue[s - 4][1]))
            if part != "pre":
                got += [("OT", 0, 0), ("OT", 0, 1)] if s == 30 else []
                got = ([("WO", 0, 0), ("WO", 0, 1)] if s == 31 else []) + got
            return got
        got = []
        for n, uses in ((7, [("S1", k) for k in (0, 1, 2)]), (6, [("S1", k) for k in (3, 4, 5)]),
                        (5, [("S1", k) for k in (6, 7, 8)]), (4, [("S1", k) for k in (9, 10, 11)]),
                        (3, [("S1", k) for k in (12, 13)]), (2, [("S1", k) for k in (14, 15)]),
                        (1, [("M", 0), ("M", 1)]), (11, [("T", 0)]), (10, [("T", 1)]), (9, [("QK", 0), ("QK", 1)]),
                        (8, [("V", 0), ("V", 1)])):
            m, t = self.before(s, n)
            if t == 0:
                got += [(kind, m, k) for kind, k in uses]
        return [g for g in got if g[1] >= 0 and (part != "last" or g[1] < self.maps)]

    def uses(self, part):
        steps = self.pre if part == "pre" else range(self.steps)
        return [g for s in steps for g in self.work(part, s)]


def rsqrt_steps(pool, nc, mean_var, rvar, guess, rstd, root_s, done, var_ready, tick):
    NEWTON = 3
    WAITS = 3 + 4 * NEWTON - 1

    tmp = guess[:].bitcast(F32)

    def inverse_root(b):
        k = [b * WAITS]

        def step(instruction):
            instruction.then_inc(root_s, 1)
            k[0] = k[0] + 1
            pool.wait_ge(root_s, k[0])
            pool.sem_inc(tick, 1)

        pool.wait_ge(var_ready, b + 1)
        pool.sem_inc(tick, 1)
        step(pool.tensor_scalar(rvar[:], mean_var[:, :, 1], EPS, None, ALU.add))
        step(pool.tensor_scalar(guess[:], rvar[:].bitcast(I32), -0.5, float(0x5F3759DF), ALU.mult, ALU.add))
        step(pool.tensor_copy(rstd[:].bitcast(I32), guess[:]))
        for n in range(NEWTON):
            step(pool.tensor_tensor(tmp, rstd[:], rstd[:], ALU.mult))
            step(pool.tensor_tensor(tmp, tmp, rvar[:], ALU.mult))
            step(pool.tensor_scalar(tmp, tmp, -0.5, 1.5, ALU.mult, ALU.add))
            y = pool.tensor_tensor(rstd[:], rstd[:], tmp, ALU.mult)
            if n < NEWTON - 1:
                step(y)
        y.then_inc(done, 1)

    return inverse_root


def score_layer(nc, sc, w, x_sb, mask_a, mask_t, ident_f, ident_b, ident_h):
    NS, S, L, dh, multi = sc.maps, sc.steps, sc.name, sc.dh, sc.multi
    PLACES = 4
    EXP_SCALE = 1.0 / SPLIT ** 2 / (float(np.sqrt(dh)) if multi else 1.0)
    KH = sc.projections + 2
    N_QK = len(w["qk"])
    PIECES = 1 if multi else 2
    PW = N // PIECES
    N_ST = 1 if multi else 2
    S1_ROWS = [96] if multi else [64]
    S2_ROWS = [97] if multi else [128, 65]
    USES = {part: sc.uses(part) for part in ("pre", "body", "last")}
    N_PRE, N_BODY = len(USES["pre"]), len(USES["body"])
    assert N_BODY % sc.work_banks == 0

    with ExitStack() as ctx:
        def sb(name, shape, dt):
            return ctx.enter_context(nc.sbuf_tensor(f"{L}_{name}", shape, dt))

        def ps(name, shape, dt=F32):
            return ctx.enter_context(nc.psum_tensor(f"{L}_{name}", shape, dt))

        def sem(name):
            return ctx.enter_context(nc.semaphore(f"{L}_{name}"))

        def sem_multi(name):
            return sem(name) if multi else None

        w_qk = [sb(f"w_qk{k}", [P, P], F32) for k in range(N_QK)]
        w_v = sb("w_v", [P, D], F32)
        stats = sb("stats", [P, T, 6], F32)
        mean_var = sb("mean_var", [P, T, 2], F32)
        rvar = sb("rvar", [P, T], F32)
        guess = sb("guess", [P, T], I32)
        rstd = sb("rstd", [P, T], F32)
        hn = sb("hn", [P, T, D], F32)
        h_t = sb("h_t", [P, N], F32)
        stage_hi = [sb(f"stage_hi{k}", [P, N], F16) for k in range(N_QK)]
        stage_lo = [sb(f"stage_lo{k}", [P, N], F16) for k in range(N_QK)]
        stage_v = sb("stage_v", [P, sc.heads, T, sc.vw], F16)
        st_q = [[sb(f"st_q{m}_{k}", [P, N], F16) for k in range(N_ST)] for m in range(NS)]
        st_k = [[sb(f"st_k{m}_{k}", [P, N], F16) for k in range(N_ST)] for m in range(NS)]
        v_sl = [sb(f"v{m}", [P, T, sc.vw], F16) for m in range(NS)]
        junk = sb("junk", [P, sc.work_banks, HALF], BF16)
        mx_half = sb("mx_half", [P, NS, 2, T], F32)
        mx = sb("mx", [P, NS, T], F32)
        mneg = sb("mneg", [P, NS, T], F16)
        pbias = sb("pbias", [P, 1], F32)
        p32 = sb("p32", [P, PLACES, N], F32)
        p_hi = sb("p_hi", [P, PLACES, N], F16)
        p_lo = sb("p_lo", [P, PLACES, N], F16)
        rec = sb("rec", [P, T], F32)
        if multi:
            w_o = sb("w_o", [P, D], F32)
            b_o = sb("b_o", [P, D], F32)
            lo_sum = sb("lo_sum", [P, T, dh], F32)
            num = sb("num", [P, T, dh], F32)
            o = sb("o", [P, T, D], F32)
            o_t = sb("o_t", [P, N], F32)

        s2 = ps("s2", [P, 2, PW])
        wk = ps("wk", [P, sc.work_banks, HALF])
        acc = ps("acc", [P, sc.acc_banks, HALF])

        def acc_tile(t, a, b):
            base = (t % sc.acc_per_bank) * sc.aw
            return acc[:, t // sc.acc_per_bank, base + a:base + b]

        def acc_cols(bank, a, b):
            n = min(sc.acc_per_bank, T - bank * sc.acc_per_bank)
            tiles = slice(bank * sc.acc_per_bank, bank * sc.acc_per_bank + n)
            return acc[:, bank, 0:n * sc.aw].rearrange("p (t c) -> p t c", t=n)[:, :, a:b], tiles

        w_in = sem("w_in")
        ready = sem("ready")
        tick_dve = sem("tick_dve")
        tick_pool = sem("tick_pool")
        stat_s = sem("stat_s")
        var_ready = sem("var_ready")
        root_s = sem("root_s")
        rstd_ready = sem("rstd_ready")
        ln_ready = sem("ln_ready")
        wk_full = sem("wk_full")
        hi_done = sem("hi_done")
        h_ready = sem("h_ready")
        qk_ready = sem("qk_ready")
        v_ready = sem("v_ready")
        s1_done = sem("s1_done")
        m_row = sem("m_row")
        ot_ready = sem_multi("ot_ready")
        x_done = sem_multi("x_done")
        st_in = [sem(f"st_in{m}") for m in range(NS)]
        v_in = [sem(f"v_in{m}") for m in range(NS)]
        mx_s = sem("mx_s")
        m_col = sem("m_col")
        s2_full = sem("s2_full")
        p32_done = sem("p32_done")
        phi_done = sem("phi_done")
        plo_dve = sem("plo_dve")
        plo_pool = sem("plo_pool")
        av_done = sem("av_done")
        acc_lo = sem_multi("acc_lo")
        ep_s = sem("ep_s")
        acc_free = sem("acc_free")
        o_ready = sem_multi("o_ready")
        xb_ready = sem_multi("xb_ready")

        def map_no(i, m):
            return i * NS + m

        def batch_no(i, m):
            return i * sc.batches + m // sc.heads

        def wait_released(eng, i, kind, m, k):
            if kind == "T":
                eng.wait_ge(h_ready, 2 * (i * sc.batches + m) + k + 1)
            elif kind == "QK":
                eng.wait_ge(qk_ready, sc.projections * (i * sc.batches + m) + k + 1)
            elif kind == "V":
                eng.wait_ge(v_ready, 2 * (i * sc.batches + m) + k + 1)
            elif kind == "S1":
                eng.wait_ge(s1_done, 2 * T * map_no(i, m) + k + 1)
            elif kind == "M":
                eng.wait_ge(m_row, 2 * map_no(i, m) + k + 1)
            elif kind == "OT":
                eng.wait_ge(ot_ready, 2 * i + k + 1)
            elif kind == "WO":
                eng.wait_ge(x_done, 2 * i + k + 1)

        def use_no(part, i, n):
            return n if part == "pre" else N_PRE + i * N_BODY + n

        def bank_of(part, n):
            return (n if part == "pre" else N_PRE + n) % sc.work_banks

        def pooled(t):
            return sum(a <= t for a in sc.pool)

        def wait_low(eng, i, u):
            m, t = divmod(u, T)
            if t in sc.pool:
                eng.wait_ge(plo_pool, map_no(i, m) * pooled(T - 1) + pooled(t))
            else:
                eng.wait_ge(plo_dve, map_no(i, m) * (T - pooled(T - 1)) + t + 1 - pooled(t))

        def parts(eng, body):
            body("pre", 0, sc.pre)
            with eng.Fori(0, sc.iters - 1) as i:
                body("body", i, range(S))
            body("last", sc.iters - 1, range(S))

        def has(part, u):
            return u >= 0 and (part != "last" or u < S)

        def ordered(part, s):
            got = sc.work(part, s)
            if has(part, s + sc.rot):
                got.insert(2, ("values", 0, 0))
            if has(part, s + sc.rot + sc.AHEAD):
                for piece in range(PIECES):
                    got.insert(2 * piece, ("scores", 0, piece))
            return got

        block = ctx.enter_context(nc.Block())

        @block.sync
        def _(sp):
            for dst, src in [*zip(w_qk, w["qk"]), (w_v, w["v"])] + ([(w_o, w["o"]), (b_o, w["b"])] if multi else []):
                sp.dma_start(dst[:], src).then_inc(w_in, 16)
            sp.wait_ge(ready, 1)

            def fill_stack(i, m):
                slot, h = m % NS, m % sc.heads
                sp.wait_ge(qk_ready, sc.projections * batch_no(i, m) + sc.projections)
                if multi:
                    rows = slice(h * dh, (h + 1) * dh)
                    moves = [(st_q[slot][0], stage_hi[0], rows, 0), (st_q[slot][0], stage_hi[0], rows, dh),
                             (st_q[slot][0], stage_lo[0], rows, 2 * dh), (st_k[slot][0], stage_hi[1], rows, 0),
                             (st_k[slot][0], stage_lo[1], rows, dh), (st_k[slot][0], stage_hi[1], rows, 2 * dh)]
                else:
                    q, k = slice(0, 64), slice(64, 128)
                    moves = [(st_q[slot][0], stage_hi[0], q, 0), (st_q[slot][0], stage_lo[0], q, 64),
                             (st_k[slot][0], stage_hi[0], k, 0), (st_k[slot][0], stage_hi[0], k, 64),
                             (st_q[slot][1], stage_hi[0], q, 0), (st_k[slot][1], stage_lo[0], k, 0)]
                for dst, src, rows, at in moves:
                    sp.dma_start(dst[at:at + rows.stop - rows.start, :], src[rows, :]).then_inc(st_in[slot], 16)

            def fill_values(i, m):
                sp.wait_ge(v_ready, 2 * batch_no(i, m) + 2)
                sp.dma_start(v_sl[m % NS][:], stage_v[:, m % sc.heads]).then_inc(v_in[m % NS], 16)

            def body(part, i, steps):
                for s in steps:
                    if multi and part == "pre" and s == steps[0]:
                        for m in range(NS):
                            fill_stack(i, m)
                            fill_values(i, m)
                    elif multi and part == "body" and s == 0:
                        for m in range(NS):
                            sp.wait_ge(av_done, (map_no(i, m) + 1) * T)
                            fill_stack(i, NS + m)
                            fill_values(i, NS + m)
                    elif not multi:
                        m, t = sc.before(s, 8)
                        if t == 0 and m >= 0 and (part != "last" or m < NS):
                            if m >= NS:
                                sp.wait_ge(s2_full, map_no(i, m - 1) * T)
                            fill_stack(i, m)
                        m, t = sc.before(s, 6)
                        if t == 0 and m >= 0 and (part != "last" or m < NS):
                            if m >= NS:
                                sp.wait_ge(av_done, map_no(i, m - 1) * T)
                            fill_values(i, m)

            parts(sp, body)

        @block.tensor
        def _(pe):
            pe.wait_ge(ready, 2)

            def take_bank(part, i, n):
                uses, back = USES[part], n - sc.work_banks
                if back >= 0:
                    wait_released(pe, i, *uses[back])
                elif part != "pre":
                    wait_released(pe, 0, *USES["pre"][N_PRE + back])
                    wait_released(pe, i - 1, *USES["body"][N_BODY + back])
                return wk[:, bank_of(part, n)]

            def work(part, i, n, kind, m, k):
                bank = take_bank(part, i, n)
                if kind == "T":
                    pe.wait_ge(ln_ready, T * (i * sc.batches + m) + 4 * k + 4)
                    for t in range(4):
                        last = pe.transpose(bank[:, t * P:(t + 1) * P], hn[:, 4 * k + t], ident_f[:])
                elif kind == "QK":
                    pe.wait_ge(h_ready, 2 * (i * sc.batches + m) + 2)
                    last = pe.matmul(bank, w_qk[k // 2][:], h_t[:, k % 2 * HALF:(k % 2 + 1) * HALF], start=True,
                                     stop=True)
                elif kind == "V":
                    for t in range(4):
                        last = pe.matmul(bank[:, t * P:(t + 1) * P], h_t[:, (4 * k + t) * P:(4 * k + t + 1) * P], w_v[:],
                                         start=(t == 0), stop=(t == 3), skip_group_check=True)
                elif kind == "S1":
                    slot, t, half = m % NS, k // 2, k % 2
                    if k == 0:
                        pe.wait_ge(st_in[slot], (i + m // NS + 1) * 6 * 16)
                    for j, r in enumerate(S1_ROWS):
                        last = pe.matmul(bank, st_q[slot][j][0:r, t * P:(t + 1) * P],
                                         st_k[slot][j][0:r, half * HALF:(half + 1) * HALF],
                                         start=(j == 0), stop=(j == len(S1_ROWS) - 1))
                elif kind == "M":
                    pe.wait_ge(m_col, map_no(i, m) + 1)
                    for t in range(4):
                        last = pe.matmul(bank[sc.mrow:sc.mrow + 1, t * P:(t + 1) * P],
                                         mneg[:, m % NS, 4 * k + t:4 * k + t + 1], ident_h[:], start=(t == 0),
                                         stop=(t == 3), skip_group_check=True)
                elif kind == "OT":
                    pe.wait_ge(o_ready, map_no(i, NS))
                    for t in range(4):
                        last = pe.transpose(bank[:, t * P:(t + 1) * P], o[:, 4 * k + t], ident_f[:])
                elif kind == "WO":
                    pe.wait_ge(ot_ready, 2 * i + k + 1)
                    for t in range(4):
                        last = pe.matmul(bank[:, t * P:(t + 1) * P], o_t[:, (4 * k + t) * P:(4 * k + t + 1) * P], w_o[:],
                                         start=(t == 0), stop=(t == 3), skip_group_check=True)
                last.then_inc(wk_full, 1)

            def values(part, i, u):
                m, t = divmod(u, T)
                slot = m % NS
                if t == 0:
                    pe.wait_ge(v_in[slot], (i + m // NS + 1) * 16)
                    pe.wait_ge(acc_free, map_no(i, m) + 1)
                pe.wait_ge(phi_done, (i * S + u + 1) * PIECES)
                wait_low(pe, i, u)
                v = v_sl[slot]
                for n in range(T):
                    hi = p_hi[:, u % PLACES, n * P:(n + 1) * P]
                    lo = p_lo[:, u % PLACES, n * P:(n + 1) * P]
                    first = t == 0 and n % sc.acc_per_bank == 0
                    pe.matmul(acc_tile(n, 0, sc.aw), hi, v[:, t, 0:sc.aw], start=first, stop=False,
                              skip_group_check=True)
                    if not multi:
                        pe.matmul(acc_tile(n, 0, dh), hi, v[:, t, dh + 1:], start=False, stop=False,
                                  skip_group_check=True)
                    last = pe.matmul(acc_tile(n, 0, dh + 1), lo, v[:, t, 0:dh + 1], start=False, stop=(t == T - 1),
                                     skip_group_check=True)
                last.then_inc(av_done, 1)

            def scores(part, i, u, piece):
                m, t = divmod(u, T)
                slot = m % NS
                if t == 0 and piece == 0:
                    pe.wait_ge(m_row, 2 * map_no(i, m) + 2)
                q = u * PIECES + piece
                if q >= 2:
                    pe.wait_ge(phi_done, i * S * PIECES + q - 1)
                for at in range(0, PW, HALF):
                    dst, cols = s2[:, q % 2, at:at + HALF], slice(piece * PW + at, piece * PW + at + HALF)
                    pe.matmul(dst, ident_b[:], mask_t[:, t, cols], start=True, stop=False)
                    for j, r in enumerate(S2_ROWS):
                        last = pe.matmul(dst, st_k[slot][j][0:r, t * P:(t + 1) * P], st_q[slot][j][0:r, cols],
                                         start=False, stop=(j == N_ST - 1))
                last.then_inc(s2_full, 1)

            def body(part, i, steps):
                n = 0
                for s in steps:
                    for kind, m, k in ordered(part, s):
                        if kind == "scores":
                            scores(part, i, s + sc.rot + sc.AHEAD, k)
                        elif kind == "values":
                            values(part, i, s + sc.rot)
                        else:
                            work(part, i, n, kind, m, k)
                            n += 1

            parts(pe, body)

        @block.scalar
        def _(act):
            act.wait_ge(ready, 1)

            def work(part, i, n, kind, m, k):
                bank = wk[:, bank_of(part, n)]
                act.wait_ge(wk_full, use_no(part, i, n) + 1)
                b = i * sc.batches + m
                if kind == "T":
                    act.activation(h_t[:, k * HALF:(k + 1) * HALF], bank, ACT.Relu).then_inc(h_ready, 1)
                elif kind == "OT":
                    act.activation(o_t[:, k * HALF:(k + 1) * HALF], bank, ACT.Copy).then_inc(ot_ready, 1)
                elif kind == "QK":
                    if k == 0 and not (part == "pre" and m == 0):
                        for slot in (range(NS) if multi else [(m - 1) % NS]):
                            act.wait_ge(st_in[slot], (i + 1 if multi else i + (m - 1) // NS + 1) * 6 * 16)
                    act.activation(stage_hi[k // 2][:, k % 2 * HALF:(k % 2 + 1) * HALF], bank, ACT.Copy)\
                       .then_inc(hi_done, 1)
                elif kind == "V":
                    if k == 0 and not (part == "pre" and m == 0):
                        for slot in (range(NS) if multi else [(m - 1) % NS]):
                            act.wait_ge(v_in[slot], (i + 1 if multi else i + (m - 1) // NS + 1) * 16)
                    act.activation(stage_v[:, :, 4 * k:4 * k + 4, 0:dh].rearrange("p h t d -> p t h d"),
                                   bank.rearrange("p (t h d) -> p t h d", t=4, h=sc.heads), ACT.Copy)\
                       .then_inc(hi_done, 1)

            def probabilities(part, i, u, piece):
                q, cols = u * PIECES + piece, slice(piece * PW, (piece + 1) * PW)
                act.wait_ge(s2_full, i * S * PIECES + q + 1)
                if u >= PLACES and piece == 0:
                    wait_low(act, i, u - PLACES)
                act.activation(p32[:, u % PLACES, cols], s2[:, q % 2], ACT.Exp, bias=pbias[:], scale=EXP_SCALE)\
                   .then_inc(p32_done, 1)
                act.activation(p_hi[:, u % PLACES, cols], s2[:, q % 2], ACT.Exp, bias=pbias[:], scale=EXP_SCALE)\
                   .then_inc(phi_done, 1)

            def low_columns(i, m):
                act.wait_ge(av_done, (map_no(i, m) + 1) * T)
                act.wait_ge(acc_free, map_no(i, m) + 1)
                for bank in range(sc.acc_banks):
                    src, tiles = acc_cols(bank, dh + 1, sc.aw)
                    act.activation(lo_sum[:, tiles], src, ACT.Copy).then_inc(acc_lo, 1)

            def body(part, i, steps):
                n = 0
                for s in steps:
                    for kind, m, k in ordered(part, s):
                        if kind == "scores":
                            probabilities(part, i, s + sc.rot + sc.AHEAD, k)
                        elif kind != "values":
                            if kind in ("T", "QK", "V", "OT"):
                                work(part, i, n, kind, m, k)
                            n += 1
                    u = s + sc.rot
                    if multi and has(part, u) and u % T == T - 1:
                        low_columns(i, u // T)

            parts(act, body)

        @block.vector
        def _(dve):
            dve.memset(pbias[:], PBIAS).then_inc(acc_free, 1)
            for m in range(NS):
                dve.memset(st_k[m][-1][sc.mrow:sc.mrow + 1, :], SHIFT)
            dve.memset(stage_v[:, :, :, dh], VSCALE).then_inc(ready, 1)
            dve.wait_ge(w_in, 16 * (N_QK + 1 + 2 * multi))
            for t in w_qk:
                dve.tensor_scalar(t[:], t[:], SPLIT, None, ALU.mult)
            dve.tensor_scalar(w_v[:], w_v[:], VSCALE, None, ALU.mult).then_inc(ready, 1)

            def norm_stats(i, m):
                b = i * sc.batches + m
                dve.wait_ge(ln_ready, T * b)
                for t in range(T):
                    last = dve.bn_stats(stats[:, t], x_sb[:, b * T + t])
                last.then_inc(stat_s, 1)
                dve.wait_ge(stat_s, b + 1)
                dve.sem_inc(tick_dve, 1)
                for t in range(T):
                    last = dve.bn_aggr(mean_var[:, t], stats[:, t])
                last.then_inc(var_ready, 1)

            def norm_rows(i, m):
                b = i * sc.batches + m
                dve.wait_ge(rstd_ready, b + 1)
                dve.wait_ge(h_ready, 2 * b)
                for t in range(T):
                    dve.tensor_scalar(hn[:, t], x_sb[:, b * T + t], mean_var[:, t, 0:1], rstd[:, t:t + 1],
                                      ALU.subtract, ALU.mult).then_inc(ln_ready, 1)

            def work(part, i, n, kind, m, k):
                bank = wk[:, bank_of(part, n)]
                half = slice(k % 2 * HALF, (k % 2 + 1) * HALF)
                if kind == "QK":
                    dve.wait_ge(hi_done, (i * sc.batches + m) * KH + k + 1)
                    dve.tensor_tensor(stage_lo[k // 2][:, half], bank, stage_hi[k // 2][:, half], ALU.subtract)\
                       .then_inc(qk_ready, 1)
                elif kind == "V":
                    dve.wait_ge(hi_done, (i * sc.batches + m) * KH + sc.projections + k + 1)
                    tiles = slice(4 * k, 4 * k + 4)
                    dve.tensor_tensor(stage_v[:, :, tiles, dh + 1:].rearrange("p h t d -> p t h d"),
                                      bank.rearrange("p (t h d) -> p t h d", t=4, h=sc.heads),
                                      stage_v[:, :, tiles, 0:dh].rearrange("p h t d -> p t h d"),
                                      ALU.subtract).then_inc(v_ready, 1)
                elif kind == "S1":
                    g = m % NS
                    dve.wait_ge(wk_full, use_no(part, i, n) + 1)
                    dve.sem_inc(tick_dve, 1)
                    dve.tensor_tensor_reduce(junk[:, bank_of(part, n)], bank, mask_a[:, k // 2, half], 1.0, -3.0e38, ALU.add, ALU.max,
                                             mx_half[:, g, k % 2, k // 2:k // 2 + 1]).then_inc(s1_done, 1)
                    if k == 2 * T - 1:
                        dve.wait_ge(s1_done, 2 * T * (map_no(i, m) + 1))
                        dve.tensor_tensor(mx[:, g], mx_half[:, g, 0], mx_half[:, g, 1], ALU.max).then_inc(mx_s, 1)
                        dve.wait_ge(mx_s, map_no(i, m) + 1)
                        dve.tensor_scalar(mneg[:, g], mx[:, g], -1.0 / SHIFT, None, ALU.mult).then_inc(m_col, 1)
                elif kind == "M":
                    dve.wait_ge(wk_full, use_no(part, i, n) + 1)
                    dve.tensor_copy(st_q[m % NS][-1][sc.mrow:sc.mrow + 1, half], bank[sc.mrow:sc.mrow + 1, :])\
                       .then_inc(m_row, 1)
                elif kind == "WO":
                    dve.wait_ge(wk_full, use_no(part, i, n) + 1)
                    dve.wait_ge(xb_ready, i + 1)
                    xs = x_sb[:, bass.ds(i * T + 4 * k, 4)]
                    dve.tensor_tensor(xs, xs, bank.rearrange("p (t d) -> p t d", t=4), ALU.add).then_inc(x_done, 1)

            def low_parts(i, u):
                dve.wait_ge(phi_done, (i * S + u + 1) * PIECES)
                dve.tensor_tensor(p_lo[:, u % PLACES], p32[:, u % PLACES], p_hi[:, u % PLACES], ALU.subtract)\
                   .then_inc(plo_dve, 1)

            def head_output(i, m):
                g, h = map_no(i, m), m % sc.heads
                for bank in range(sc.acc_banks):
                    dve.wait_ge(acc_lo, g * sc.acc_banks + bank + 1)
                    hi, tiles = acc_cols(bank, 0, dh)
                    dve.tensor_tensor(num[:, tiles], hi, lo_sum[:, tiles], ALU.add)
                    den, tiles = acc_cols(bank, dh, dh + 1)
                    last = dve.reciprocal(rec[:, tiles].unsqueeze(2), den)
                last.then_inc(acc_free, 1)
                dve.wait_ge(acc_free, g + 2)
                dve.tensor_tensor(o[:, :, h * dh:(h + 1) * dh], num[:], rec[:].unsqueeze(2).to_broadcast([P, T, dh]),
                                  ALU.mult).then_inc(o_ready, 1)

            def batch_output(i, m):
                g = map_no(i, m)
                dve.wait_ge(av_done, (g + 1) * T)
                for bank in range(sc.acc_banks):
                    den, tiles = acc_cols(bank, dh, dh + 1)
                    last = dve.reciprocal(rec[:, tiles].unsqueeze(2), den)
                last.then_inc(ep_s, 1)
                dve.wait_ge(ep_s, g + 1)
                for t in range(T):
                    xs = x_sb[:, g * T + t]
                    last = dve.scalar_tensor_tensor(out=xs, in0=acc_tile(t, 0, dh), scalar=rec[:, t:t + 1], in1=xs,
                                                    op0=ALU.mult, op1=ALU.add)
                last.then_inc(acc_free, 1)

            def body(part, i, steps):
                n = 0
                for s in steps:
                    u = s + sc.rot
                    uses = sc.work(part, s)
                    for kind, m, k in uses[:2]:
                        work(part, i, n, kind, m, k)
                        n += 1
                    if has(part, u + sc.LOW) and (u + sc.LOW) % T not in sc.pool:
                        low_parts(i, u + sc.LOW)
                    for kind, m, k in uses[2:]:
                        work(part, i, n, kind, m, k)
                        n += 1
                    if sc.norm_at(part, s) is not None:
                        norm_stats(i, sc.norm_at(part, s))
                    if sc.norm_at(part, s, sc.root_lag) is not None:
                        norm_rows(i, sc.norm_at(part, s, sc.root_lag))
                    if has(part, u) and u % T == T - 1:
                        (head_output if multi else batch_output)(i, u // T)

            parts(dve, body)

        @block.gpsimd
        def _(pool):
            if multi:
                pool.wait_ge(w_in, 16 * (N_QK + 3))

            def low_parts(i, u):
                pool.wait_ge(phi_done, (i * S + u + 1) * PIECES)
                pool.tensor_tensor(p_lo[:, u % PLACES], p32[:, u % PLACES], p_hi[:, u % PLACES], ALU.subtract)\
                    .then_inc(plo_pool, 1)

            inverse_root = rsqrt_steps(pool, nc, mean_var, rvar, guess, rstd, root_s, rstd_ready, var_ready, tick_pool)

            def add_bias(b):
                pool.wait_ge(ln_ready, T * (b + 1))
                xs = x_sb[:, bass.ds(b * T, T)]
                pool.tensor_tensor(xs, xs, b_o[:].unsqueeze(1).to_broadcast([P, T, D]), ALU.add).then_inc(xb_ready, 1)

            def body(part, i, steps):
                for s in steps:
                    if sc.norm_at(part, s) is not None:
                        inverse_root(i * sc.batches + sc.norm_at(part, s))
                    if multi and sc.norm_at(part, s, sc.root_lag + 1) is not None:
                        add_bias(i + sc.norm_at(part, s, sc.root_lag + 1))
                    u = s + sc.rot + sc.LOW
                    if has(part, u) and u % T in sc.pool:
                        low_parts(i, u)

            parts(pool, body)


def finish(nc, x_sb, out):
    with nc.semaphore("stored") as stored, nc.Block() as block:
        @block.sync
        def _(sp):
            for b in range(B):
                sp.dma_start(out[b].rearrange("(t p) d -> p t d", p=P), x_sb[:, b * T:(b + 1) * T]).then_inc(stored, 16)
            sp.wait_ge(stored, 16 * B)


class Gat:
    maps, steps, iters, LAG = 2, 2 * T, B // 2, 3

    def __init__(self, name, gated):
        self.name, self.gated = name, gated
        self.pre = list(range(-16, 0))
        self.stats, self.rows = 13, 11
        self.order = {-10: [("T", 0), ("T", 1)], -9: [("V", 0), ("V", 1)], -1: [("CR", 0), ("CR", 1)]}
        if gated:
            self.order |= {-6: [("T2", 0), ("T2", 1)], -5: [("SB", 0), ("SB", 1)],
                           -4: [("SC", 0), ("SA", 0), ("SA", 1)]}
            self.neighbours = {4: (0, 1, 2), 3: (3, 4), 2: (5, 6, 7)}
        else:
            self.order |= {-7: [("SB", 0), ("SB", 1)], -6: [("SC", 0), ("SA", 0), ("SA", 1)]}
            self.neighbours = {5: (0, 1), 4: (2, 3), 3: (4, 5), 2: (6, 7)}

    def lead(self, part, s, n):
        m, t = divmod(s + self.LAG + n, T)
        return m if t == 0 and m >= 0 and (part != "last" or m < self.maps) else None

    def work(self, part, s):
        return [(kind, self.lead(part, s, -at), k) for at in sorted(self.order, reverse=True)
                if self.lead(part, s, -at) is not None for kind, k in self.order[at]]

    def uses(self, part):
        steps = self.pre if part == "pre" else range(self.steps)
        return [g for s in steps for g in self.work(part, s)]


def gat_layer(nc, sc, w, x_sb, mask_a, mask_t, ident_f, ident_b, ident_h):
    S, L, gated, NS = sc.steps, sc.name, sc.gated, sc.maps
    PLACES = 4
    USES = {part: sc.uses(part) for part in ("pre", "body", "last")}
    N_PRE, N_BODY = len(USES["pre"]), len(USES["body"])
    VW = D + 1
    APB = 3
    ACC_BANKS = -(-T // APB)
    WK_BANKS = 2
    assert N_BODY % WK_BANKS == 0

    with ExitStack() as ctx:
        def sb(name, shape, dt):
            return ctx.enter_context(nc.sbuf_tensor(f"{L}_{name}", shape, dt))

        def ps(name, shape, dt=F32):
            return ctx.enter_context(nc.psum_tensor(f"{L}_{name}", shape, dt))

        def sem(name):
            return ctx.enter_context(nc.semaphore(f"{L}_{name}"))

        def sem_gated(name):
            return sem(name) if gated else None

        w_v = sb("w_v", [P, D], F32)
        w_s = sb("w_s", [P, 2], F32)
        w_r = sb("w_r", [P, 2, P], F32)
        stats = sb("stats", [P, T, 6], F32)
        mean_var = sb("mean_var", [P, T, 2], F32)
        rvar = sb("rvar", [P, T], F32)
        guess = sb("guess", [P, T], I32)
        rstd = sb("rstd", [P, T], F32)
        hn = sb("hn", [P, T, D], F32)
        h_t = sb("h_t", [P, N], F32)
        stage_v = sb("stage_v", [P, T, VW], F32)
        v_sl = [sb(f"v{m}", [P, T, VW], F32) for m in range(2)]
        s1_col = sb("s1_col", [P, 2, T], F32)
        s2_rise = sb("s2_rise", [P, 2, T], F32)
        s2_slope = sb("s2_slope", [P, 2, T], F32)
        s2_all = sb("s2_all", [P, 2, N], F32)
        s1_all = sb("s1_all", [P, 2, N], F32)
        c_row = sb("c_row", [1, 2, N], F16)
        ones = sb("ones", [1, P], F16)
        junk = sb("junk", [P, 2, N], BF16)
        g_max = sb("g_max", [P, 2, T], F32)
        top = sb("top", [P, 2, T], F32)
        most = sb("most", [P, 2, T], F32)
        c_col = sb("c_col", [P, 2, T], F16)
        r = sb("r", [P, PLACES, N], F32)
        z = sb("z", [P, PLACES, N], F32)
        p = sb("p", [P, PLACES, N], F32)
        rec = sb("rec", [P, T], F32)
        if gated:
            gate, shift = sb("gate", [P, T], F32), sb("shift", [P, T], F32)
            col_sum = sb("col_sum", [P, D], F32)
            shifted = sb("shifted", [P, T, D], F32)
            gamma_c, beta_c = sb("gamma_c", [P, 1], F32), sb("beta_c", [P, 1], F32)
            all_ones = sb("all_ones", [P, P], F32)
            gamma, beta = sb("gamma", [P, D], F32), sb("beta", [P, D], F32)
            raw = sb("raw", [P, T, D], F32)
            v_t = sb("v_t", [P, N], F32)
            stats2 = sb("stats2", [P, T, 6], F32)
            mean_var2 = sb("mean_var2", [P, T, 2], F32)
            rvar2 = sb("rvar2", [P, T], F32)
            guess2 = sb("guess2", [P, T], I32)
            rstd2 = sb("rstd2", [P, T], F32)
            scaled = sb("scaled", [P, T, D], F32)
            hp = sb("hp", [P, T, D], F32)
            neg = sb("neg", [P, T, D], F32)
        else:
            w_vt, a_s = sb("w_vt", [P, D], F32), sb("a_s", [P, 2], F32)
            v_t = h_t

        s2 = ps("s2", [P, 2, HALF])
        wk_banks = ps("wk", [P, WK_BANKS, HALF])
        acc = ps("acc", [P, ACC_BANKS, HALF])

        def acc_tile(t, a, b):
            return acc[:, t // APB, t % APB * VW + a:t % APB * VW + b]

        w_in = sem("w_in")
        ready = sem("ready")
        fold = sem("fold")
        tick_dve, tick_pool, tick_sp = sem("tick_dve"), sem("tick_pool"), sem("tick_sp")
        stat_s = sem("stat_s")
        var_ready = sem("var_ready")
        root_s = sem("root_s")
        rstd_ready = sem("rstd_ready")
        ln_ready = sem("ln_ready")
        wk_full = sem("wk_full")
        h_ready = sem("h_ready")
        v_ready = sem("v_ready")
        st2_s = sem_gated("st2_s")
        var2_ready = sem_gated("var2_ready")
        root2_s = sem_gated("root2_s")
        rstd2_ready = sem_gated("rstd2_ready")
        n2_ready = sem_gated("n2_ready")
        gb_s = sem_gated("gb_s")
        staged = sem("staged") if gated else v_ready
        per_stage = 1 if gated else 2
        t2_ready = sem_gated("t2_ready")
        sc_ready = sem("sc_ready")
        sb_ready = sem("sb_ready")
        sa_ready = sem("sa_ready")
        cr_ready = sem("cr_ready")
        v_in = [sem(f"v_in{m}") for m in range(2)]
        g_done = sem("g_done")
        top_s = sem("top_s")
        c_ready = sem("c_ready")
        s2_full = sem("s2_full")
        r_done = sem("r_done")
        z_done = sem("z_done")
        p_done = sem("p_done")
        av_done = sem("av_done")
        rec_s = sem_gated("rec_s")
        x_out = sem_gated("x_out")
        acc_free = sem("acc_free")
        neg_s = sem_gated("neg_s")
        elu_ready = sem_gated("elu_ready")
        xa_s = sem("xa_s")

        def wait_released(eng, i, kind, m, k):
            b = i * NS + m
            if kind == "T":
                eng.wait_ge(h_ready, 2 * b + k + 1)
            elif kind == "V":
                eng.wait_ge(v_ready, 2 * b + k + 1)
            elif kind == "T2":
                eng.wait_ge(t2_ready, 2 * b + k + 1)
            elif kind == "SC":
                eng.wait_ge(sc_ready, b + 1)
            elif kind == "SB":
                eng.wait_ge(sb_ready, 2 * b + k + 1)
            elif kind == "SA":
                eng.wait_ge(sa_ready, 2 * b + k + 1)
            elif kind == "CR":
                eng.wait_ge(cr_ready, 2 * b + k + 1)

        def bank_of(part, n):
            return wk_banks[:, (n if part == "pre" else N_PRE + n) % WK_BANKS]

        def use_no(part, i, n):
            return n if part == "pre" else N_PRE + i * N_BODY + n

        def parts(eng, body):
            body("pre", 0, sc.pre)
            with eng.Fori(0, sc.iters - 1) as i:
                body("body", i, range(S))
            body("last", sc.iters - 1, range(S))

        def has(part, u):
            return u >= 0 and (part != "last" or u < S)

        def ordered(part, s):
            got = sc.work(part, s)
            got.insert(0, ("scores", 0, 0))
            got.insert(2, ("scores", 0, 1))
            got.insert(4, ("values", 0, 0))
            return [g for g in got if g[0] != "scores" or has(part, s + sc.LAG) if g[0] != "values" or has(part, s)]

        block = ctx.enter_context(nc.Block())

        @block.sync
        def _(sp):
            loads = [(w_v, w["v"])]
            loads += [(w_s, w["s"]), (gate, w["gate"]), (shift, w["shift"]), (gamma, w["gamma"]), (beta, w["beta"]),
                      (gamma_c, w["gamma_c"]), (beta_c, w["beta_c"])] \
                if gated else [(w_vt, w["vt"]), (a_s, w["s"])]
            for dst, src in loads:
                sp.dma_start(dst[:], src).then_inc(w_in, 16)
            sp.wait_ge(ready, 2)

            def body(part, i, steps):
                for s in steps:
                    m = sc.lead(part, s, 6)
                    if m is not None:
                        sp.wait_ge(staged, per_stage * (i * NS + m + 1))
                        sp.sem_inc(tick_sp, 1)
                        if part != "pre":
                            sp.wait_ge(acc_free, i * NS + m)
                        sp.dma_start(v_sl[m % 2][:], stage_v[:]).then_inc(v_in[m % 2], 16)

            parts(sp, body)

        @block.tensor
        def _(pe):
            if gated:
                pe.wait_ge(w_in, 16 * 8)
                pe.wait_ge(top_s, 1)
                pe.matmul(wk_banks[:, 0, 0:D], all_ones[:], w_v[:], start=True, stop=True).then_inc(fold, 1)
                pe.wait_ge(ready, 3)
            else:
                pe.wait_ge(w_in, 16 * 3)
                pe.matmul(wk_banks[:, 0, 0:2], w_vt[:], a_s[:], start=True, stop=True).then_inc(fold, 1)
                pe.wait_ge(ready, 3)

            def work(part, i, n, kind, m, k):
                b = i * NS + m
                wk, back = bank_of(part, n), n - WK_BANKS
                if back >= 0:
                    wait_released(pe, i, *USES[part][back])
                elif part != "pre":
                    wait_released(pe, 0, *USES["pre"][N_PRE + back])
                    wait_released(pe, i - 1, *USES["body"][N_BODY + back])
                half = slice(k * HALF, (k + 1) * HALF)
                if kind in ("T", "T2"):
                    src = hn if kind == "T" else raw
                    if kind == "T":
                        pe.wait_ge(ln_ready, b + 1)
                    else:
                        pe.wait_ge(n2_ready, b + 1)
                    for t in range(4):
                        last = pe.transpose(wk[:, t * P:(t + 1) * P], src[:, 4 * k + t], ident_f[:])
                elif kind == "V":
                    pe.wait_ge(h_ready, 2 * b + 2)
                    for t in range(4):
                        last = pe.matmul(wk[:, t * P:(t + 1) * P], h_t[:, (4 * k + t) * P:(4 * k + t + 1) * P], w_v[:],
                                         start=(t == 0), stop=(t == 3), skip_group_check=True)
                elif kind == "SC":
                    for t in range(T):
                        last = pe.matmul(wk[:, 2 * t:2 * t + 2], v_t[:, t * P:(t + 1) * P], w_s[:], start=(t == 0),
                                         stop=(t == T - 1), skip_group_check=True)
                elif kind == "SB":
                    if gated:
                        pe.wait_ge(t2_ready, 2 * b + 2)
                    last = pe.matmul(wk, w_r[:, 1], v_t[:, half], start=True, stop=True)
                elif kind == "SA":
                    last = pe.matmul(wk, w_r[:, 0], v_t[:, half], start=True, stop=True)
                elif kind == "CR":
                    pe.wait_ge(c_ready, b + 1)
                    for t in range(4):
                        last = pe.matmul(wk[0:1, t * P:(t + 1) * P], c_col[:, m % 2, 4 * k + t:4 * k + t + 1], ident_h[:],
                                         start=(t == 0), stop=(t == 3), skip_group_check=True)
                last.then_inc(wk_full, 1)

            def values(part, i, u):
                m, t = divmod(u, T)
                if t == 0:
                    pe.wait_ge(v_in[m % 2], (i + m // 2 + 1) * 16)
                    pe.wait_ge(acc_free, i * NS + m + 1)
                pe.wait_ge(p_done, i * S + u + 1)
                for n in range(T):
                    last = pe.matmul(acc_tile(n, 0, VW), p[:, u % PLACES, n * P:(n + 1) * P], v_sl[m % 2][:, t],
                                     start=(t == 0 and n % APB == 0), stop=(t == T - 1), skip_group_check=True)
                last.then_inc(av_done, 1)

            def scores(part, i, u, k):
                m, t = divmod(u, T)
                if t == 0 and k == 0:
                    pe.wait_ge(cr_ready, 2 * (i * NS + m) + 2)
                if u >= 1:
                    pe.wait_ge(z_done, 2 * (i * S + u - 1) + k + 1)
                half = slice(k * HALF, (k + 1) * HALF)
                pe.matmul(s2[:, k], ident_b[:], mask_t[:, t, half], start=True, stop=False)
                pe.matmul(s2[:, k], ones[:], c_row[:, m % 2, half], start=False, stop=True).then_inc(s2_full, 1)

            def body(part, i, steps):
                n = 0
                for s in steps:
                    for kind, m, k in ordered(part, s):
                        if kind == "scores":
                            scores(part, i, s + sc.LAG, k)
                        elif kind == "values":
                            values(part, i, s)
                        else:
                            work(part, i, n, kind, m, k)
                            n += 1

            parts(pe, body)

        @block.scalar
        def _(act):
            act.wait_ge(ready, 3)

            def work(part, i, n, kind, m, k):
                if kind == "V" and gated:
                    return
                act.wait_ge(wk_full, use_no(part, i, n) + 1)
                wk = bank_of(part, n)
                b = i * NS + m
                half = slice(k * HALF, (k + 1) * HALF)
                if kind == "T":
                    act.activation(h_t[:, half], wk, ACT.Relu).then_inc(h_ready, 1)
                elif kind == "V":
                    if k == 0 and not (part == "pre" and m == 0):
                        act.wait_ge(v_in[(m - 1) % 2], (i + (m - 1) // 2 + 1) * 16)
                    act.activation(stage_v[:, 4 * k:4 * k + 4, 0:D], wk.rearrange("p (t d) -> p t d", t=4), ACT.Copy)\
                       .then_inc(v_ready, 1)
                elif kind == "T2":
                    act.activation(v_t[:, half], wk, ACT.Identity, bias=beta_c[:], scale=gamma_c[:]).then_inc(t2_ready, 1)
                elif kind == "SC":
                    if m >= 2:
                        act.wait_ge(p_done, (b - 1) * T)
                    cols = wk[:, 0:2 * T].rearrange("p (t s) -> p t s", s=2)
                    act.activation(s1_col[:, m % 2].unsqueeze(2), cols[:, :, 0:1], ACT.Copy)
                    act.activation(s2_rise[:, m % 2].unsqueeze(2), cols[:, :, 1:2], ACT.Copy, scale=1.0 - ALPHA)
                    act.activation(s2_slope[:, m % 2].unsqueeze(2), cols[:, :, 1:2], ACT.Copy, scale=ALPHA)\
                       .then_inc(sc_ready, 1)
                elif kind == "SB":
                    act.activation(s2_all[:, m % 2, half], wk, ACT.Copy).then_inc(sb_ready, 1)
                elif kind == "SA":
                    act.activation(s1_all[:, m % 2, half], wk, ACT.Copy).then_inc(sa_ready, 1)
                elif kind == "CR":
                    act.activation(c_row[:, m % 2, half], wk[0:1, :], ACT.Copy).then_inc(cr_ready, 1)

            def rises(i, u):
                m, t = divmod(u, T)
                if t == 0:
                    act.wait_ge(sa_ready, 2 * (i * NS + m) + 2)
                act.activation(r[:, u % PLACES], s1_all[:, m % 2], ACT.Relu, bias=s2_rise[:, m % 2, t:t + 1],
                               scale=1.0 - ALPHA).then_inc(r_done, 1)

            def probabilities(i, u):
                m, t = divmod(u, T)
                act.wait_ge(z_done, 2 * (i * S + u) + 2)
                act.activation(p[:, u % PLACES], z[:, u % PLACES], ACT.Exp, bias=s2_slope[:, m % 2, t:t + 1])\
                   .then_inc(p_done, 1)

            def elu(i, m):
                act.wait_ge(acc_free, i * NS + m + 2)
                act.activation(neg[:], hp[:], ACT.Relu, scale=-1.0).then_inc(neg_s, 1)
                act.wait_ge(neg_s, i * NS + m + 1)
                act.activation(neg[:], neg[:], ACT.Exp, scale=-1.0).then_inc(elu_ready, 1)

            def body(part, i, steps):
                n = 0
                for s in steps:
                    for kind, m, k in sc.work(part, s)[:1]:
                        work(part, i, n, kind, m, k)
                        n += 1
                    if has(part, s + sc.LAG):
                        rises(i, s + sc.LAG)
                    for kind, m, k in sc.work(part, s)[1:2]:
                        work(part, i, n, kind, m, k)
                        n += 1
                    if has(part, s + 2):
                        probabilities(i, s + 2)
                    for kind, m, k in sc.work(part, s)[2:]:
                        work(part, i, n, kind, m, k)
                        n += 1
                    if gated and has(part, s) and s % T == T - 1:
                        elu(i, s // T)

            parts(act, body)

        @block.vector
        def _(dve):
            dve.memset(ones[:], 1.0).then_inc(acc_free, 1)
            dve.wait_ge(acc_free, 1)
            dve.sem_inc(ready, 1)
            dve.memset(stage_v[:, :, D], 1.0).then_inc(ready, 1)
            if gated:
                dve.wait_ge(w_in, 16 * 8)
                dve.tensor_scalar(gate[:], gate[:], 1.0, None, ALU.add)
                dve.memset(all_ones[:], 1.0).then_inc(top_s, 1)
                dve.wait_ge(fold, 1)
                dve.tensor_copy(col_sum[:], wk_banks[:, 0, 0:D]).then_inc(top_s, 1)
                dve.wait_ge(top_s, 2)
                for t in range(T):
                    dve.tensor_scalar(shifted[:, t], col_sum[:], shift[:, t:t + 1], None, ALU.mult)
            else:
                dve.wait_ge(fold, 1)
                dve.tensor_copy(w_s[:], wk_banks[:, 0, 0:2]).then_inc(top_s, 1)
                dve.wait_ge(top_s, 1)
            dve.tensor_copy(w_r[:, 0], w_s[:, 0:1].to_broadcast([P, P]))
            dve.tensor_copy(w_r[:, 1], w_s[:, 1:2].to_broadcast([P, P])).then_inc(ready, 1)

            def norm_stats(i, m):
                b = i * NS + m
                dve.wait_ge(ln_ready, b)
                for t in range(T):
                    last = dve.bn_stats(stats[:, t], x_sb[:, b * T + t])
                last.then_inc(stat_s, 1)
                dve.wait_ge(stat_s, b + 1)
                dve.sem_inc(tick_dve, 1)
                for t in range(T):
                    last = dve.bn_aggr(mean_var[:, t], stats[:, t])
                last.then_inc(var_ready, 1)

            def norm_rows(i, m):
                b = i * NS + m
                dve.wait_ge(rstd_ready, b + 1)
                dve.wait_ge(h_ready, 2 * b)
                for t in range(T):
                    last = dve.tensor_scalar(hn[:, t], x_sb[:, b * T + t], mean_var[:, t, 0:1], rstd[:, t:t + 1],
                                             ALU.subtract, ALU.mult)
                last.then_inc(ln_ready, 1)

            def project(part, i, n, m, k):
                dve.wait_ge(wk_full, use_no(part, i, n) + 1)
                wk = bank_of(part, n)
                if k == 0:
                    dve.wait_ge(staged, i * NS + m)
                for t in range(4):
                    last = dve.scalar_tensor_tensor(out=raw[:, 4 * k + t], in0=wk[:, t * P:(t + 1) * P],
                                                    scalar=gate[:, 4 * k + t:4 * k + t + 1], in1=shifted[:, 4 * k + t],
                                                    op0=ALU.mult, op1=ALU.add)
                last.then_inc(v_ready, 1)

            def project_stats(i, m):
                b = i * NS + m
                dve.wait_ge(v_ready, 2 * b + 2)
                for t in range(T):
                    last = dve.bn_stats(stats2[:, t], raw[:, t])
                last.then_inc(st2_s, 1)
                dve.wait_ge(st2_s, b + 1)
                dve.sem_inc(tick_dve, 1)
                for t in range(T):
                    last = dve.bn_aggr(mean_var2[:, t], stats2[:, t])
                last.then_inc(var2_ready, 1)

            def project_rows(i, m):
                b = i * NS + m
                dve.wait_ge(rstd2_ready, b + 1)
                for t in range(T):
                    last = dve.tensor_scalar(raw[:, t], raw[:, t], mean_var2[:, t, 0:1], rstd2[:, t:t + 1],
                                             ALU.subtract, ALU.mult)
                last.then_inc(n2_ready, 1)

            def neighbours(i, m, t):
                b = i * NS + m
                if t == 0:
                    dve.wait_ge(sb_ready, 2 * b + 2)
                    dve.sem_inc(tick_dve, 1)
                if t >= 2:
                    dve.wait_ge(g_done, T * b + t - 1)
                    dve.sem_inc(tick_dve, 1)
                dve.tensor_tensor_reduce(junk[:, t % 2], s2_all[:, m % 2], mask_a[:, t], 1.0, -3.0e38, ALU.add, ALU.max,
                                         g_max[:, m % 2, t:t + 1]).then_inc(g_done, 1)
                if t == T - 1:
                    dve.wait_ge(g_done, T * b + T)
                    extra = 2 if gated else 1
                    dve.wait_ge(sc_ready, b + 1)
                    dve.tensor_tensor(top[:, m % 2], g_max[:, m % 2], s1_col[:, m % 2], ALU.add).then_inc(top_s, 1)
                    dve.wait_ge(top_s, 2 * b + 1 + extra)
                    dve.scalar_tensor_tensor(out=most[:, m % 2], in0=top[:, m % 2], scalar=ALPHA, in1=top[:, m % 2],
                                             op0=ALU.mult, op1=ALU.max).then_inc(top_s, 1)
                    dve.wait_ge(top_s, 2 * b + 2 + extra)
                    dve.scalar_tensor_tensor(out=c_col[:, m % 2], in0=s1_col[:, m % 2], scalar=ALPHA, in1=most[:, m % 2],
                                             op0=ALU.mult, op1=ALU.subtract).then_inc(c_ready, 1)

            def sums(i, u):
                dve.wait_ge(r_done, i * S + u + 1)
                for k in range(2):
                    half = slice(k * HALF, (k + 1) * HALF)
                    dve.wait_ge(s2_full, 2 * (i * S + u) + k + 1)
                    dve.tensor_tensor(z[:, u % PLACES, half], s2[:, k], r[:, u % PLACES, half], ALU.add)\
                       .then_inc(z_done, 1)

            def output(i, m):
                b = i * NS + m
                dve.wait_ge(av_done, (b + 1) * T)
                for bank in range(ACC_BANKS):
                    n = min(APB, T - bank * APB)
                    den = acc[:, bank, 0:n * VW].rearrange("p (t c) -> p t c", t=n)[:, :, D:VW]
                    last = dve.reciprocal(rec[:, bank * APB:bank * APB + n].unsqueeze(2), den)
                last.then_inc(xa_s, 1)
                dve.wait_ge(xa_s, (b + 1) if not gated else 2 * b + 1)
                for t in range(T):
                    xs = x_sb[:, b * T + t]
                    dst, add = (hp[:, t], v_sl[m % 2][:, t, 0:D]) if gated else (xs, xs)
                    last = dve.scalar_tensor_tensor(out=dst, in0=acc_tile(t, 0, D), scalar=rec[:, t:t + 1], in1=add,
                                                    op0=ALU.mult, op1=ALU.add)
                last.then_inc(acc_free, 1)
                if gated:
                    xs = x_sb[:, bass.ds(b * T, T)]
                    dve.wait_ge(acc_free, b + 2)
                    dve.scalar_tensor_tensor(out=xs, in0=hp[:], scalar=0.0, in1=xs, op0=ALU.max, op1=ALU.add)\
                       .then_inc(xa_s, 1)
                    dve.wait_ge(elu_ready, b + 1)
                    dve.wait_ge(xa_s, 2 * b + 2)
                    dve.scalar_tensor_tensor(out=xs, in0=neg[:], scalar=-1.0, in1=xs, op0=ALU.add, op1=ALU.add)\
                       .then_inc(x_out, 1)

            def body(part, i, steps):
                n = 0
                for s in steps:
                    if has(part, s + sc.LAG):
                        sums(i, s + sc.LAG)
                    if has(part, s) and s % T == T - 1:
                        output(i, s // T)
                    for kind, m, k in sc.work(part, s):
                        if gated and kind == "V":
                            project(part, i, n, m, k)
                            if k == 1:
                                project_stats(i, m)
                        n += 1
                    for at, act_on in sorted({sc.stats: norm_stats, sc.rows: norm_rows}.items()) + (
                            [(7, project_rows)] if gated else []):
                        if sc.lead(part, s, at) is not None:
                            act_on(i, sc.lead(part, s, at))
                    for at, tiles in sc.neighbours.items():
                        if sc.lead(part, s, at) is not None:
                            for t in tiles:
                                neighbours(i, sc.lead(part, s, at), t)

            parts(dve, body)

        @block.gpsimd
        def _(pool):
            pool.wait_ge(w_in, 16 * (8 if gated else 3))
            root = rsqrt_steps(pool, nc, mean_var, rvar, guess, rstd, root_s, rstd_ready, var_ready, tick_pool)
            if gated:
                root2 = rsqrt_steps(pool, nc, mean_var2, rvar2, guess2, rstd2, root2_s, rstd2_ready, var2_ready,
                                    tick_pool)

            def body(part, i, steps):
                for s in steps:
                    m = sc.lead(part, s, sc.stats)
                    if m is not None:
                        root(i * NS + m)
                    m = sc.lead(part, s, 9)
                    if gated and m is not None:
                        root2(i * NS + m)
                    m = sc.lead(part, s, 7)
                    if gated and m is not None:
                        b = i * NS + m
                        pool.wait_ge(n2_ready, b + 1)
                        pool.tensor_tensor(scaled[:], raw[:], gamma[:].unsqueeze(1).to_broadcast([P, T, D]), ALU.mult)\
                            .then_inc(gb_s, 1)
                        if not (part == "pre" and m == 0):
                            pool.wait_ge(v_in[(m - 1) % 2], (i + (m - 1) // 2 + 1) * 16)
                        pool.wait_ge(gb_s, b + 1)
                        pool.tensor_tensor(stage_v[:, :, 0:D], scaled[:], beta[:].unsqueeze(1).to_broadcast([P, T, D]),
                                           ALU.add).then_inc(staged, 1)

            parts(pool, body)


def kernel(x, adj, L0_gnn_Ws, L0_gnn_Wt, L0_gnn_Wc, L1_gnn_Wq, L1_gnn_Wk, L1_gnn_Wv, L1_gnn_Wo, L1_gnn_bo, L2_gnn_W,
           L2_gnn_a, L2_gnn_node_weights, L2_gnn_node_bias, L2_gnn_ln_gamma, L2_gnn_ln_beta, L3_gnn_W, L3_gnn_a):
    import concourse.bacc as bacc
    from concourse.bass_utils import run_bass_kernel_spmd

    def rows(v):
        return np.broadcast_to(np.asarray(v)[None, :], (P, len(v)))

    arrays = {
        "x": x, "adj": adj, "adj_t": np.asarray(adj).T,
        "w_st": np.concatenate([L0_gnn_Ws, L0_gnn_Wt], axis=1), "w_c": L0_gnn_Wc,
        "w_q": np.asarray(L1_gnn_Wq).T, "w_k": np.asarray(L1_gnn_Wk).T, "w_v": np.asarray(L1_gnn_Wv).T,
        "w_o": np.asarray(L1_gnn_Wo).T, "b_o": rows(L1_gnn_bo),
        "w_2": L2_gnn_W, "a_2": np.asarray(L2_gnn_a).reshape(2, D).T,
        "nw": np.asarray(L2_gnn_node_weights).reshape(T, P).T, "nb": np.asarray(L2_gnn_node_bias).reshape(T, P).T,
        "gamma": rows(L2_gnn_ln_gamma), "beta": rows(L2_gnn_ln_beta),
        "gamma_c": np.asarray(L2_gnn_ln_gamma)[:, None], "beta_c": np.asarray(L2_gnn_ln_beta)[:, None],
        "w_3": L3_gnn_W, "w_3t": np.asarray(L3_gnn_W).T, "a_3": np.asarray(L3_gnn_a).reshape(2, D).T,
    }
    arrays = {k: np.ascontiguousarray(v) for k, v in arrays.items()}
    nc = bacc.Bacc("TRN2", target_bir_lowering=False, num_devices=1)
    args = {k: nc.dram_tensor(k, v.shape, mybir.dt.from_np(v.dtype), kind="ExternalInput").ap() for k, v in arrays.items()}
    out = nc.dram_tensor("out", (B, N, D), F32, kind="ExternalOutput").ap()
    build(nc, out=out, **args)
    return run_bass_kernel_spmd(nc, [arrays], core_ids=[0]).results[0]["out"]
```

```python
from contextlib import ExitStack

import numpy as np
import concourse.bass as bass
from concourse import mybir
from concourse.alu_op_type import AluOpType as ALU

ACT = mybir.ActivationFunctionType
F32, F16, BF16, I32 = mybir.dt.float32, mybir.dt.float16, mybir.dt.bfloat16, mybir.dt.int32

P = 128
B = 8
N = 1024
D = 128
T = N // P
HALF = 512
BIG = 1.0e30
EPS = 1e-5
SPLIT = 64.0
VSCALE = 256.0
SHIFT = 1024.0
PBIAS = float(12 * np.log(2.0))
ALPHA = 0.2


def build(nc, x, adj, w_st, w_c, w_q, w_k, w_v, w_o, b_o, w_2, a_2, nw, nb, gamma, beta, gamma_c, beta_c, w_3, w_3t,
          a_3, out):
    with ExitStack() as ctx:
        x_sb = ctx.enter_context(nc.sbuf_tensor("x_sb", [P, B * T, D], F32))
        mask_a = ctx.enter_context(nc.sbuf_tensor("mask_a", [P, T, N], BF16))
        mask_t = ctx.enter_context(nc.sbuf_tensor("mask_t", [P, T, N], BF16))
        ident_f = ctx.enter_context(nc.sbuf_tensor("ident_f", [P, P], F32))
        ident_b = ctx.enter_context(nc.sbuf_tensor("ident_b", [P, P], BF16))
        ident_h = ctx.enter_context(nc.sbuf_tensor("ident_h", [P, P], F16))
        shared = dict(x_sb=x_sb, mask_a=mask_a, mask_t=mask_t, ident_f=ident_f, ident_b=ident_b, ident_h=ident_h)
        x_rest = ctx.enter_context(nc.semaphore("x_rest"))
        set_up(nc, x, adj, x_rest, **shared)
        score_layer(nc, Score("L0", heads=1, maps=2, work_banks=3, rot=0, pool=(1, 3, 5, 7)),
                    dict(qk=[w_st], v=w_c), x_rest=x_rest, **shared)
        score_layer(nc, Score("L1", heads=4, maps=4, work_banks=3, rot=3, pool=(0, 2, 3, 5, 6)),
                    dict(qk=[w_q, w_k], v=w_v, o=w_o, b=b_o), **shared)
        gat_layer(nc, Gat("L2", gated=True), dict(v=w_2, s=a_2, gate=nw, shift=nb, gamma=gamma, beta=beta,
                                                  gamma_c=gamma_c, beta_c=beta_c), **shared)
        gat_layer(nc, Gat("L3", gated=False), dict(v=w_3, vt=w_3t, s=a_3), out=out, **shared)


def set_up(nc, x, adj, x_rest, x_sb, mask_a, mask_t, ident_f, ident_b, ident_h):
    RING = 4
    with ExitStack() as ctx:
        ring = ctx.enter_context(nc.sbuf_tensor("adj_ring", [P, RING, N], I32))
        turned = ctx.enter_context(nc.psum_tensor("turned", [P, 2, N], BF16))
        x_in = ctx.enter_context(nc.semaphore("x_in"))
        adj_in = [ctx.enter_context(nc.semaphore(f"adj_in{r}")) for r in range(RING)]
        masked = ctx.enter_context(nc.semaphore("masked"))
        blank = ctx.enter_context(nc.semaphore("blank"))
        idents = ctx.enter_context(nc.semaphore("idents"))
        turned_full = ctx.enter_context(nc.semaphore("turned_full"))
        turned_out = ctx.enter_context(nc.semaphore("turned_out"))
        block = ctx.enter_context(nc.Block())

        @block.sync
        def _(sp):
            sp.dma_start(x_sb[:, 0:T], x[0].rearrange("(t p) d -> p t d", p=P)).then_inc(x_in, 16)
            for k in range(T):
                if k >= RING:
                    sp.wait_ge(masked, k - RING + 1)
                sp.dma_start(ring[:, k % RING], adj[k * P:(k + 1) * P, :]).then_inc(adj_in[k % RING], 16)
            for b in range(1, B):
                sp.dma_start(x_sb[:, b * T:(b + 1) * T], x[b].rearrange("(t p) d -> p t d", p=P)).then_inc(x_rest, 16)
            sp.wait_ge(x_in, 16)

        @block.tensor
        def _(pe):
            pe.wait_ge(idents, 1)
            for k in range(T):
                pe.wait_ge(masked, k + 1)
                if k >= 2:
                    pe.wait_ge(turned_out, k - 1)
                for t in range(T):
                    last = pe.transpose(turned[:, k % 2, t * P:(t + 1) * P], mask_a[:, k, t * P:(t + 1) * P], ident_b[:])
                last.then_inc(turned_full, 1)

        @block.scalar
        def _(act):
            for k in range(T):
                act.wait_ge(turned_full, k + 1)
                act.activation(mask_t[:, :, k * P:(k + 1) * P], turned[:, k % 2].rearrange("p (t c) -> p t c", t=T),
                               ACT.Copy).then_inc(turned_out, 1)

        @block.vector
        def _(dve):
            for k in range(T):
                dve.wait_ge(adj_in[k % RING], 16 * (k // RING + 1))
                dve.tensor_scalar(mask_a[:, k], ring[:, k % RING], 0.0, -BIG, ALU.is_le, ALU.mult).then_inc(masked, 1)

        @block.gpsimd
        def _(pool):
            for ident in (ident_f, ident_b, ident_h):
                pool.memset(ident[:], 0.0).then_inc(blank, 1)
            for k, ident in enumerate((ident_f, ident_b, ident_h)):
                pool.wait_ge(blank, k + 1)
                last = pool.affine_select(out=ident[:], in_=ident[:], compare_op=ALU.not_equal, fill=1.0,
                                          base=0, pattern=[[-1, P]], channel_multiplier=1)
            last.then_inc(idents, 1)


class Score:

    def __init__(self, name, heads, maps, work_banks, rot, pool):
        self.name, self.heads, self.maps, self.work_banks, self.rot, self.pool = name, heads, maps, work_banks, rot, pool
        self.batches = maps // heads
        self.iters = B // self.batches
        self.steps = T * maps
        self.dh = D // heads
        self.multi = heads > 1
        self.ahead = 5 if self.multi else 3
        self.places = 8 if self.multi else 4
        self.mrow = 96 if self.multi else 64
        self.projections = 4 if self.multi else 2
        self.vw = 2 * self.dh + 1
        self.aw = self.dh + 1
        self.acc_per_bank = min(T, HALF // self.aw)
        self.acc_banks = -(-T // self.acc_per_bank)
        self.root_lag = 3 if self.multi else 1
        self.pre = list(range(-(rot + self.ahead + 22) if self.multi else -(rot + 16), 0))

    def before(self, s, n):
        return divmod(s + self.rot + self.ahead + n, T)

    def norm_at(self, part, s, later=0):
        if self.multi:
            return 0 if part == "pre" and s == self.pre[0] + later else 1 if part == "body" and s == later else None
        m, t = self.before(s - later, 13)
        return m if t == 0 and m >= 0 and (part != "last" or m < self.maps) else None

    def work(self, part, s):
        prologue = [("T", 0), ("T", 1)] + [("QK", k) for k in range(self.projections)] + [("V", 0), ("V", 1)]
        if self.multi:
            if part == "pre" and s - self.pre[0] < 11:
                j = s - self.pre[0] - 3
                return [(kind, 0, k) for kind, k in prologue[j:j + 1]] if j >= 0 else []
            m, t = self.before(s, 11)
            got = [("S1", m, 2 * t), ("S1", m, 2 * t + 1)]
            m, t = self.before(s, 2)
            if t == 0:
                got += [("M", m, 0), ("M", m, 1)]
            got = [g for g in got if g[1] >= 0 and (part != "last" or g[1] < self.maps)]
            if part == "body" and 4 <= s < 12:
                got.append((prologue[s - 4][0], 1, prologue[s - 4][1]))
            if part != "pre":
                got += [("OT", 0, 0), ("OT", 0, 1)] if s == 30 else []
                got = ([("WO", 0, 0), ("WO", 0, 1)] if s == 31 else []) + got
            return got
        got = []
        for n, uses in ((7, [("S1", k) for k in (0, 1, 2)]), (6, [("S1", k) for k in (3, 4, 5)]),
                        (5, [("S1", k) for k in (6, 7, 8)]), (4, [("S1", k) for k in (9, 10, 11)]),
                        (3, [("S1", k) for k in (12, 13)]), (2, [("S1", k) for k in (14, 15)]),
                        (1, [("M", 0), ("M", 1)]), (11, [("T", 0)]), (10, [("T", 1)]), (9, [("QK", 0), ("QK", 1)]),
                        (8, [("V", 0), ("V", 1)])):
            m, t = self.before(s, n)
            if t == 0:
                got += [(kind, m, k) for kind, k in uses]
        return [g for g in got if g[1] >= 0 and (part != "last" or g[1] < self.maps)]

    def uses(self, part):
        steps = self.pre if part == "pre" else range(self.steps)
        return [g for s in steps for g in self.work(part, s)]


def rsqrt_steps(pool, nc, mean_var, rvar, guess, rstd, root_s, done, var_ready, tick, offset=None):
    NEWTON = 3
    WAITS = 3 + 4 * NEWTON - 1 + (2 if offset is not None else 0)

    tmp = guess[:].bitcast(F32)

    def inverse_root(b):
        k = [b * WAITS]

        def step(instruction):
            instruction.then_inc(root_s, 1)
            k[0] = k[0] + 1
            pool.wait_ge(root_s, k[0])
            pool.sem_inc(tick, 1)

        pool.wait_ge(var_ready, b + 1)
        pool.sem_inc(tick, 1)
        if offset is not None:
            step(pool.tensor_scalar(offset[:], mean_var[:, :, 0], -1.0, None, ALU.mult))
        step(pool.tensor_scalar(rvar[:], mean_var[:, :, 1], EPS, None, ALU.add))
        step(pool.tensor_scalar(guess[:], rvar[:].bitcast(I32), -0.5, float(0x5F3759DF), ALU.mult, ALU.add))
        step(pool.tensor_copy(rstd[:].bitcast(I32), guess[:]))
        for n in range(NEWTON):
            step(pool.tensor_tensor(tmp, rstd[:], rstd[:], ALU.mult))
            step(pool.tensor_tensor(tmp, tmp, rvar[:], ALU.mult))
            step(pool.tensor_scalar(tmp, tmp, -0.5, 1.5, ALU.mult, ALU.add))
            y = pool.tensor_tensor(rstd[:], rstd[:], tmp, ALU.mult)
            if n < NEWTON - 1:
                step(y)
        if offset is None:
            y.then_inc(done, 1)
        else:
            step(y)
            pool.tensor_tensor(offset[:], offset[:], rstd[:], ALU.mult).then_inc(done, 1)

    return inverse_root


def score_layer(nc, sc, w, x_sb, mask_a, mask_t, ident_f, ident_b, ident_h, x_rest=None):
    NS, S, L, dh, multi = sc.maps, sc.steps, sc.name, sc.dh, sc.multi
    PLACES = sc.places
    EXP_SCALE = 1.0 / SPLIT ** 2 / (float(np.sqrt(dh)) if multi else 1.0)
    KH = sc.projections + 2
    N_QK = len(w["qk"])
    PIECES = 1 if multi else 2
    PW = N // PIECES
    N_ST = 1 if multi else 2
    S1_ROWS = [96] if multi else [64]
    S2_ROWS = [97] if multi else [128, 65]
    USES = {part: sc.uses(part) for part in ("pre", "body", "last")}
    N_PRE, N_BODY = len(USES["pre"]), len(USES["body"])
    assert N_BODY % sc.work_banks == 0

    with ExitStack() as ctx:
        def sb(name, shape, dt):
            return ctx.enter_context(nc.sbuf_tensor(f"{L}_{name}", shape, dt))

        def ps(name, shape, dt=F32):
            return ctx.enter_context(nc.psum_tensor(f"{L}_{name}", shape, dt))

        def sem(name):
            return ctx.enter_context(nc.semaphore(f"{L}_{name}"))

        def sem_multi(name):
            return sem(name) if multi else None

        w_qk = [sb(f"w_qk{k}", [P, P], F32) for k in range(N_QK)]
        w_v = sb("w_v", [P, D], F32)
        stats = sb("stats", [P, T, 6], F32)
        mean_var = sb("mean_var", [P, T, 2], F32)
        rvar = sb("rvar", [P, T], F32)
        guess = sb("guess", [P, T], I32)
        rstd = sb("rstd", [P, T], F32)
        hn = sb("hn", [P, T, D], F32)
        h_t = sb("h_t", [P, N], F32)
        stage_hi = [sb(f"stage_hi{k}", [P, N], F16) for k in range(N_QK)]
        stage_lo = [sb(f"stage_lo{k}", [P, N], F16) for k in range(N_QK)]
        stage_v = sb("stage_v", [P, sc.heads, T, sc.vw], F16)
        st_q = [[sb(f"st_q{m}_{k}", [P, N], F16) for k in range(N_ST)] for m in range(NS)]
        st_k = [[sb(f"st_k{m}_{k}", [P, N], F16) for k in range(N_ST)] for m in range(NS)]
        v_sl = [sb(f"v{m}", [P, T, sc.vw], F16) for m in range(NS)]
        junk = sb("junk", [P, sc.work_banks, HALF], BF16)
        mx_half = sb("mx_half", [P, NS, 2, T], F32)
        mx = sb("mx", [P, NS, T], F32)
        mneg = sb("mneg", [P, NS, T], F16)
        pbias = sb("pbias", [P, 1], F32)
        p32 = sb("p32", [P, PLACES, N], F32)
        p_hi = sb("p_hi", [P, PLACES, N], F16)
        p_lo = sb("p_lo", [P, PLACES, N], F16)
        rec = sb("rec", [P, T], F32)
        if multi:
            w_o = sb("w_o", [P, D], F32)
            b_o = sb("b_o", [P, D], F32)
            o = sb("o", [P, T, D], F32)
            o_t = sb("o_t", [P, N], F32)

        s2 = ps("s2", [P, 2, PW])
        wk = ps("wk", [P, sc.work_banks, HALF])
        acc = ps("acc", [P, sc.acc_banks, HALF])

        def acc_tile(t, a, b):
            base = (t % sc.acc_per_bank) * sc.aw
            return acc[:, t // sc.acc_per_bank, base + a:base + b]

        def acc_cols(bank, a, b):
            n = min(sc.acc_per_bank, T - bank * sc.acc_per_bank)
            tiles = slice(bank * sc.acc_per_bank, bank * sc.acc_per_bank + n)
            return acc[:, bank, 0:n * sc.aw].rearrange("p (t c) -> p t c", t=n)[:, :, a:b], tiles

        w_in = sem("w_in")
        consts = sem("consts")
        ready = sem("ready")
        tick_dve = sem("tick_dve")
        tick_pool = sem("tick_pool")
        stat_s = sem("stat_s")
        var_ready = sem("var_ready")
        root_s = sem("root_s")
        rstd_ready = sem("rstd_ready")
        ln_ready = sem("ln_ready")
        wk_full = sem("wk_full")
        hi_done = sem("hi_done")
        h_ready = sem("h_ready")
        qk_ready = sem("qk_ready")
        v_ready = sem("v_ready")
        s1_done = sem("s1_done")
        m_row = sem("m_row")
        ot_ready = sem_multi("ot_ready")
        x_done = sem_multi("x_done")
        st_in = [sem(f"st_in{m}") for m in range(NS)]
        v_in = [sem(f"v_in{m}") for m in range(NS)]
        mx_s = sem("mx_s")
        m_col = sem("m_col")
        s2_full = sem("s2_full")
        p32_done = sem("p32_done")
        phi_done = sem("phi_done")
        plo_dve = sem("plo_dve")
        plo_pool = sem("plo_pool")
        av_done = sem("av_done")
        ep_s = sem("ep_s")
        acc_free = sem("acc_free")
        xb_ready = sem_multi("xb_ready")

        def map_no(i, m):
            return i * NS + m

        def batch_no(i, m):
            return i * sc.batches + m // sc.heads

        def wait_released(eng, i, kind, m, k):
            if kind == "T":
                eng.wait_ge(h_ready, 2 * (i * sc.batches + m) + k + 1)
            elif kind == "QK":
                eng.wait_ge(qk_ready, sc.projections * (i * sc.batches + m) + k + 1)
            elif kind == "V":
                eng.wait_ge(v_ready, 2 * (i * sc.batches + m) + k + 1)
            elif kind == "S1":
                eng.wait_ge(s1_done, 2 * T * map_no(i, m) + k + 1)
            elif kind == "M":
                eng.wait_ge(m_row, 2 * map_no(i, m) + k + 1)
            elif kind == "OT":
                eng.wait_ge(ot_ready, 2 * i + k + 1)
            elif kind == "WO":
                eng.wait_ge(x_done, 2 * i + k + 1)

        def use_no(part, i, n):
            return n if part == "pre" else N_PRE + i * N_BODY + n

        def bank_of(part, n):
            return (n if part == "pre" else N_PRE + n) % sc.work_banks

        def pooled(t):
            return sum(a <= t for a in sc.pool)

        def wait_low(eng, i, u):
            m, t = divmod(u, T)
            if t in sc.pool:
                eng.wait_ge(plo_pool, map_no(i, m) * pooled(T - 1) + pooled(t))
            else:
                eng.wait_ge(plo_dve, map_no(i, m) * (T - pooled(T - 1)) + t + 1 - pooled(t))

        def parts(eng, body):
            body("pre", 0, sc.pre)
            with eng.Fori(0, sc.iters - 1) as i:
                body("body", i, range(S))
            body("last", sc.iters - 1, range(S))

        def has(part, u):
            return u >= 0 and (part != "last" or u < S)

        def ordered(part, s):
            got = sc.work(part, s)
            if has(part, s + sc.rot):
                got.insert(2, ("values", 0, 0))
            if has(part, s + sc.rot + sc.ahead):
                for piece in range(PIECES):
                    got.insert(2 * piece, ("scores", 0, piece))
            return got

        block = ctx.enter_context(nc.Block())

        @block.sync
        def _(sp):
            for dst, src in [*zip(w_qk, w["qk"]), (w_v, w["v"])] + ([(w_o, w["o"]), (b_o, w["b"])] if multi else []):
                sp.dma_start(dst[:], src).then_inc(w_in, 16)
            sp.wait_ge(consts, 1)

            def fill_stack(i, m):
                slot, h = m % NS, m % sc.heads
                sp.wait_ge(qk_ready, sc.projections * batch_no(i, m) + sc.projections)
                if multi:
                    rows = slice(h * dh, (h + 1) * dh)
                    moves = [(st_q[slot][0], stage_hi[0], rows, 0), (st_q[slot][0], stage_hi[0], rows, dh),
                             (st_q[slot][0], stage_lo[0], rows, 2 * dh), (st_k[slot][0], stage_hi[1], rows, 0),
                             (st_k[slot][0], stage_lo[1], rows, dh), (st_k[slot][0], stage_hi[1], rows, 2 * dh)]
                else:
                    q, k = slice(0, 64), slice(64, 128)
                    moves = [(st_q[slot][0], stage_hi[0], q, 0), (st_q[slot][0], stage_lo[0], q, 64),
                             (st_k[slot][0], stage_hi[0], k, 0), (st_k[slot][0], stage_hi[0], k, 64),
                             (st_q[slot][1], stage_hi[0], q, 0), (st_k[slot][1], stage_lo[0], k, 0)]
                for dst, src, rows, at in moves:
                    sp.dma_start(dst[at:at + rows.stop - rows.start, :], src[rows, :]).then_inc(st_in[slot], 16)

            def fill_values(i, m):
                sp.wait_ge(v_ready, 2 * batch_no(i, m) + 2)
                sp.dma_start(v_sl[m % NS][:], stage_v[:, m % sc.heads]).then_inc(v_in[m % NS], 16)

            def body(part, i, steps):
                for s in steps:
                    if multi and part == "pre" and s == steps[0]:
                        for m in range(NS):
                            fill_stack(i, m)
                            fill_values(i, m)
                    elif multi and part == "body" and s == 0:
                        for m in range(NS):
                            sp.wait_ge(av_done, (map_no(i, m) + 1) * T)
                            fill_stack(i, NS + m)
                            fill_values(i, NS + m)
                    elif not multi:
                        m, t = sc.before(s, 8)
                        if t == 0 and m >= 0 and (part != "last" or m < NS):
                            if m >= NS:
                                sp.wait_ge(s2_full, map_no(i, m - 1) * T * PIECES)
                            fill_stack(i, m)
                        m, t = sc.before(s, 6)
                        if t == 0 and m >= 0 and (part != "last" or m < NS):
                            if m >= NS:
                                sp.wait_ge(av_done, map_no(i, m - 1) * T)
                            fill_values(i, m)

            parts(sp, body)

        @block.tensor
        def _(pe):
            pe.wait_ge(consts, 1)
            pe.wait_ge(ready, 1)

            def take_bank(part, i, n):
                uses, back = USES[part], n - sc.work_banks
                if back >= 0:
                    wait_released(pe, i, *uses[back])
                elif part != "pre":
                    wait_released(pe, 0, *USES["pre"][N_PRE + back])
                    wait_released(pe, i - 1, *USES["body"][N_BODY + back])
                return wk[:, bank_of(part, n)]

            def work(part, i, n, kind, m, k):
                bank = take_bank(part, i, n)
                if kind == "T":
                    pe.wait_ge(ln_ready, T * (i * sc.batches + m) + 4 * k + 4)
                    for t in range(4):
                        last = pe.transpose(bank[:, t * P:(t + 1) * P], hn[:, 4 * k + t], ident_f[:])
                elif kind == "QK":
                    pe.wait_ge(h_ready, 2 * (i * sc.batches + m) + 2)
                    last = pe.matmul(bank, w_qk[k // 2][:], h_t[:, k % 2 * HALF:(k % 2 + 1) * HALF], start=True,
                                     stop=True)
                elif kind == "V":
                    for t in range(4):
                        last = pe.matmul(bank[:, t * P:(t + 1) * P], h_t[:, (4 * k + t) * P:(4 * k + t + 1) * P], w_v[:],
                                         start=(t == 0), stop=(t == 3), skip_group_check=True)
                elif kind == "S1":
                    slot, t, half = m % NS, k // 2, k % 2
                    if k == 0:
                        pe.wait_ge(st_in[slot], (i + m // NS + 1) * 6 * 16)
                    for j, r in enumerate(S1_ROWS):
                        last = pe.matmul(bank, st_q[slot][j][0:r, t * P:(t + 1) * P],
                                         st_k[slot][j][0:r, half * HALF:(half + 1) * HALF],
                                         start=(j == 0), stop=(j == len(S1_ROWS) - 1))
                elif kind == "M":
                    pe.wait_ge(m_col, map_no(i, m) + 1)
                    for t in range(4):
                        last = pe.matmul(bank[sc.mrow:sc.mrow + 1, t * P:(t + 1) * P],
                                         mneg[:, m % NS, 4 * k + t:4 * k + t + 1], ident_h[:], start=(t == 0),
                                         stop=(t == 3), skip_group_check=True)
                elif kind == "OT":
                    pe.wait_ge(acc_free, map_no(i, NS) + 1)
                    for t in range(4):
                        last = pe.transpose(bank[:, t * P:(t + 1) * P], o[:, 4 * k + t], ident_f[:])
                elif kind == "WO":
                    pe.wait_ge(ot_ready, 2 * i + k + 1)
                    for t in range(4):
                        last = pe.matmul(bank[:, t * P:(t + 1) * P], o_t[:, (4 * k + t) * P:(4 * k + t + 1) * P], w_o[:],
                                         start=(t == 0), stop=(t == 3), skip_group_check=True)
                last.then_inc(wk_full, 1)

            def values(part, i, u):
                m, t = divmod(u, T)
                slot = m % NS
                if t == 0:
                    pe.wait_ge(v_in[slot], (i + m // NS + 1) * 16)
                    pe.wait_ge(acc_free, map_no(i, m) + 1)
                pe.wait_ge(phi_done, (i * S + u + 1) * PIECES)
                wait_low(pe, i, u)
                v = v_sl[slot]
                for n in range(T):
                    hi = p_hi[:, u % PLACES, n * P:(n + 1) * P]
                    lo = p_lo[:, u % PLACES, n * P:(n + 1) * P]
                    first = t == 0 and n % sc.acc_per_bank == 0
                    pe.matmul(acc_tile(n, 0, dh + 1), hi, v[:, t, 0:dh + 1], start=first, stop=False,
                              skip_group_check=True)
                    pe.matmul(acc_tile(n, 0, dh), hi, v[:, t, dh + 1:], start=False, stop=False,
                              skip_group_check=True)
                    last = pe.matmul(acc_tile(n, 0, dh + 1), lo, v[:, t, 0:dh + 1], start=False, stop=(t == T - 1),
                                     skip_group_check=True)
                last.then_inc(av_done, 1)

            def scores(part, i, u, piece):
                m, t = divmod(u, T)
                slot = m % NS
                if t == 0 and piece == 0:
                    pe.wait_ge(m_row, 2 * map_no(i, m) + 2)
                q = u * PIECES + piece
                if q >= 2:
                    pe.wait_ge(phi_done, i * S * PIECES + q - 1)
                for at in range(0, PW, HALF):
                    dst, cols = s2[:, q % 2, at:at + HALF], slice(piece * PW + at, piece * PW + at + HALF)
                    pe.matmul(dst, ident_b[:], mask_t[:, t, cols], start=True, stop=False)
                    for j, r in enumerate(S2_ROWS):
                        last = pe.matmul(dst, st_k[slot][j][0:r, t * P:(t + 1) * P], st_q[slot][j][0:r, cols],
                                         start=False, stop=(j == N_ST - 1))
                last.then_inc(s2_full, 1)

            def body(part, i, steps):
                n = 0
                for s in steps:
                    for kind, m, k in ordered(part, s):
                        if kind == "scores":
                            scores(part, i, s + sc.rot + sc.ahead, k)
                        elif kind == "values":
                            values(part, i, s + sc.rot)
                        else:
                            work(part, i, n, kind, m, k)
                            n += 1

            parts(pe, body)

        @block.scalar
        def _(act):
            act.wait_ge(acc_free, 1)
            act.wait_ge(consts, 1)

            def work(part, i, n, kind, m, k):
                bank = wk[:, bank_of(part, n)]
                act.wait_ge(wk_full, use_no(part, i, n) + 1)
                b = i * sc.batches + m
                if kind == "T":
                    act.activation(h_t[:, k * HALF:(k + 1) * HALF], bank, ACT.Relu).then_inc(h_ready, 1)
                elif kind == "OT":
                    act.activation(o_t[:, k * HALF:(k + 1) * HALF], bank, ACT.Copy).then_inc(ot_ready, 1)
                elif kind == "QK":
                    if k == 0 and not (part == "pre" and m == 0):
                        for slot in (range(NS) if multi else [(m - 1) % NS]):
                            act.wait_ge(st_in[slot], (i + 1 if multi else i + (m - 1) // NS + 1) * 6 * 16)
                    act.activation(stage_hi[k // 2][:, k % 2 * HALF:(k % 2 + 1) * HALF], bank, ACT.Copy)\
                       .then_inc(hi_done, 1)
                elif kind == "V":
                    if k == 0 and not (part == "pre" and m == 0):
                        for slot in (range(NS) if multi else [(m - 1) % NS]):
                            act.wait_ge(v_in[slot], (i + 1 if multi else i + (m - 1) // NS + 1) * 16)
                    act.activation(stage_v[:, :, 4 * k:4 * k + 4, 0:dh].rearrange("p h t d -> p t h d"),
                                   bank.rearrange("p (t h d) -> p t h d", t=4, h=sc.heads), ACT.Copy)\
                       .then_inc(hi_done, 1)

            def probabilities(part, i, u, piece):
                q, cols = u * PIECES + piece, slice(piece * PW, (piece + 1) * PW)
                act.wait_ge(s2_full, i * S * PIECES + q + 1)
                if u >= PLACES and piece == 0:
                    wait_low(act, i, u - PLACES)
                act.activation(p32[:, u % PLACES, cols], s2[:, q % 2], ACT.Exp, bias=pbias[:], scale=EXP_SCALE)\
                   .then_inc(p32_done, 1)
                act.activation(p_hi[:, u % PLACES, cols], s2[:, q % 2], ACT.Exp, bias=pbias[:], scale=EXP_SCALE)\
                   .then_inc(phi_done, 1)

            def body(part, i, steps):
                n = 0
                for s in steps:
                    for kind, m, k in ordered(part, s):
                        if kind == "scores":
                            probabilities(part, i, s + sc.rot + sc.ahead, k)
                        elif kind != "values":
                            if kind in ("T", "QK", "V", "OT"):
                                work(part, i, n, kind, m, k)
                            n += 1

            parts(act, body)

        @block.vector
        def _(dve):
            dve.memset(pbias[:], PBIAS).then_inc(acc_free, 1)

            def constants():
                for m in range(NS):
                    dve.memset(st_k[m][-1][sc.mrow:sc.mrow + 1, :], SHIFT)
                dve.memset(stage_v[:, :, :, dh], VSCALE).then_inc(consts, 1)
                dve.wait_ge(w_in, 16 * (N_QK + 1 + 2 * multi))
                for t in w_qk:
                    dve.tensor_scalar(t[:], t[:], SPLIT, None, ALU.mult)
                dve.tensor_scalar(w_v[:], w_v[:], VSCALE, None, ALU.mult).then_inc(ready, 1)

            def norm_stats(i, m):
                b = i * sc.batches + m
                dve.wait_ge(ln_ready, T * b)
                for t in range(T):
                    last = dve.bn_stats(stats[:, t], x_sb[:, b * T + t])
                last.then_inc(stat_s, 1)
                dve.wait_ge(stat_s, b + 1)
                dve.sem_inc(tick_dve, 1)
                for t in range(T):
                    last = dve.bn_aggr(mean_var[:, t], stats[:, t])
                last.then_inc(var_ready, 1)

            def norm_rows(i, m):
                b = i * sc.batches + m
                dve.wait_ge(rstd_ready, b + 1)
                dve.wait_ge(h_ready, 2 * b)
                for t in range(T):
                    dve.tensor_scalar(hn[:, t], x_sb[:, b * T + t], mean_var[:, t, 0:1], rstd[:, t:t + 1],
                                      ALU.subtract, ALU.mult).then_inc(ln_ready, 1)

            def work(part, i, n, kind, m, k):
                bank = wk[:, bank_of(part, n)]
                half = slice(k % 2 * HALF, (k % 2 + 1) * HALF)
                if kind == "QK":
                    dve.wait_ge(hi_done, (i * sc.batches + m) * KH + k + 1)
                    dve.tensor_tensor(stage_lo[k // 2][:, half], bank, stage_hi[k // 2][:, half], ALU.subtract)\
                       .then_inc(qk_ready, 1)
                elif kind == "V":
                    dve.wait_ge(hi_done, (i * sc.batches + m) * KH + sc.projections + k + 1)
                    tiles = slice(4 * k, 4 * k + 4)
                    dve.tensor_tensor(stage_v[:, :, tiles, dh + 1:].rearrange("p h t d -> p t h d"),
                                      bank.rearrange("p (t h d) -> p t h d", t=4, h=sc.heads),
                                      stage_v[:, :, tiles, 0:dh].rearrange("p h t d -> p t h d"),
                                      ALU.subtract).then_inc(v_ready, 1)
                elif kind == "S1":
                    g = m % NS
                    dve.wait_ge(wk_full, use_no(part, i, n) + 1)
                    dve.sem_inc(tick_dve, 1)
                    dve.tensor_tensor_reduce(junk[:, bank_of(part, n)], bank, mask_a[:, k // 2, half], 1.0, -3.0e38,
                                             ALU.add, ALU.max, mx_half[:, g, k % 2, k // 2:k // 2 + 1])\
                       .then_inc(s1_done, 1)
                    if k == 2 * T - 1:
                        dve.wait_ge(s1_done, 2 * T * (map_no(i, m) + 1))
                        dve.tensor_tensor(mx[:, g], mx_half[:, g, 0], mx_half[:, g, 1], ALU.max).then_inc(mx_s, 1)
                        dve.wait_ge(mx_s, map_no(i, m) + 1)
                        dve.tensor_scalar(mneg[:, g], mx[:, g], -1.0 / SHIFT, None, ALU.mult).then_inc(m_col, 1)
                elif kind == "M":
                    dve.wait_ge(wk_full, use_no(part, i, n) + 1)
                    dve.tensor_copy(st_q[m % NS][-1][sc.mrow:sc.mrow + 1, half], bank[sc.mrow:sc.mrow + 1, :])\
                       .then_inc(m_row, 1)
                elif kind == "WO":
                    dve.wait_ge(wk_full, use_no(part, i, n) + 1)
                    dve.wait_ge(xb_ready, i + 1)
                    xs = x_sb[:, bass.ds(i * T + 4 * k, 4)]
                    dve.tensor_tensor(xs, xs, bank.rearrange("p (t d) -> p t d", t=4), ALU.add).then_inc(x_done, 1)

            def low_parts(i, u):
                dve.wait_ge(phi_done, (i * S + u + 1) * PIECES)
                dve.tensor_tensor(p_lo[:, u % PLACES], p32[:, u % PLACES], p_hi[:, u % PLACES], ALU.subtract)\
                   .then_inc(plo_dve, 1)

            def head_output(i, m):
                g, h = map_no(i, m), m % sc.heads
                dve.wait_ge(av_done, (g + 1) * T)
                den, _ = acc_cols(0, dh, dh + 1)
                num, _ = acc_cols(0, 0, dh)
                dve.reciprocal(rec[:].unsqueeze(2), den).then_inc(ep_s, 1)
                dve.wait_ge(ep_s, g + 1)
                dve.tensor_tensor(o[:, :, h * dh:(h + 1) * dh], num, rec[:].unsqueeze(2).to_broadcast([P, T, dh]),
                                  ALU.mult).then_inc(acc_free, 1)

            def batch_output(i, m):
                g = map_no(i, m)
                dve.wait_ge(av_done, (g + 1) * T)
                for bank in range(sc.acc_banks):
                    den, tiles = acc_cols(bank, dh, dh + 1)
                    last = dve.reciprocal(rec[:, tiles].unsqueeze(2), den)
                last.then_inc(ep_s, 1)
                dve.wait_ge(ep_s, g + 1)
                for t in range(T):
                    xs = x_sb[:, g * T + t]
                    last = dve.scalar_tensor_tensor(out=xs, in0=acc_tile(t, 0, dh), scalar=rec[:, t:t + 1], in1=xs,
                                                    op0=ALU.mult, op1=ALU.add)
                last.then_inc(acc_free, 1)

            def body(part, i, steps):
                n = 0
                for s in steps:
                    u = s + sc.rot
                    if sc.norm_at(part, s) is not None:
                        if x_rest is not None and part == "pre" and s > sc.pre[0]:
                            dve.wait_ge(x_rest, 16 * (B - 1))
                        norm_stats(i, sc.norm_at(part, s))
                    uses = sc.work(part, s)
                    for kind, m, k in uses[:2]:
                        work(part, i, n, kind, m, k)
                        n += 1
                    if has(part, u + sc.ahead - 1) and (u + sc.ahead - 1) % T not in sc.pool:
                        low_parts(i, u + sc.ahead - 1)
                    for kind, m, k in uses[2:]:
                        work(part, i, n, kind, m, k)
                        n += 1
                    if part == "pre" and s == sc.pre[0]:
                        constants()
                    if sc.norm_at(part, s, sc.root_lag) is not None:
                        norm_rows(i, sc.norm_at(part, s, sc.root_lag))
                    if has(part, u) and u % T == T - 1:
                        (head_output if multi else batch_output)(i, u // T)

            parts(dve, body)

        @block.gpsimd
        def _(pool):
            if multi:
                pool.wait_ge(w_in, 16 * (N_QK + 3))

            def low_parts(i, u):
                pool.wait_ge(phi_done, (i * S + u + 1) * PIECES)
                pool.tensor_tensor(p_lo[:, u % PLACES], p32[:, u % PLACES], p_hi[:, u % PLACES], ALU.subtract)\
                    .then_inc(plo_pool, 1)

            inverse_root = rsqrt_steps(pool, nc, mean_var, rvar, guess, rstd, root_s, rstd_ready, var_ready, tick_pool)

            def add_bias(b):
                pool.wait_ge(ln_ready, T * (b + 1))
                xs = x_sb[:, bass.ds(b * T, T)]
                pool.tensor_tensor(xs, xs, b_o[:].unsqueeze(1).to_broadcast([P, T, D]), ALU.add).then_inc(xb_ready, 1)

            def body(part, i, steps):
                for s in steps:
                    u = s + sc.rot + sc.ahead - 1
                    if has(part, u) and u % T in sc.pool:
                        low_parts(i, u)
                    if sc.norm_at(part, s, 1 if multi else 0) is not None:
                        inverse_root(i * sc.batches + sc.norm_at(part, s, 1 if multi else 0))
                    if multi and sc.norm_at(part, s, sc.root_lag + 1) is not None:
                        add_bias(i + sc.norm_at(part, s, sc.root_lag + 1))

            parts(pool, body)


class Gat:
    maps, steps, turns, AHEAD = 2, 2 * T, B // 2 - 2, 4

    def __init__(self, name, gated):
        self.name, self.gated = name, gated
        self.stats = 17 if gated else 16
        if gated:
            self.order = {-13: [("T", 0), ("T", 1)], -12: [("V", 0), ("V", 1)], -7: [("T2", 0), ("T2", 1)],
                          -6: [("SB", 0), ("SB", 1)], -3: [("SC", 0)], -2: [("SA", 0), ("SA", 1)],
                          -1: [("CR", 0), ("CR", 1)]}
        else:
            self.order = {-12: [("T", 0), ("T", 1)], -10: [("V", 0), ("V", 1)], -7: [("SB", 0), ("SB", 1)],
                          -6: [("SC", 0)], -5: [("SA", 0), ("SA", 1)], -1: [("CR", 0), ("CR", 1)]}
        self.stats2, self.rows2 = 11, 9
        self.neighbours = {5: (0, 1, 2), 4: (3, 4), 3: (5, 6), 2: (7,)} if gated else \
            {6: (0, 1), 5: (2, 3), 4: (4, 5), 3: (6, 7)}
        self.pre = list(range(-(self.stats + self.AHEAD), 0))

    def lead(self, part, s, n):
        m, t = divmod(s + self.AHEAD + n, T)
        return m if t == 0 and m >= 0 and (part != "last" or m < 2 * self.maps) else None

    def work(self, part, s):
        return [(kind, self.lead(part, s, -at), k) for at in sorted(self.order, reverse=True)
                if self.lead(part, s, -at) is not None for kind, k in self.order[at]]

    def uses(self, part):
        steps = self.pre if part == "pre" else range((2 if part == "last" else 1) * self.steps)
        return [g for s in steps for g in self.work(part, s)]


def gat_layer(nc, sc, w, x_sb, mask_a, mask_t, ident_f, ident_b, ident_h, out=None):
    S, L, gated, NS = sc.steps, sc.name, sc.gated, sc.maps
    PLACES = 4
    USES = {part: sc.uses(part) for part in ("pre", "body", "last")}
    N_PRE, N_BODY = len(USES["pre"]), len(USES["body"])
    VW = D + 1
    APB = 3
    ACC_BANKS = -(-T // APB)
    WK_BANKS = 3

    with ExitStack() as ctx:
        def sb(name, shape, dt):
            return ctx.enter_context(nc.sbuf_tensor(f"{L}_{name}", shape, dt))

        def ps(name, shape, dt=F32):
            return ctx.enter_context(nc.psum_tensor(f"{L}_{name}", shape, dt))

        def sem(name):
            return ctx.enter_context(nc.semaphore(f"{L}_{name}"))

        def sem_gated(name):
            return sem(name) if gated else None

        w_v = sb("w_v", [P, D], F32)
        w_s = sb("w_s", [P, 2], F32)
        w_r = sb("w_r", [P, 2, P], F32)
        stats = sb("stats", [P, T, 6], F32)
        mean_var = sb("mean_var", [P, T, 2], F32)
        rvar = sb("rvar", [P, T], F32)
        guess = sb("guess", [P, T], I32)
        rstd = sb("rstd", [P, T], F32)
        hn = sb("hn", [P, T, D], F32)
        h_t = sb("h_t", [P, N], F32)
        stage_v = sb("stage_v", [P, T, VW], F32)
        v_sl = [sb(f"v{m}", [P, T, VW], F32) for m in range(2)]
        s1_col = sb("s1_col", [P, 2, T], F32)
        s2_rise = sb("s2_rise", [P, 2, T], F32)
        s2_slope = sb("s2_slope", [P, 2, T], F32)
        s2_all = sb("s2_all", [P, 2, N], F32)
        s1_all = sb("s1_all", [P, 2, N], F32)
        c_row = sb("c_row", [1, 2, N], F16)
        ones = sb("ones", [1, P], F16)
        junk = sb("junk", [P, 2, N], BF16)
        g_max = sb("g_max", [P, 2, T], F32)
        top = sb("top", [P, 2, T], F32)
        most = sb("most", [P, 2, T], F32)
        c_col = sb("c_col", [P, 2, T], F16)
        r = sb("r", [P, PLACES, N], F32)
        z = sb("z", [P, PLACES, N], F32)
        p = sb("p", [P, PLACES, N], F32)
        rec = sb("rec", [P, T], F32)
        if gated:
            gate, shift = sb("gate", [P, T], F32), sb("shift", [P, T], F32)
            col_sum = sb("col_sum", [P, D], F32)
            shifted = sb("shifted", [P, T, D], F32)
            gamma_c, beta_c = sb("gamma_c", [P, 1], F32), sb("beta_c", [P, 1], F32)
            all_ones = sb("all_ones", [P, P], F32)
            gamma, beta = sb("gamma", [P, D], F32), sb("beta", [P, D], F32)
            raw = sb("raw", [P, T, D], F32)
            v_t = sb("v_t", [P, N], F32)
            stats2 = sb("stats2", [P, T, 6], F32)
            mean_var2 = sb("mean_var2", [P, T, 2], F32)
            rvar2 = sb("rvar2", [P, T], F32)
            guess2 = sb("guess2", [P, T], I32)
            rstd2 = sb("rstd2", [P, T], F32)
            offset2 = sb("offset2", [P, T], F32)
            scaled = sb("scaled", [P, T, D], F32)
            hp = sb("hp", [P, T, D], F32)
            neg = sb("neg", [P, T, D], F32)
        else:
            w_vt, a_s = sb("w_vt", [P, D], F32), sb("a_s", [P, 2], F32)
            v_t = h_t

        s2 = ps("s2", [P, 2, HALF])
        wk_banks = ps("wk", [P, WK_BANKS, HALF])
        acc = ps("acc", [P, ACC_BANKS, HALF])

        def acc_tile(t, a, b):
            return acc[:, t // APB, t % APB * VW + a:t % APB * VW + b]

        w_in = sem("w_in")
        ready = sem("ready")
        fold = sem("fold")
        tick_dve, tick_pool, tick_sp = sem("tick_dve"), sem("tick_pool"), sem("tick_sp")
        stat_s = sem("stat_s")
        var_ready = sem("var_ready")
        root_s = sem("root_s")
        rstd_ready = sem("rstd_ready")
        rows_s = sem("rows_s")
        ln_ready = sem("ln_ready")
        wk_full = sem("wk_full")
        h_ready = sem("h_ready")
        v_ready = sem("v_ready")
        st2_s = sem_gated("st2_s")
        var2_ready = sem_gated("var2_ready")
        root2_s = sem_gated("root2_s")
        rstd2_ready = sem_gated("rstd2_ready")
        n2_ready = sem_gated("n2_ready")
        gb_s = sem_gated("gb_s")
        staged = sem("staged") if gated else v_ready
        per_stage = 1 if gated else 2
        t2_ready = sem_gated("t2_ready")
        sc_ready = sem("sc_ready")
        sb_ready = sem("sb_ready")
        sa_ready = sem("sa_ready")
        cr_ready = sem("cr_ready")
        v_in = [sem(f"v_in{m}") for m in range(2)]
        g_done = sem("g_done")
        top_s = sem("top_s")
        c_ready = sem("c_ready")
        s2_full = sem("s2_full")
        r_done = sem("r_done")
        z_done = sem("z_done")
        p_done = sem("p_done")
        av_done = sem("av_done")
        stored = sem("stored") if out is not None else None
        pos_s = sem_gated("pos_s")
        acc_free = sem("acc_free")
        neg_s = sem_gated("neg_s")
        elu_ready = sem_gated("elu_ready")
        xa_s = sem("xa_s")

        def wait_released(eng, i, kind, m, k):
            b = i * NS + m
            if kind == "T":
                eng.wait_ge(h_ready, 2 * b + k + 1)
            elif kind == "V":
                eng.wait_ge(v_ready, 2 * b + k + 1)
            elif kind == "T2":
                eng.wait_ge(t2_ready, 2 * b + k + 1)
            elif kind == "SC":
                eng.wait_ge(sc_ready, b + 1)
            elif kind == "SB":
                eng.wait_ge(sb_ready, 2 * b + k + 1)
            elif kind == "SA":
                eng.wait_ge(sa_ready, 2 * b + k + 1)
            elif kind == "CR":
                eng.wait_ge(cr_ready, 2 * b + k + 1)

        def bank_of(part, n):
            return wk_banks[:, (n + N_BODY - N_PRE if part == "pre" else n) % WK_BANKS]

        def use_no(part, i, n):
            return n if part == "pre" else N_PRE + i * N_BODY + n

        def parts(eng, body):
            body("pre", 0, sc.pre)
            with eng.Fori(0, sc.turns) as i:
                body("body", i, range(S))
            body("last", sc.turns, range(2 * S))

        def has(part, u):
            return u >= 0 and (part != "last" or u < 2 * S)

        def ordered(part, s):
            got = sc.work(part, s)
            late = len(got) > 0 and got[0][0] == "CR"
            got.insert(0, ("scores", 0, 0))
            got.insert(1 if late else 2, ("scores", 0, 1))
            got.insert(2 if late else 4, ("values", 0, 0))
            return [g for g in got if g[0] != "scores" or has(part, s + sc.AHEAD)
                    if g[0] != "values" or has(part, s + 1)]

        block = ctx.enter_context(nc.Block())

        @block.sync
        def _(sp):
            loads = [(w_v, w["v"])]
            loads += [(w_s, w["s"]), (gate, w["gate"]), (shift, w["shift"]), (gamma, w["gamma"]), (beta, w["beta"]),
                      (gamma_c, w["gamma_c"]), (beta_c, w["beta_c"])] \
                if gated else [(w_vt, w["vt"]), (a_s, w["s"])]
            for dst, src in loads:
                sp.dma_start(dst[:], src).then_inc(w_in, 16)
            sp.wait_ge(ready, 2)

            def body(part, i, steps):
                for s in steps:
                    m = sc.lead(part, s, 6)
                    if m is not None:
                        sp.wait_ge(staged, per_stage * (i * NS + m + 1))
                        sp.sem_inc(tick_sp, 1)
                        if part != "pre":
                            sp.wait_ge(acc_free, i * NS + m)
                        sp.dma_start(v_sl[m % 2][:], stage_v[:]).then_inc(v_in[m % 2], 16)
                    if out is not None and part != "pre" and s % T == T - 2:
                        b = i * NS + s // T
                        sp.wait_ge(acc_free, b + 2)
                        sp.dma_start(out[bass.ds(b, 1)].rearrange("b (t p) d -> p (b t) d", p=P),
                                     x_sb[:, bass.ds(b * T, T)]).then_inc(stored, 16)

            parts(sp, body)
            if out is not None:
                sp.wait_ge(stored, 16 * B)

        @block.tensor
        def _(pe):
            if gated:
                pe.wait_ge(w_in, 16 * 8)
                pe.wait_ge(top_s, 1)
                pe.matmul(wk_banks[:, 0, 0:D], all_ones[:], w_v[:], start=True, stop=True).then_inc(fold, 1)
                pe.wait_ge(ready, 3)
            else:
                pe.wait_ge(w_in, 16 * 3)
                pe.matmul(wk_banks[:, 0, 0:2], w_vt[:], a_s[:], start=True, stop=True).then_inc(fold, 1)
                pe.wait_ge(ready, 3)

            def work(part, i, n, kind, m, k):
                b = i * NS + m
                wk = bank_of(part, n)
                if n >= WK_BANKS:
                    wait_released(pe, i, *USES[part][n - WK_BANKS])
                elif part != "pre":
                    back = 1 + (N_BODY - 1 - n) % WK_BANKS
                    wait_released(pe, 0, *USES["pre"][N_PRE - back])
                    wait_released(pe, i - 1, *USES["body"][N_BODY - back])
                half = slice(k * HALF, (k + 1) * HALF)
                if kind in ("T", "T2"):
                    src = hn if kind == "T" else raw
                    if kind == "T":
                        pe.wait_ge(ln_ready, b + 1)
                    else:
                        pe.wait_ge(n2_ready, b + 1)
                    for t in range(4):
                        last = pe.transpose(wk[:, t * P:(t + 1) * P], src[:, 4 * k + t], ident_f[:])
                elif kind == "V":
                    pe.wait_ge(h_ready, 2 * b + 2)
                    for t in range(4):
                        last = pe.matmul(wk[:, t * P:(t + 1) * P], h_t[:, (4 * k + t) * P:(4 * k + t + 1) * P], w_v[:],
                                         start=(t == 0), stop=(t == 3), skip_group_check=True)
                elif kind == "SC":
                    for t in range(T):
                        last = pe.matmul(wk[:, 2 * t:2 * t + 2], v_t[:, t * P:(t + 1) * P], w_s[:], start=(t == 0),
                                         stop=(t == T - 1), skip_group_check=True)
                elif kind == "SB":
                    if gated:
                        pe.wait_ge(t2_ready, 2 * b + 2)
                    last = pe.matmul(wk, w_r[:, 1], v_t[:, half], start=True, stop=True)
                elif kind == "SA":
                    last = pe.matmul(wk, w_r[:, 0], v_t[:, half], start=True, stop=True)
                elif kind == "CR":
                    pe.wait_ge(c_ready, b + 1)
                    for t in range(4):
                        last = pe.matmul(wk[0:1, t * P:(t + 1) * P], c_col[:, m % 2, 4 * k + t:4 * k + t + 1], ident_h[:],
                                         start=(t == 0), stop=(t == 3), skip_group_check=True)
                last.then_inc(wk_full, 1)

            def values(part, i, u):
                m, t = divmod(u, T)
                if t == 0:
                    pe.wait_ge(v_in[m % 2], (i + m // 2 + 1) * 16)
                    pe.wait_ge(acc_free, i * NS + m + 1)
                pe.wait_ge(p_done, i * S + u + 1)
                for n in range(T):
                    last = pe.matmul(acc_tile(n, 0, VW), p[:, u % PLACES, n * P:(n + 1) * P], v_sl[m % 2][:, t],
                                     start=(t == 0 and n % APB == 0), stop=(t == T - 1), skip_group_check=True)
                last.then_inc(av_done, 1)

            def scores(part, i, u, k):
                m, t = divmod(u, T)
                if t == 0 and k == 0:
                    pe.wait_ge(cr_ready, 2 * (i * NS + m) + 2)
                if u >= 1:
                    pe.wait_ge(z_done, 2 * (i * S + u - 1) + k + 1)
                half = slice(k * HALF, (k + 1) * HALF)
                pe.matmul(s2[:, k], ident_b[:], mask_t[:, t, half], start=True, stop=False)
                pe.matmul(s2[:, k], ones[:], c_row[:, m % 2, half], start=False, stop=True).then_inc(s2_full, 1)

            def body(part, i, steps):
                n = 0
                for s in steps:
                    for kind, m, k in ordered(part, s):
                        if kind == "scores":
                            scores(part, i, s + sc.AHEAD, k)
                        elif kind == "values":
                            values(part, i, s + 1)
                        else:
                            work(part, i, n, kind, m, k)
                            n += 1

            parts(pe, body)

        @block.scalar
        def _(act):
            act.wait_ge(ready, 3)

            def work(part, i, n, kind, m, k):
                if kind == "V" and gated:
                    return
                act.wait_ge(wk_full, use_no(part, i, n) + 1)
                wk = bank_of(part, n)
                b = i * NS + m
                half = slice(k * HALF, (k + 1) * HALF)
                if kind == "T":
                    act.activation(h_t[:, half], wk, ACT.Relu).then_inc(h_ready, 1)
                elif kind == "V":
                    if k == 0 and not (part == "pre" and m == 0):
                        act.wait_ge(v_in[(m - 1) % 2], (i + (m - 1) // 2 + 1) * 16)
                    act.activation(stage_v[:, 4 * k:4 * k + 4, 0:D], wk.rearrange("p (t d) -> p t d", t=4), ACT.Copy)\
                       .then_inc(v_ready, 1)
                elif kind == "T2":
                    act.activation(v_t[:, half], wk, ACT.Identity, bias=beta_c[:], scale=gamma_c[:]).then_inc(t2_ready, 1)
                elif kind == "SC":
                    if m >= 2:
                        act.wait_ge(p_done, (b - 1) * T)
                    cols = wk[:, 0:2 * T].rearrange("p (t s) -> p t s", s=2)
                    act.activation(s1_col[:, m % 2].unsqueeze(2), cols[:, :, 0:1], ACT.Copy)
                    act.activation(s2_rise[:, m % 2].unsqueeze(2), cols[:, :, 1:2], ACT.Copy, scale=1.0 - ALPHA)
                    act.activation(s2_slope[:, m % 2].unsqueeze(2), cols[:, :, 1:2], ACT.Copy, scale=ALPHA)\
                       .then_inc(sc_ready, 1)
                elif kind == "SB":
                    act.activation(s2_all[:, m % 2, half], wk, ACT.Copy).then_inc(sb_ready, 1)
                elif kind == "SA":
                    act.activation(s1_all[:, m % 2, half], wk, ACT.Copy).then_inc(sa_ready, 1)
                elif kind == "CR":
                    act.activation(c_row[:, m % 2, half], wk[0:1, :], ACT.Copy).then_inc(cr_ready, 1)

            def rises(i, u):
                m, t = divmod(u, T)
                if t == 0:
                    act.wait_ge(sa_ready, 2 * (i * NS + m) + 2)
                act.activation(r[:, u % PLACES], s1_all[:, m % 2], ACT.Relu, bias=s2_rise[:, m % 2, t:t + 1],
                               scale=1.0 - ALPHA).then_inc(r_done, 1)

            def probabilities(i, u):
                m, t = divmod(u, T)
                act.wait_ge(z_done, 2 * (i * S + u) + 2)
                act.activation(p[:, u % PLACES], z[:, u % PLACES], ACT.Exp, bias=s2_slope[:, m % 2, t:t + 1])\
                   .then_inc(p_done, 1)

            def project_rows(i, m):
                act.wait_ge(rstd2_ready, i * NS + m + 1)
                for t in range(T):
                    last = act.activation(raw[:, t], raw[:, t], ACT.Identity, bias=offset2[:, t:t + 1],
                                          scale=rstd2[:, t:t + 1])
                last.then_inc(n2_ready, 1)

            def elu(i, m):
                act.wait_ge(acc_free, i * NS + m + 2)
                act.activation(neg[:], hp[:], ACT.Relu, scale=-1.0).then_inc(neg_s, 1)
                act.wait_ge(neg_s, i * NS + m + 1)
                act.activation(neg[:], neg[:], ACT.Exp, scale=-1.0).then_inc(elu_ready, 1)

            def body(part, i, steps):
                n = 0
                for s in steps:
                    if has(part, s + sc.AHEAD + 1):
                        rises(i, s + sc.AHEAD + 1)
                    for kind, m, k in sc.work(part, s)[:2]:
                        work(part, i, n, kind, m, k)
                        n += 1
                    if has(part, s + 3):
                        probabilities(i, s + 3)
                    for kind, m, k in sc.work(part, s)[2:]:
                        work(part, i, n, kind, m, k)
                        n += 1
                    if gated and part != "pre" and s % T == T - 1:
                        elu(i, s // T)
                    if gated and sc.lead(part, s, sc.rows2) is not None:
                        project_rows(i, sc.lead(part, s, sc.rows2))

            parts(act, body)

        @block.vector
        def _(dve):
            dve.memset(ones[:], 1.0).then_inc(acc_free, 1)
            dve.wait_ge(acc_free, 1)
            dve.sem_inc(ready, 1)
            dve.memset(stage_v[:, :, D], 1.0).then_inc(ready, 1)
            if gated:
                dve.memset(all_ones[:], 1.0).then_inc(top_s, 1)

            def prepare_weights():
                if gated:
                    dve.wait_ge(w_in, 16 * 8)
                    dve.tensor_scalar(gate[:], gate[:], 1.0, None, ALU.add)
                    dve.wait_ge(fold, 1)
                    dve.tensor_copy(col_sum[:], wk_banks[:, 0, 0:D]).then_inc(top_s, 1)
                    dve.wait_ge(top_s, 2)
                    for t in range(T):
                        dve.tensor_scalar(shifted[:, t], col_sum[:], shift[:, t:t + 1], None, ALU.mult)
                else:
                    dve.wait_ge(fold, 1)
                    dve.tensor_copy(w_s[:], wk_banks[:, 0, 0:2]).then_inc(top_s, 1)
                    dve.wait_ge(top_s, 1)
                dve.tensor_copy(w_r[:, 0], w_s[:, 0:1].to_broadcast([P, P]))
                dve.tensor_copy(w_r[:, 1], w_s[:, 1:2].to_broadcast([P, P])).then_inc(ready, 1)

            def norm_stats(i, m):
                b = i * NS + m
                dve.wait_ge(ln_ready, b)
                for t in range(T):
                    last = dve.bn_stats(stats[:, t], x_sb[:, b * T + t])
                last.then_inc(stat_s, 1)
                dve.wait_ge(stat_s, b + 1)
                dve.sem_inc(tick_dve, 1)
                for t in range(T):
                    last = dve.bn_aggr(mean_var[:, t], stats[:, t])
                last.then_inc(var_ready, 1)

            def project(part, i, n, m, k):
                dve.wait_ge(wk_full, use_no(part, i, n) + 1)
                wk = bank_of(part, n)
                if k == 0:
                    dve.wait_ge(staged, i * NS + m)
                for t in range(4):
                    last = dve.scalar_tensor_tensor(out=raw[:, 4 * k + t], in0=wk[:, t * P:(t + 1) * P],
                                                    scalar=gate[:, 4 * k + t:4 * k + t + 1], in1=shifted[:, 4 * k + t],
                                                    op0=ALU.mult, op1=ALU.add)
                last.then_inc(v_ready, 1)

            def project_stats(i, m):
                b = i * NS + m
                dve.wait_ge(v_ready, 2 * b + 2)
                for t in range(T):
                    last = dve.bn_stats(stats2[:, t], raw[:, t])
                last.then_inc(st2_s, 1)
                dve.wait_ge(st2_s, b + 1)
                dve.sem_inc(tick_dve, 1)
                for t in range(T):
                    last = dve.bn_aggr(mean_var2[:, t], stats2[:, t])
                last.then_inc(var2_ready, 1)

            def neighbours(i, m, t):
                b = i * NS + m
                if t == 0:
                    dve.wait_ge(sb_ready, 2 * b + 2)
                    dve.sem_inc(tick_dve, 1)
                if t >= 2:
                    dve.wait_ge(g_done, T * b + t - 1)
                    dve.sem_inc(tick_dve, 1)
                dve.tensor_tensor_reduce(junk[:, t % 2], s2_all[:, m % 2], mask_a[:, t], 1.0, -3.0e38, ALU.add, ALU.max,
                                         g_max[:, m % 2, t:t + 1]).then_inc(g_done, 1)
                if t == T - 1:
                    dve.wait_ge(g_done, T * b + T)
                    extra = 2 if gated else 1
                    dve.wait_ge(sc_ready, b + 1)
                    dve.tensor_tensor(top[:, m % 2], g_max[:, m % 2], s1_col[:, m % 2], ALU.add).then_inc(top_s, 1)
                    dve.wait_ge(top_s, 2 * b + 1 + extra)
                    dve.scalar_tensor_tensor(out=most[:, m % 2], in0=top[:, m % 2], scalar=ALPHA, in1=top[:, m % 2],
                                             op0=ALU.mult, op1=ALU.max).then_inc(top_s, 1)
                    dve.wait_ge(top_s, 2 * b + 2 + extra)
                    dve.scalar_tensor_tensor(out=c_col[:, m % 2], in0=s1_col[:, m % 2], scalar=ALPHA, in1=most[:, m % 2],
                                             op0=ALU.mult, op1=ALU.subtract).then_inc(c_ready, 1)

            def sums(i, u):
                dve.wait_ge(r_done, i * S + u + 1)
                for k in range(2):
                    half = slice(k * HALF, (k + 1) * HALF)
                    dve.wait_ge(s2_full, 2 * (i * S + u) + k + 1)
                    dve.tensor_tensor(z[:, u % PLACES, half], s2[:, k], r[:, u % PLACES, half], ALU.add)\
                       .then_inc(z_done, 1)

            def output(i, m):
                b = i * NS + m
                dve.wait_ge(av_done, (b + 1) * T)
                for bank in range(ACC_BANKS):
                    n = min(APB, T - bank * APB)
                    den = acc[:, bank, 0:n * VW].rearrange("p (t c) -> p t c", t=n)[:, :, D:VW]
                    last = dve.reciprocal(rec[:, bank * APB:bank * APB + n].unsqueeze(2), den)
                last.then_inc(xa_s, 1)
                dve.wait_ge(xa_s, b + 1)
                for t in range(T):
                    xs = x_sb[:, b * T + t]
                    dst, add = (hp[:, t], v_sl[m % 2][:, t, 0:D]) if gated else (xs, xs)
                    last = dve.scalar_tensor_tensor(out=dst, in0=acc_tile(t, 0, D), scalar=rec[:, t:t + 1], in1=add,
                                                    op0=ALU.mult, op1=ALU.add)
                last.then_inc(acc_free, 1)
                if gated:
                    xs = x_sb[:, bass.ds(b * T, T)]
                    dve.wait_ge(acc_free, b + 2)
                    dve.scalar_tensor_tensor(out=xs, in0=hp[:], scalar=0.0, in1=xs, op0=ALU.max, op1=ALU.add)\
                       .then_inc(pos_s, 1)

            def negative_part(i, m):
                b = i * NS + m
                xs = x_sb[:, bass.ds(b * T, T)]
                dve.wait_ge(elu_ready, b + 1)
                dve.wait_ge(pos_s, b + 1)
                dve.scalar_tensor_tensor(out=xs, in0=neg[:], scalar=-1.0, in1=xs, op0=ALU.add, op1=ALU.add)

            def body(part, i, steps):
                n = 0
                for s in steps:
                    if has(part, s + sc.AHEAD):
                        sums(i, s + sc.AHEAD)
                    if has(part, s + 1) and s % T == T - 2 and part != "pre":
                        output(i, s // T)
                    for kind, m, k in sc.work(part, s):
                        if gated and kind == "V":
                            project(part, i, n, m, k)
                        n += 1
                    for at, tiles in sc.neighbours.items():
                        if sc.lead(part, s, at) is not None:
                            for t in tiles:
                                neighbours(i, sc.lead(part, s, at), t)
                    if gated and sc.lead(part, s, sc.stats2) is not None:
                        project_stats(i, sc.lead(part, s, sc.stats2))
                    if gated and part != "pre" and s % T == T - 1:
                        negative_part(i, s // T)
                    if sc.lead(part, s, sc.stats) is not None:
                        norm_stats(i, sc.lead(part, s, sc.stats))
                    if part == "pre" and s == steps[0]:
                        prepare_weights()

            parts(dve, body)

        @block.gpsimd
        def _(pool):
            root = rsqrt_steps(pool, nc, mean_var, rvar, guess, rstd, root_s, rstd_ready, var_ready, tick_pool)
            if gated:
                root2 = rsqrt_steps(pool, nc, mean_var2, rvar2, guess2, rstd2, root2_s, rstd2_ready, var2_ready,
                                    tick_pool, offset2)

            def norm_rows(part, i, m):
                b = i * NS + m
                if not (part == "pre" and m == 0):
                    pool.wait_ge(h_ready, 2 * b)
                pool.tensor_tensor(hn[:], x_sb[:, bass.ds(b * T, T)],
                                   mean_var[:, :, 0:1].to_broadcast([P, T, D]), ALU.subtract).then_inc(rows_s, 1)
                pool.wait_ge(rstd_ready, b + 1)
                pool.sem_inc(tick_pool, 1)
                pool.wait_ge(rows_s, b + 1)
                pool.tensor_tensor(hn[:], hn[:], rstd[:].unsqueeze(2).to_broadcast([P, T, D]), ALU.mult)\
                    .then_inc(ln_ready, 1)

            def body(part, i, steps):
                for s in steps:
                    m = sc.lead(part, s, sc.stats)
                    if m is not None:
                        root(i * NS + m)
                        norm_rows(part, i, m)
                    m = sc.lead(part, s, sc.stats2)
                    if gated and m is not None:
                        root2(i * NS + m)
                    m = sc.lead(part, s, sc.rows2)
                    if gated and m is not None:
                        b = i * NS + m
                        if part == "pre" and m == 0:
                            pool.wait_ge(w_in, 16 * 8)
                        pool.wait_ge(n2_ready, b + 1)
                        pool.tensor_tensor(scaled[:], raw[:], gamma[:].unsqueeze(1).to_broadcast([P, T, D]), ALU.mult)\
                            .then_inc(gb_s, 1)
                        if not (part == "pre" and m == 0):
                            pool.wait_ge(v_in[(m - 1) % 2], (i + (m - 1) // 2 + 1) * 16)
                        pool.wait_ge(gb_s, b + 1)
                        pool.tensor_tensor(stage_v[:, :, 0:D], scaled[:], beta[:].unsqueeze(1).to_broadcast([P, T, D]),
                                           ALU.add).then_inc(staged, 1)

            parts(pool, body)


def kernel(x, adj, L0_gnn_Ws, L0_gnn_Wt, L0_gnn_Wc, L1_gnn_Wq, L1_gnn_Wk, L1_gnn_Wv, L1_gnn_Wo, L1_gnn_bo, L2_gnn_W,
           L2_gnn_a, L2_gnn_node_weights, L2_gnn_node_bias, L2_gnn_ln_gamma, L2_gnn_ln_beta, L3_gnn_W, L3_gnn_a):
    import concourse.bacc as bacc
    from concourse.bass_utils import run_bass_kernel_spmd

    def rows(v):
        return np.broadcast_to(np.asarray(v)[None, :], (P, len(v)))

    arrays = {
        "x": x, "adj": adj,
        "w_st": np.concatenate([L0_gnn_Ws, L0_gnn_Wt], axis=1), "w_c": L0_gnn_Wc,
        "w_q": np.asarray(L1_gnn_Wq).T, "w_k": np.asarray(L1_gnn_Wk).T, "w_v": np.asarray(L1_gnn_Wv).T,
        "w_o": np.asarray(L1_gnn_Wo).T, "b_o": rows(L1_gnn_bo),
        "w_2": L2_gnn_W, "a_2": np.asarray(L2_gnn_a).reshape(2, D).T,
        "nw": np.asarray(L2_gnn_node_weights).reshape(T, P).T, "nb": np.asarray(L2_gnn_node_bias).reshape(T, P).T,
        "gamma": rows(L2_gnn_ln_gamma), "beta": rows(L2_gnn_ln_beta),
        "gamma_c": np.asarray(L2_gnn_ln_gamma)[:, None], "beta_c": np.asarray(L2_gnn_ln_beta)[:, None],
        "w_3": L3_gnn_W, "w_3t": np.asarray(L3_gnn_W).T, "a_3": np.asarray(L3_gnn_a).reshape(2, D).T,
    }
    arrays = {k: np.ascontiguousarray(v) for k, v in arrays.items()}
    nc = bacc.Bacc("TRN2", target_bir_lowering=False, num_devices=1)
    args = {k: nc.dram_tensor(k, v.shape, mybir.dt.from_np(v.dtype), kind="ExternalInput").ap()
            for k, v in arrays.items()}
    out = nc.dram_tensor("out", (B, N, D), F32, kind="ExternalOutput").ap()
    build(nc, out=out, **args)
    return run_bass_kernel_spmd(nc, [arrays], core_ids=[0]).results[0]["out"]
```
